# Optimizing a Trainium2 kernel written in Bass

```python
import numpy as np
import jax
import jax.numpy as jnp

def _softmax(x, axis=-1):
    return jax.nn.softmax(x, axis=axis)

def _gelu(x):
    return jax.nn.gelu(x, approximate=True)

def _silu(x):
    return jax.nn.silu(x)

def _sigmoid(x):
    return jax.nn.sigmoid(x)

def _layernorm(x, axis=-1, eps=1e-05):
    m = jnp.mean(x, axis=axis, keepdims=True)
    v = jnp.var(x, axis=axis, keepdims=True)
    return (x - m) / jnp.sqrt(v + eps)

def _scatter_add(tgt, idx, src, axis=0):
    return tgt.at[idx].add(src)

def _segment_sum(src, seg, n):
    return jax.ops.segment_sum(src, seg, n)
kernel_name = 'mk_gnn_preln_d4_gnn_r8_db2727'

def setup_inputs(seed: int=0):
    np.random.seed(seed)
    _w = jnp.asarray

    def _rec_inputs():
        import jax
        import jax.numpy as jnp
        _gk = jax.random.key(seed)
        x = -8.776e-05 + 1 * jax.random.normal(jax.random.fold_in(_gk, 1), (2500, 256), jnp.float32)
        src = jax.random.randint(jax.random.fold_in(_gk, 2), (40000,), 0, 2500, jnp.int32)
        dst = jnp.minimum((2500 * jax.random.uniform(jax.random.fold_in(_gk, 3), (40000,)) ** 2.0).astype(jnp.int32), 19999)
        _o = jnp.argsort(dst, stable=True)
        src = src[_o]
        dst = dst[_o]
        edge_weight = -0.000423496 + 0.100023 * jax.random.normal(jax.random.fold_in(_gk, 13), (40000,), jnp.float32)
        return (x, src, dst, edge_weight)
    x, src, dst, edge_weight = _rec_inputs()

    def _L0_gnn_setup():
        import jax, jax.numpy as jnp
        import numpy as np
        N = 2500
        E = 40000
        H = 8
        D = 32
        NEG_SLOPE = 0.2

        def gat_conv(x, W, al, ar, b, src, dst):
            h = (x @ W).reshape(N, H, D)
            el = jnp.einsum('nhd,hd->nh', h, al)
            er = jnp.einsum('nhd,hd->nh', h, ar)
            e = jax.nn.leaky_relu(el[src] + er[dst], NEG_SLOPE)
            m = jax.ops.segment_max(e, dst, num_segments=N)
            ex = jnp.exp(e - m[dst])
            s = jax.ops.segment_sum(ex, dst, num_segments=N)
            alpha = ex / s[dst]
            out = jax.ops.segment_sum(alpha[:, :, None] * h[src], dst, num_segments=N)
            out = out.reshape(N, H * D) + b
            return jax.nn.elu(out)
        key = jax.random.key(seed)
        ks = jax.random.split(key, 11)
        p = lambda k, s: jax.random.normal(k, s, jnp.float32) * 0.1
        return {'features': jax.random.normal(ks[0], (N, H * D), jnp.float32), 'W0': p(ks[1], (H * D, H * D)), 'al0': p(ks[2], (H, D)), 'ar0': p(ks[3], (H, D)), 'b0': p(ks[4], (H * D,)), 'W1': p(ks[5], (H * D, H * D)), 'al1': p(ks[6], (H, D)), 'ar1': p(ks[7], (H, D)), 'b1': p(ks[8], (H * D,)), 'src': jax.random.randint(ks[9], (E,), 0, N, jnp.int32), 'dst': jax.random.randint(ks[10], (E,), 0, N, jnp.int32)}
    _L0_gnn_all = _L0_gnn_setup()
    _L0_gnn_in = {k: v for k, v in _L0_gnn_all.items() if k in ('W0', 'al0', 'ar0', 'b0', 'W1', 'al1', 'ar1', 'b1')}
    del _L0_gnn_all

    def _L1_gnn_setup():
        import jax, jax.numpy as jnp
        import numpy as np
        BLOCK_DIMS = [8] * 32

        def _mask_indices():
            d = sum(BLOCK_DIMS)
            mask = np.ones((d, d), dtype=np.int8)
            off = 0
            for b in BLOCK_DIMS:
                mask[off:off + b, off:off + b] = 0
                off += b
            rows, cols = np.nonzero(mask)
            return (d, rows.astype(np.int32), cols.astype(np.int32))
        key = jax.random.key(seed)
        k1, k2 = jax.random.split(key)
        d, rows, cols = _mask_indices()
        N = 62500
        X = jax.random.normal(k1, (N, d), dtype=jnp.float32)
        w_est = 0.1 * jax.random.normal(k2, (rows.shape[0],), dtype=jnp.float32)
        return {'X': X, 'w_est': w_est, 'rows': jnp.asarray(rows), 'cols': jnp.asarray(cols)}
    _L1_gnn_all = _L1_gnn_setup()
    _L1_gnn_in = {k: v for k, v in _L1_gnn_all.items() if k in ()}
    del _L1_gnn_all

    def _L2_gnn_setup():
        import jax, jax.numpy as jnp
        import numpy as np
        N_NODES = 6250
        N_EDGES = 100000
        FEAT = 256
        HIDDEN = [512, 256, 128]

        def _glorot(key, fan_in, fan_out):
            s = jnp.sqrt(2.0 / (fan_in + fan_out)).astype(jnp.float32)
            return jax.random.normal(key, (fan_in, fan_out), dtype=jnp.float32) * s

        def _sage_conv(x, src, dst, wn, wr, b, n_nodes):
            msg = x[src]
            agg = jax.ops.segment_sum(msg, dst, num_segments=n_nodes)
            deg = jax.ops.segment_sum(jnp.ones((src.shape[0],), dtype=x.dtype), dst, num_segments=n_nodes)
            mean = agg / jnp.maximum(deg, 1.0)[:, None]
            return mean @ wn + x @ wr + b
        key = jax.random.key(seed)
        ks = jax.random.split(key, 20)
        x = jax.random.normal(ks[0], (N_NODES, FEAT), dtype=jnp.float32)
        edge_index = jax.random.randint(ks[1], (2, N_EDGES), 0, N_NODES, dtype=jnp.int64)
        enc_dims = [FEAT] + HIDDEN
        dec_dims = list(reversed(enc_dims))
        inp = {'x': x, 'edge_index': edge_index}
        k = 2
        for i in range(3):
            din, dout = (enc_dims[i], enc_dims[i + 1])
            inp[f'wn{i}'] = _glorot(ks[k], din, dout)
            k += 1
            inp[f'wr{i}'] = _glorot(ks[k], din, dout)
            k += 1
            inp[f'b{i}'] = jnp.zeros((dout,), dtype=jnp.float32)
        for i in range(3):
            din, dout = (dec_dims[i], dec_dims[i + 1])
            inp[f'dw{i}'] = _glorot(ks[k], din, dout)
            k += 1
            inp[f'db{i}'] = jnp.zeros((dout,), dtype=jnp.float32)
        return inp
    _L2_gnn_all = _L2_gnn_setup()
    _L2_gnn_in = {k: v for k, v in _L2_gnn_all.items() if k in ('wn0', 'wr0', 'b0', 'wn1', 'wr1', 'b1', 'wn2', 'wr2', 'b2', 'dw0', 'db0', 'dw1', 'db1', 'dw2', 'db2')}
    del _L2_gnn_all

    def _L3_gnn_setup():
        import jax, jax.numpy as jnp
        import numpy as np
        ALPHA = 0.2
        N_NODES = 12500
        N_EDGES = 200000
        NFEAT = 256
        HID = 64
        NHEADS = 4

        def _gat_head(x, src, dst, Wh, ah, n_nodes):
            hid = Wh.shape[1]
            h = x @ Wh
            h = jnp.where(jnp.isnan(h), 0.0, h)
            a1, a2 = (ah[0, :hid], ah[0, hid:])
            alpha_src = h @ a1
            alpha_dst = h @ a2
            s = alpha_src[src] + alpha_dst[dst]
            e = jnp.exp(-jax.nn.leaky_relu(s, ALPHA))
            e = jnp.where(jnp.isnan(e), 0.0, e)
            rowsum = jax.ops.segment_sum(e, src, num_segments=n_nodes)
            hp = jax.ops.segment_sum(e[:, None] * h[dst], src, num_segments=n_nodes)
            hp = jnp.where(jnp.isnan(hp), 0.0, hp)
            hp = hp / rowsum[:, None]
            hp = jnp.where(jnp.isnan(hp), 0.0, hp)
            return jax.nn.elu(hp)
        key = jax.random.key(seed)
        k1, k2, k3, k4 = jax.random.split(key, 4)
        x = jax.random.normal(k1, (N_NODES, NFEAT), dtype=jnp.float32)
        edge_index = jax.random.randint(k2, (2, N_EDGES), 0, N_NODES, dtype=jnp.int64)
        W = jax.random.normal(k3, (NHEADS, NFEAT, HID), dtype=jnp.float32) * (1.414 * np.sqrt(2.0 / (NFEAT + HID)))
        a = jax.random.normal(k4, (NHEADS, 1, 2 * HID), dtype=jnp.float32) * (1.414 * np.sqrt(2.0 / (1 + 2 * HID)))
        return {'x': x, 'edge_index': edge_index, 'W': W, 'a': a}
    _L3_gnn_all = _L3_gnn_setup()
    _L3_gnn_in = {k: v for k, v in _L3_gnn_all.items() if k in ('W', 'a')}
    del _L3_gnn_all
    return {'x': x, 'src': src, 'dst': dst, 'edge_weight': edge_weight, 'L0_gnn_W0': _L0_gnn_in['W0'], 'L0_gnn_al0': _L0_gnn_in['al0'], 'L0_gnn_ar0': _L0_gnn_in['ar0'], 'L0_gnn_b0': _L0_gnn_in['b0'], 'L0_gnn_W1': _L0_gnn_in['W1'], 'L0_gnn_al1': _L0_gnn_in['al1'], 'L0_gnn_ar1': _L0_gnn_in['ar1'], 'L0_gnn_b1': _L0_gnn_in['b1'], 'L2_gnn_wn0': _L2_gnn_in['wn0'], 'L2_gnn_wr0': _L2_gnn_in['wr0'], 'L2_gnn_b0': _L2_gnn_in['b0'], 'L2_gnn_wn1': _L2_gnn_in['wn1'], 'L2_gnn_wr1': _L2_gnn_in['wr1'], 'L2_gnn_b1': _L2_gnn_in['b1'], 'L2_gnn_wn2': _L2_gnn_in['wn2'], 'L2_gnn_wr2': _L2_gnn_in['wr2'], 'L2_gnn_b2': _L2_gnn_in['b2'], 'L2_gnn_dw0': _L2_gnn_in['dw0'], 'L2_gnn_db0': _L2_gnn_in['db0'], 'L2_gnn_dw1': _L2_gnn_in['dw1'], 'L2_gnn_db1': _L2_gnn_in['db1'], 'L2_gnn_dw2': _L2_gnn_in['dw2'], 'L2_gnn_db2': _L2_gnn_in['db2'], 'L3_gnn_W': _L3_gnn_in['W'], 'L3_gnn_a': _L3_gnn_in['a']}

def reference(x, src, dst, edge_weight, L0_gnn_W0, L0_gnn_al0, L0_gnn_ar0, L0_gnn_b0, L0_gnn_W1, L0_gnn_al1, L0_gnn_ar1, L0_gnn_b1, L2_gnn_wn0, L2_gnn_wr0, L2_gnn_b0, L2_gnn_wn1, L2_gnn_wr1, L2_gnn_b1, L2_gnn_wn2, L2_gnn_wr2, L2_gnn_b2, L2_gnn_dw0, L2_gnn_db0, L2_gnn_dw1, L2_gnn_db1, L2_gnn_dw2, L2_gnn_db2, L3_gnn_W, L3_gnn_a):
    import jax
    import jax.numpy as jnp

    def _L0_gnn_ref(features, W0, al0, ar0, b0, W1, al1, ar1, b1, src, dst):
        import jax, jax.numpy as jnp
        import numpy as np
        N = 2500
        E = 40000
        H = 8
        D = 32
        NEG_SLOPE = 0.2

        def gat_conv(x, W, al, ar, b, src, dst):
            h = (x @ W).reshape(N, H, D)
            el = jnp.einsum('nhd,hd->nh', h, al)
            er = jnp.einsum('nhd,hd->nh', h, ar)
            e = jax.nn.leaky_relu(el[src] + er[dst], NEG_SLOPE)
            m = jax.ops.segment_max(e, dst, num_segments=N)
            ex = jnp.exp(e - m[dst])
            s = jax.ops.segment_sum(ex, dst, num_segments=N)
            alpha = ex / s[dst]
            out = jax.ops.segment_sum(alpha[:, :, None] * h[src], dst, num_segments=N)
            out = out.reshape(N, H * D) + b
            return jax.nn.elu(out)
        x = gat_conv(features, W0, al0, ar0, b0, src, dst)
        x = gat_conv(x, W1, al1, ar1, b1, src, dst)
        return x

    def _L1_gnn_ref(X, w_est, rows, cols):
        import jax, jax.numpy as jnp
        import numpy as np
        BLOCK_DIMS = [8] * 32

        def _mask_indices():
            d = sum(BLOCK_DIMS)
            mask = np.ones((d, d), dtype=np.int8)
            off = 0
            for b in BLOCK_DIMS:
                mask[off:off + b, off:off + b] = 0
                off += b
            rows, cols = np.nonzero(mask)
            return (d, rows.astype(np.int32), cols.astype(np.int32))
        d = X.shape[1]
        W = jnp.zeros((d, d), dtype=X.dtype).at[rows, cols].set(w_est)
        return X @ W

    def _L2_gnn_ref(x, edge_index, wn0, wr0, b0, wn1, wr1, b1, wn2, wr2, b2, dw0, db0, dw1, db1, dw2, db2):
        import jax, jax.numpy as jnp
        import numpy as np
        N_NODES = 6250
        N_EDGES = 100000
        FEAT = 256
        HIDDEN = [512, 256, 128]

        def _glorot(key, fan_in, fan_out):
            s = jnp.sqrt(2.0 / (fan_in + fan_out)).astype(jnp.float32)
            return jax.random.normal(key, (fan_in, fan_out), dtype=jnp.float32) * s

        def _sage_conv(x, src, dst, wn, wr, b, n_nodes):
            msg = x[src]
            agg = jax.ops.segment_sum(msg, dst, num_segments=n_nodes)
            deg = jax.ops.segment_sum(jnp.ones((src.shape[0],), dtype=x.dtype), dst, num_segments=n_nodes)
            mean = agg / jnp.maximum(deg, 1.0)[:, None]
            return mean @ wn + x @ wr + b
        src, dst = (edge_index[0], edge_index[1])
        n = x.shape[0]
        h = x
        for wn, wr, b in ((wn0, wr0, b0), (wn1, wr1, b1), (wn2, wr2, b2)):
            h = jax.nn.relu(_sage_conv(h, src, dst, wn, wr, b, n))
        for dw, db in ((dw0, db0), (dw1, db1), (dw2, db2)):
            h = jax.nn.relu(h @ dw + db)
        return h

    def _L3_gnn_ref(x, edge_index, W, a):
        import jax, jax.numpy as jnp
        import numpy as np
        ALPHA = 0.2
        N_NODES = 12500
        N_EDGES = 200000
        NFEAT = 256
        HID = 64
        NHEADS = 4

        def _gat_head(x, src, dst, Wh, ah, n_nodes):
            hid = Wh.shape[1]
            h = x @ Wh
            h = jnp.where(jnp.isnan(h), 0.0, h)
            a1, a2 = (ah[0, :hid], ah[0, hid:])
            alpha_src = h @ a1
            alpha_dst = h @ a2
            s = alpha_src[src] + alpha_dst[dst]
            e = jnp.exp(-jax.nn.leaky_relu(s, ALPHA))
            e = jnp.where(jnp.isnan(e), 0.0, e)
            rowsum = jax.ops.segment_sum(e, src, num_segments=n_nodes)
            hp = jax.ops.segment_sum(e[:, None] * h[dst], src, num_segments=n_nodes)
            hp = jnp.where(jnp.isnan(hp), 0.0, hp)
            hp = hp / rowsum[:, None]
            hp = jnp.where(jnp.isnan(hp), 0.0, hp)
            return jax.nn.elu(hp)
        n_nodes = x.shape[0]
        src, dst = (edge_index[0], edge_index[1])
        outs = [_gat_head(x, src, dst, W[h], a[h], n_nodes) for h in range(W.shape[0])]
        out = jnp.concatenate(outs, axis=1)
        return jax.nn.elu(out)
    edge_index = jnp.stack([src, dst])
    h = jnp.maximum(_layernorm(x, axis=-1), 0.0)
    x = x + _L0_gnn_ref(h, L0_gnn_W0, L0_gnn_al0, L0_gnn_ar0, L0_gnn_b0, L0_gnn_W1, L0_gnn_al1, L0_gnn_ar1, L0_gnn_b1, src, dst)
    h = jnp.maximum(_layernorm(x, axis=-1), 0.0)
    x = x + _L1_gnn_ref(h, edge_weight, src, dst)
    h = jnp.maximum(_layernorm(x, axis=-1), 0.0)
    x = x + _L2_gnn_ref(h, edge_index, L2_gnn_wn0, L2_gnn_wr0, L2_gnn_b0, L2_gnn_wn1, L2_gnn_wr1, L2_gnn_b1, L2_gnn_wn2, L2_gnn_wr2, L2_gnn_b2, L2_gnn_dw0, L2_gnn_db0, L2_gnn_dw1, L2_gnn_db1, L2_gnn_dw2, L2_gnn_db2)
    h = jnp.maximum(_layernorm(x, axis=-1), 0.0)
    x = x + _L3_gnn_ref(h, edge_index, L3_gnn_W, L3_gnn_a)
    return x

_drawn_inputs = setup_inputs


def setup_inputs(seed=0):
    import zlib

    import numpy as np

    out = dict(_drawn_inputs(seed))
    spreads = {'L2_gnn_b0': (0.0, 0.513),
     'L2_gnn_b1': (0.0, 0.574),
     'L2_gnn_b2': (0.0, 0.698),
     'L2_gnn_db0': (0.0, 0.352),
     'L2_gnn_db1': (0.0, 0.1),
     'L2_gnn_db2': (0.0, 0.1)}
    factors = {'L0_gnn_ar0': 4.196, 'L0_gnn_al1': 3.153, 'L0_gnn_ar1': 8.0}
    for name, (base, spread) in spreads.items():
        noise = np.random.default_rng([zlib.crc32(name.encode()), seed]).standard_normal(out[name].shape)
        drawn = base * np.exp(spread * noise) if base else spread * noise
        out[name] = jnp.asarray(drawn.astype(out[name].dtype))
    for name, factor in factors.items():
        out[name] = (out[name] * factor).astype(out[name].dtype)
    return out
```

```python
import concourse.bass as bass
from concourse import mybir
from contextlib import ExitStack

P = 128
N = 2500
E = 40000
D = 256
NT = (N + P - 1) // P
NP = NT * P
LAST = N - (NT - 1) * P
NCH = (E + P - 1) // P
NG = (NCH + P - 1) // P
CENTRE = NP // 2
FAR = 1.0e6
BIG = float(2 ** 60)
LO = 2048.0
TOP = 32768.0
SLOPE = 0.2
EPS = 1e-5
OOB = 1 << 20


class Chain:

    def __init__(self, eng, sem):
        self.eng, self.sem, self.base, self.n = eng, sem, 0, 0

    def __call__(self, ins):
        ins.then_inc(self.sem, 1)
        self.n += 1
        return ins

    def wait(self):
        self.eng.wait_ge(self.sem, self.base + self.n)

    def begin(self, i, per):
        self.start, self.per = self.base + self.n, per
        self.base, self.n = self.start + i * per, 0

    def end(self, trips):
        assert self.n == self.per, (self.n, self.per)
        self.base, self.n = self.start + trips * self.per, 0


def build(nc, x, src, dst, ew, gat0, gat1, sage, dec, gat3, out):
    f32, f16, bf16, i32 = mybir.dt.float32, mybir.dt.float16, mybir.dt.bfloat16, mybir.dt.int32
    ALU, ACT, AX = mybir.AluOpType, mybir.ActivationFunctionType, mybir.AxisListType
    ds = bass.ds
    top = ExitStack()
    with top:
        def sb(name, shape, dt, ctx=top):
            return ctx.enter_context(nc.sbuf_tensor(name, shape, dt))

        names = [0]
        used = []

        class Phase(ExitStack):

            def sb(self, name, shape, dt):
                names[0] += 1
                return self.enter_context(nc.sbuf_tensor(f"{name}_{names[0]}", shape, dt))

            def ps(self, name, shape, dt=f32):
                names[0] += 1
                return self.enter_context(nc.psum_tensor(f"{name}_{names[0]}", shape, dt))

            def sem(self, name):
                names[0] += 1
                handle = nc.alloc_semaphore(f"{name}_{names[0]}")
                self.callback(lambda: used.append(handle))
                return handle

            def __exit__(self, *failure):
                done = super().__exit__(*failure)
                if used and failure[0] is None:
                    nc.clear_and_free_semaphores(list(used))
                    nc.all_engine_barrier()
                    used.clear()
                return done

        C = sb("C", [P, NT * NP], f16)
        HB = sb("HB", [P, NT * 264], f32)
        R = sb("R", [P, NT * 528], f32)
        Rh = R[:, :].bitcast(f16)
        ident = sb("ident", [P, P], f32)
        ident16 = sb("ident16", [P, P], f16)
        padneg = sb("padneg", [P, 1], f32)
        eps = sb("eps", [P, 1], f32)
        rdeg = sb("rdeg", [P, NT], f32)
        AB = sb("AB", [P, NT * 16], f32)
        table = sb("table", [1, 4 * NT], i32)
        wd = nc.dram_tensor("wd", [D * D, 1], f32, kind="Internal").ap()
        xd = nc.dram_tensor("xd", [P, NT * D], f32, kind="Internal").ap()
        rowd = nc.dram_tensor("rowd", [8, NP], f32, kind="Internal").ap()
        keyd = nc.dram_tensor("keyd", [NG * P, P], f32, kind="Internal").ap()
        late_ = ExitStack()
        edge = ExitStack()
        widx = sb("widx", [P, NG * P], i32, late_)
        ewT = sb("ewT", [P, NG * P], f32, late_)
        srcT = sb("srcT", [P, NG * P], f32, edge)
        dstT = sb("dstT", [P, NG * P], f32, edge)
        keyT = sb("keyT", [P, NG * P], f32, edge)
        wcell = sb("wcell", [P, NG * P], f32, edge)
        late = sb("late", [P, NG * P], f32, edge)

        def chunk(value, most):
            return nc.s_assert_within(value, 0, most, skip_runtime_bounds_check_because=
                                      "a range of chunks starts below NCH and is at most NCH or four chunks long")

        def rows_in(eng, dest, dram, sem):
            eng.dma_start(dest[:, 0:(NT - 1) * D].rearrange("p (t f) -> p t f", f=D),
                          dram[0:(NT - 1) * P, :].rearrange("(t p) f -> p t f", p=P)).then_inc(sem, 16)
            eng.dma_start(dest[0:LAST, (NT - 1) * D:NT * D], dram[(NT - 1) * P:N, :]).then_inc(sem, 16)

        with Phase() as ph:
            raw = [ph.sb(f"raw{i}", [P, NG * P], dt) for i, dt in enumerate((i32, i32, f32))]
            rf = [ph.sb(f"rf{i}", [P, NG * P], f32) for i in range(2)]
            key = ph.sb("key", [P, NG * P], f32)
            tmp = ph.sb("tmp", [P, NG * P], f32)
            zero = ph.sb("zero", [P, 512], f32)
            cmin, cmax = ph.sb("cmin", [P, NG], f32), ph.sb("cmax", [P, NG], f32)
            tlo = ph.sb("tlo", [P, NT], f32)
            cidx = ph.sb("cidx", [P, NG], f32)
            away = ph.sb("away", [P, NG], f32)
            ov = ph.sb("ov", [P, NG * NT], f32)
            ov2 = ph.sb("ov2", [P, NG * NT], f32)
            lohi = ph.sb("lohi", [P, 2, NG, NT], f32)
            lohir = ph.sb("lohir", [P, 2, NG, NT], f32)
            lh = ph.sb("lh", [1, 2, NT], f32)
            row = ph.sb("row", [1, 8, NT], f32)
            pst = [ph.ps(f"pst{i}", [P, P]) for i in range(4)]
            s_set, s_in, s_rf, s_t, s_ev, s_lohi, s_all, s_iota, s_z, s_st, s_v = (
                ph.sem(n) for n in ("set", "in", "rf", "t", "ev", "lohi", "all", "iota", "z", "st", "v"))
            block = ph.enter_context(nc.Block())

            @block.gpsimd
            def _(g):
                for q in range(2):
                    g.memset(raw[q][:, :], -1).then_inc(s_set, 1)
                g.memset(raw[2][:, :], 0.0).then_inc(s_set, 1)
                g.memset(zero[:, :], 0.0).then_inc(s_set, 1)
                g.memset(ident[:, :], 0.0).then_inc(s_z, 1)
                g.memset(padneg[:, :], 0.0).then_inc(s_z, 1)
                g.memset(eps[:, :], EPS).then_inc(s_z, 1)
                g.iota(tlo[:, :], pattern=[[P, NT]], base=0, channel_multiplier=0,
                       allow_small_or_imprecise_dtypes=True).then_inc(s_iota, 1)
                g.iota(cidx[:, :], pattern=[[P, NG]], base=0, channel_multiplier=1,
                       allow_small_or_imprecise_dtypes=True).then_inc(s_iota, 1)
                g.wait_ge(s_z, 3)
                g.affine_select(out=ident[:, :], in_=ident[:, :], compare_op=ALU.not_equal, fill=1.0, base=0,
                                pattern=[[-1, P]], channel_multiplier=1).then_inc(s_z, 1)
                g.affine_select(out=padneg[:, :], in_=padneg[:, :], compare_op=ALU.is_gt, fill=-1e9, base=LAST,
                                pattern=[[0, 1]], channel_multiplier=-1).then_inc(s_z, 1)
                g.wait_ge(s_z, 5)
                g.tensor_copy(ident16[:, :], ident[:, :]).then_inc(s_z, 1)
                g.wait_ge(s_lohi, 1)
                g.partition_all_reduce(lohir[:, :, :, :].rearrange("p a g t -> p (a g t)"),
                                       lohi[:, :, :, :].rearrange("p a g t -> p (a g t)"), P,
                                       bass.bass_isa.ReduceOp.max).then_inc(s_all, 1)

            @block.sync
            def _(sp):
                sp.wait_ge(s_set, 4)
                full = NCH - 1 - (NG - 1) * P
                for q, a in enumerate((src, dst, ew)):
                    for g in range(NG - 1):
                        sp.dma_start(raw[q][:, g * P:(g + 1) * P],
                                     a[g * P * P:(g + 1) * P * P].rearrange("(c j) -> c j", j=P)).then_inc(s_in, 16)
                    sp.dma_start(raw[q][0:full, (NG - 1) * P:NG * P],
                                 a[(NG - 1) * P * P:(NCH - 1) * P].rearrange("(c j) -> c j", j=P)).then_inc(s_in, 16)
                    sp.dma_start(raw[q][full:full + 1, (NG - 1) * P:(NG - 1) * P + E - (NCH - 1) * P],
                                 a[(NCH - 1) * P:E].rearrange("(c j) -> c j", c=1)).then_inc(s_in, 16)
                sp.dma_start(wd.rearrange("(p c) a -> p (c a)", p=P), zero[:, :]).then_inc(s_st, 16)
                sp.wait_ge(s_rf, 1)
                for g in range(NG):
                    sp.dma_start(keyd[g * P:(g + 1) * P, :], key[:, g * P:(g + 1) * P]).then_inc(s_st, 16)
                sp.wait_ge(s_st, 16 * (NG + 1))

            @block.tensor
            def _(pe):
                pe.wait_ge(s_z, 6)
                pe.wait_ge(s_rf, 1)
                for n in range(4 * NG):
                    q, g = divmod(n, NG)
                    if n >= 4:
                        pe.wait_ge(s_ev, n - 3)
                    a = (rf[0], rf[1], raw[2], key)[q]
                    pe.transpose(pst[n % 4][:, :], a[:, g * P:(g + 1) * P], ident[:, :]).then_inc(s_t, 1)

            @block.vector
            def _(v):
                ch = Chain(v, s_v)
                v.wait_ge(s_in, 16 * 3 * (NG + 1))
                for q in range(2):
                    ch(v.tensor_copy(rf[q][:, :], raw[q][:, :]))
                ch.wait()
                v.scalar_tensor_tensor(key[:, :], rf[0][:, :], float(4096), rf[1][:, :], ALU.mult,
                                       ALU.add).then_inc(s_rf, 1)
                ch(v.tensor_scalar(tmp[:, :], rf[1][:, :], 0.0, FAR, ALU.is_lt, ALU.mult))
                ch(v.tensor_reduce(cmax[:, :], rf[1][:, :].rearrange("p (g j) -> p g j", j=P), AX.X, ALU.max))
                ch.wait()
                ch(v.tensor_tensor(tmp[:, :], tmp[:, :], rf[1][:, :], ALU.add))
                ch.wait()
                ch(v.tensor_reduce(cmin[:, :], tmp[:, :].rearrange("p (g j) -> p g j", j=P), AX.X, ALU.min))
                v.wait_ge(s_iota, 2)
                ch(v.tensor_scalar(away[:, :], cidx[:, :], -1.0, FAR, ALU.mult, ALU.add))
                ch(v.tensor_scalar(cidx[:, :], cidx[:, :], 1.0, None, ALU.add))
                ch.wait()
                for g in range(NG):
                    o = ov[:, g * NT:(g + 1) * NT]
                    o2 = ov2[:, g * NT:(g + 1) * NT]
                    ch(v.tensor_scalar(o, tlo[:, :], float(P), cmin[:, g:g + 1], ALU.add, ALU.is_gt))
                    ch(v.tensor_scalar(o2, tlo[:, :], cmax[:, g:g + 1], None, ALU.is_le))
                ch.wait()
                ch(v.tensor_tensor(ov[:, :], ov[:, :], ov2[:, :], ALU.mult))
                ch.wait()
                for g in range(NG):
                    o = ov[:, g * NT:(g + 1) * NT]
                    ch(v.tensor_scalar(lohi[:, 0, g, :], o, away[:, g:g + 1], None, ALU.mult))
                    ch(v.tensor_scalar(lohi[:, 1, g, :], o, cidx[:, g:g + 1], None, ALU.mult))
                ch.wait()
                v.sem_inc(s_lohi, 1)
                for n in range(4 * NG):
                    q, g = divmod(n, NG)
                    v.wait_ge(s_t, n + 1)
                    if q < 2:
                        v.tensor_scalar((srcT, dstT)[q][:, g * P:(g + 1) * P], pst[n % 4][:, :], -float(CENTRE),
                                        None, ALU.add).then_inc(s_ev, 1)
                    else:
                        v.tensor_copy((ewT, keyT)[q - 2][:, g * P:(g + 1) * P], pst[n % 4][:, :]).then_inc(s_ev, 1)
                v.wait_ge(s_ev, 4 * NG)
                ch(v.tensor_scalar(wcell[:, :], srcT[:, :], float(D - CENTRE), None, ALU.is_lt))
                ch(v.tensor_scalar(late[:, :], dstT[:, :], float(D - CENTRE), None, ALU.is_lt))
                ch.wait()
                ch(v.tensor_tensor(wcell[:, :], wcell[:, :], late[:, :], ALU.mult))
                ch(v.tensor_scalar(tmp[:, :], srcT[:, :], float(-CENTRE), None, ALU.is_ge))
                ch.wait()
                ch(v.tensor_tensor(wcell[:, :], wcell[:, :], tmp[:, :], ALU.mult))
                ch.wait()
                ch(v.tensor_scalar(tmp[:, :], srcT[:, :], float(D), float(CENTRE * D + CENTRE - OOB), ALU.mult, ALU.add))
                ch.wait()
                ch(v.tensor_tensor(tmp[:, :], tmp[:, :], dstT[:, :], ALU.add))
                ch.wait()
                ch(v.tensor_tensor(tmp[:, :], tmp[:, :], wcell[:, :], ALU.mult))
                ch(v.memset(late[:, :], 0.0))
                ch.wait()
                ch(v.tensor_scalar(wcell[:, :], tmp[:, :], float(OOB), None, ALU.add))
                v.wait_ge(s_all, 1)
                ch(v.tensor_reduce(lh[:, :, :], lohir[0:1, :, :, :].rearrange("p a g t -> p a t g"), AX.X, ALU.max))
                ch.wait()
                first, pairs, acc, acc2 = (row[:, i, :] for i in range(4))
                ch(v.tensor_scalar(first, lh[:, 0, :], -1.0, FAR, ALU.mult, ALU.add))
                ch.wait()
                ch(v.tensor_scalar(first, first, float(NCH - 1), None, ALU.min))
                ch.wait()
                ch(v.tensor_tensor(pairs, lh[:, 1, :], first, ALU.subtract))
                ch.wait()
                ch(v.tensor_scalar(pairs, pairs, 0.5, 0.25, ALU.mult, ALU.add))
                ch.wait()
                ch(v.tensor_scalar(table[:, NT:2 * NT], pairs, 2.0, None, ALU.max))
                ch.wait()
                ch(v.tensor_copy(acc, table[:, NT:2 * NT]))
                ch(v.tensor_copy(table[:, 0:NT], first))
                ch.wait()
                ch(v.tensor_copy(row[:, 4, :], acc))
                step = 1
                while step < NT:
                    ch.wait()
                    ch(v.tensor_tensor(acc2[:, step:NT], acc[:, step:NT], acc[:, 0:NT - step], ALU.add))
                    ch(v.tensor_copy(acc2[:, 0:step], acc[:, 0:step]))
                    acc, acc2 = acc2, acc
                    step *= 2
                ch.wait()
                ch(v.tensor_tensor(table[:, 2 * NT:3 * NT], acc, row[:, 4, :], ALU.subtract))
                wlo, whi = row[:, 5, 0:1], row[:, 5, 1:2]
                WT = D // P
                ch(v.tensor_reduce(wlo, first[:, 0:WT], AX.X, ALU.min))
                ch(v.tensor_reduce(whi, lh[:, 1, 0:WT], AX.X, ALU.max))
                ch.wait()
                ch(v.tensor_tensor(row[:, 5, 2:3], whi, wlo, ALU.subtract))
                ch.wait()
                ch(v.tensor_scalar(row[:, 5, 3:4], row[:, 5, 2:3], 0.25, 0.375, ALU.mult, ALU.add))
                ch.wait()
                ch(v.tensor_scalar(table[:, 3 * NT + 1:3 * NT + 2], row[:, 5, 3:4], 1.0, None, ALU.max))
                ch(v.tensor_copy(table[:, 3 * NT:3 * NT + 1], wlo))
                ch.wait()

        with Phase() as ph:
            node16 = ph.sb("node16", [P, NP], f16)
            ohs = ph.sb("ohs", [P, 2, NP], f16)
            ohd = ph.sb("ohd", [P, 2, P], f16)
            keyr = ph.sb("keyr", [P, 4, P], f32)
            same = ph.sb("same", [P, 4, P], f32)
            notlater = ph.sb("notlater", [P, P], f32)
            junk = ph.sb("junk", [P, 4, P], f32)
            acc = ph.ps("acc", [P, NT * P])
            s_c, s_oh, s_used, s_out, s_key, s_same, s_late, s_dum, s_abs, s_kdone = (
                ph.sem(n) for n in ("c", "oh", "used", "out", "key", "same", "late", "dum", "abs", "kd"))
            block = ph.enter_context(nc.Block())
            PERBANK = 4
            NB = NT // PERBANK

            @block.gpsimd
            def _(g):
                g.iota(node16[:, :], pattern=[[1, NP]], base=-CENTRE, channel_multiplier=0,
                       allow_small_or_imprecise_dtypes=True).then_inc(s_c, 1)
                g.memset(notlater[:, :], 0.0).then_inc(s_c, 1)
                g.wait_ge(s_c, 2)
                g.affine_select(out=notlater[:, :], in_=notlater[:, :], compare_op=ALU.is_gt, fill=1e9, base=0,
                                pattern=[[1, P]], channel_multiplier=-1).then_inc(s_c, 1)
                g.wait_ge(s_c, 3)
                lo = g.value_load(table[0:1, 3 * NT:3 * NT + 1], min_val=0, max_val=NCH - 1)
                n = g.value_load(table[0:1, 3 * NT + 1:3 * NT + 2], min_val=1, max_val=(NCH + 3) // 4)
                with g.Fori(0, n) as i:
                    c = chunk(lo + i * 4, NG * P - 4)
                    g.wait_ge(s_key, (i + 1) * 16)
                    g.sem_inc(s_dum, 1)
                    g.wait_ge(s_late, i * 4 + 1)
                    g.sem_inc(s_dum, 1)
                    g.tensor_tensor(same[:, :, :], keyr[:, :, :],
                                    keyT[:, ds(c, 4)].unsqueeze(2).to_broadcast([P, 4, P]),
                                    ALU.subtract).then_inc(s_same, 1)
                    g.wait_ge(s_same, i * 2 + 1)
                    g.sem_inc(s_dum, 1)
                    g.tensor_tensor(same[:, :, :], same[:, :, :],
                                    notlater[:, :].unsqueeze(1).to_broadcast([P, 4, P]), ALU.add).then_inc(s_same, 1)

            @block.sync
            def _(sp):
                lo = sp.value_load(table[0:1, 3 * NT:3 * NT + 1], min_val=0, max_val=NCH - 1)
                n = sp.value_load(table[0:1, 3 * NT + 1:3 * NT + 2], min_val=1, max_val=(NCH + 3) // 4)
                with sp.Fori(0, n) as i:
                    c = chunk(lo + i * 4, NG * P - 4)
                    sp.wait_ge(s_kdone, i + 1)
                    sp.dma_start(keyr[:, :, :], keyd[ds(c, 4), :].unsqueeze(0).to_broadcast([P, 4, P])
                                 ).then_inc(s_key, 16)

            @block.scalar
            def _(a):
                lo = a.value_load(table[0:1, 3 * NT:3 * NT + 1], min_val=0, max_val=NCH - 1)
                n = a.value_load(table[0:1, 3 * NT + 1:3 * NT + 2], min_val=1, max_val=(NCH + 3) // 4)
                a.sem_inc(s_late, 1)
                a.sem_inc(s_kdone, 1)
                with a.Fori(0, n) as i:
                    c = chunk(lo + i * 4, NG * P - 4)
                    a.wait_ge(s_same, i * 2 + 2)
                    a.activation(junk[:, :, :], same[:, :, :], ACT.Abs).then_inc(s_abs, 1)
                    a.wait_ge(s_abs, i + 1)
                    for u in range(4):
                        ins = a.activation(same[:, u, :], junk[:, u, :], ACT.Relu, bias=1.0, scale=-1.0,
                                           accum_out=late[:, ds(c + u, 1)])
                        ins.then_inc(s_late, 1)
                    a.wait_ge(s_late, i * 4 + 5)
                    a.sem_inc(s_kdone, 1)

            @block.vector
            def _(v):
                v.wait_ge(s_c, 2)
                with v.Fori(0, NT) as t:
                    first = v.value_load(table[0:1, ds(t, 1)], min_val=0, max_val=NCH - 1)
                    pairs = v.value_load(table[0:1, ds(t + NT, 1)], min_val=2, max_val=(NCH + 1) // 2 + 1)
                    before = v.value_load(table[0:1, ds(t + 2 * NT, 1)], min_val=0, max_val=NT * NCH)
                    with v.Fori(0, pairs) as i:
                        for u in range(2):
                            k = chunk(first + i * 2 + u, NG * P - 1)
                            v.wait_ge(s_used, (before + i) * 2 + u + 1)
                            v.tensor_scalar(ohs[:, u, :], node16[:, :], srcT[:, ds(k, 1)], None,
                                            ALU.is_equal).then_inc(s_oh, 1)
                            v.tensor_scalar(ohd[:, u, :], node16[:, ds(t * P, P)], dstT[:, ds(k, 1)], None,
                                            ALU.is_equal).then_inc(s_oh, 1)
                    v.wait_ge(s_used, (before + pairs) * 2 + 2)
                    for b in range(NB):
                        dest = C[:, :].rearrange("p (s d) -> p s d", d=NP)[:, b * PERBANK:(b + 1) * PERBANK, ds(t * P, P)]
                        v.tensor_copy(dest, acc[:, b * PERBANK * P:(b + 1) * PERBANK * P].rearrange(
                            "p (s d) -> p s d", d=P)).then_inc(s_out, 1)

            @block.tensor
            def _(pe):
                pe.sem_inc(s_used, 2)
                pe.sem_inc(s_out, NB)
                with pe.Fori(0, NT) as t:
                    pairs = pe.value_load(table[0:1, ds(t + NT, 1)], min_val=2, max_val=(NCH + 1) // 2 + 1)
                    before = pe.value_load(table[0:1, ds(t + 2 * NT, 1)], min_val=0, max_val=NT * NCH)

                    def pair(i, opening):
                        for u in range(2):
                            pe.wait_ge(s_oh, (before + i) * 4 + u * 2 + 2)
                            for s in range(NT):
                                if opening and u == 0 and s % PERBANK == 0:
                                    pe.wait_ge(s_out, t * NB + s // PERBANK + 1)
                                m = pe.matmul(acc[:, s * P:(s + 1) * P], ohs[:, u, s * P:(s + 1) * P], ohd[:, u, :],
                                              start=opening and u == 0 and s % PERBANK == 0, stop=True,
                                              skip_group_check=True)
                            m.then_inc(s_used, 1)

                    pair(0, True)
                    with pe.Fori(1, pairs) as i:
                        pair(i, False)

        with Phase() as ph:
            s_w = ph.sem("w")
            block = ph.enter_context(nc.Block())

            @block.vector
            def _(v):
                v.scalar_tensor_tensor(widx[:, :], late[:, :], float(OOB), wcell[:, :], ALU.mult, ALU.add).then_inc(s_w, 1)
        edge.close()

        XB = R[:, 0:NT * D]
        X2 = R[:, NT * D:2 * NT * D]
        dum = top.enter_context(nc.semaphore("dum"))

        def hold(eng, sem, value):
            eng.wait_ge(sem, value)
            eng.sem_inc(dum, 1)

        def bc(ap, shape):
            return ap.to_broadcast(shape)

        def norm_memory(ph):
            return {**{n: ph.sb(n, [P, w * NT], f32) for n, w in (("st", 6), ("mv", 2), ("sd", 1), ("nmr", 1))},
                    **{n: ph.sem(n) for n in ("s_add", "s_bn", "s_mv", "s_sd", "s_rs")}}

        def norm_vector(v, m, residual=None):
            with v.Fori(0, NT) as t:
                tile = XB[:, ds(t * D, D)]
                if residual is not None:
                    v.tensor_tensor(tile, tile, residual[:, ds(t * D, D)], ALU.add).then_inc(m["s_add"], 1)
                    v.wait_ge(m["s_add"], t + 1)
                v.bn_stats(m["st"][:, ds(t * 6, 6)], tile).then_inc(m["s_bn"], 1)
            v.wait_ge(m["s_bn"], NT)
            for t in range(NT):
                last = v.bn_aggr(m["mv"][:, 2 * t:2 * t + 2], m["st"][:, 6 * t:6 * t + 6])
            last.then_inc(m["s_mv"], 1)
            v.wait_ge(m["s_sd"], 1)
            v.reciprocal(m["sd"][:, :], m["sd"][:, :]).then_inc(m["s_rs"], 1)
            v.wait_ge(m["s_rs"], 1)
            mean = m["mv"][:, :].rearrange("p (t c) -> p t c", c=2)[:, :, 0]
            v.scalar_tensor_tensor(m["nmr"][:, :], mean, -1.0, m["sd"][:, :], ALU.mult, ALU.mult).then_inc(m["s_rs"], 1)

        def norm_scalar(a, m):
            a.wait_ge(m["s_mv"], 1)
            var = m["mv"][:, :].rearrange("p (t c) -> p t c", c=2)[:, :, 1]
            a.activation(m["sd"][:, :], var, ACT.Sqrt, bias=eps[:, 0:1]).then_inc(m["s_sd"], 1)
            a.wait_ge(m["s_rs"], 2)

        def attention(gat, nh, dh, split, norm, sgn, AB, scatter):
            K = D // P
            W2 = D + 2 * nh
            ABv = AB[:, 0:NT * 2 * nh].rearrange("p (t c) -> p t c", c=2 * nh)
            with Phase() as ph:
                Wx = ph.sb("Wx", [P, K, W2], f32)
                av = ph.sb("av", [P, 2, D], f32)
                prod = ph.sb("prod", [P, 2 * K, D], f32)
                xn = ph.sb("xn", [P, 2, D], f32)
                xT = ph.sb("xT", [P, 2, D], f32)
                rT = ph.sb("rT", [nh, NP], f32)
                m_ = norm_memory(ph) if norm else None
                psT = [ph.ps(f"psT{u}", [P, D]) for u in range(2)]
                psH = [ph.ps(f"psH{u}", [P, W2]) for u in range(2)]
                psR = [ph.ps(f"psR{u}", [nh, P]) for u in range(2)]
                s_w, s_wx, s_xn, s_T, s_xT, s_M, s_out, s_rb, s_v, s_rd = (
                    ph.sem(n) for n in ("w", "wx", "xn", "T", "xT", "M", "out", "rb", "v", "rd"))
                block = ph.enter_context(nc.Block())
                @block.sync
                def _(sp):
                    if split:
                        for h in range(nh):
                            sp.dma_start(Wx[:, :, h * dh:(h + 1) * dh],
                                         gat[0][h].rearrange("(k p) f -> p k f", p=P)).then_inc(s_w, 16)
                            for j in range(2):
                                sp.dma_start(av[:, 1 - j, h * dh:(h + 1) * dh],
                                             gat[1][h, :, j * dh:(j + 1) * dh].to_broadcast([P, dh])).then_inc(s_w, 16)
                    else:
                        sp.dma_start(Wx[:, :, 0:D], gat[0].rearrange("(k p) f -> p k f", p=P)).then_inc(s_w, 16)
                        for j in range(2):
                            sp.dma_start(av[:, j, :], gat[1 + j].rearrange("(a h) d -> a (h d)", a=1)
                                         .to_broadcast([P, D])).then_inc(s_w, 16)
                    sp.wait_ge(s_rb, NT + 2)
                    sp.dma_start(rowd[0:nh, :], rT[:, :]).then_inc(s_rd, 16)
                    sp.wait_ge(s_rd, 16)

                @block.vector
                def _(v):
                    ch = Chain(v, s_v)
                    v.wait_ge(s_w, 16 * (3 * nh if split else 3))
                    for k in range(K):
                        for j in range(2):
                            ch(v.tensor_tensor(prod[:, 2 * k + j, :], Wx[:, k, 0:D], av[:, j, :], ALU.mult))
                    ch.wait()
                    for k in range(K):
                        for j in range(2):
                            last = v.tensor_reduce(Wx[:, k, D + j * nh:D + (j + 1) * nh],
                                                   prod[:, 2 * k + j, :].rearrange("p (h d) -> p h d", d=dh), AX.X,
                                                   ALU.add)
                    last.then_inc(s_wx, 1)
                    if norm:
                        norm_vector(v, m_)
                    v.sem_inc(s_out, 4)
                    with v.Fori(0, NT // 2) as i:
                        for u in range(2):
                            t = i * 2 + u
                            hold(v, s_M, t + 3)
                            v.tensor_copy(AB[:, ds(t * 2 * nh, 2 * nh)], psH[u][:, D:W2]).then_inc(s_out, 1)
                            v.tensor_copy(HB[:, ds(t * D, D)], psH[u][:, 0:D]).then_inc(s_out, 1)

                @block.scalar
                def _(a):
                    if norm:
                        norm_scalar(a, m_)
                    with a.Fori(0, NT // 2) as i:
                        for u in range(2):
                            t = i * 2 + u
                            hold(a, s_T, t + 1)
                            if norm:
                                a.activation(xn[:, u, :], XB[:, ds(t * D, D)], ACT.Relu, bias=m_["nmr"][:, ds(t, 1)],
                                             scale=m_["sd"][:, ds(t, 1)]).then_inc(s_xn, 1)
                            else:
                                a.activation(xn[:, u, :], XB[:, ds(t * D, D)], ACT.Copy).then_inc(s_xn, 1)
                        for u in range(2):
                            t = i * 2 + u
                            hold(a, s_T, t + 3)
                            hold(a, s_M, t + 1)
                            a.activation(xT[:, u, :], psT[u][:, :], ACT.Copy).then_inc(s_xT, 1)
                        for u in range(2):
                            t = i * 2 + u
                            hold(a, s_M, t + 3)
                            a.activation(rT[:, ds(t * P, P)], psR[u][:, :], ACT.Copy).then_inc(s_rb, 1)

                @block.tensor
                def _(pe):
                    pe.sem_inc(s_T, 2)
                    pe.sem_inc(s_M, 2)
                    pe.sem_inc(s_xT, 2)
                    pe.sem_inc(s_rb, 2)
                    pe.wait_ge(s_wx, 1)
                    with pe.Fori(0, NT // 2) as i:
                        for u in range(2):
                            t = i * 2 + u
                            hold(pe, s_xn, t + 1)
                            hold(pe, s_xT, t + 1)
                            for k in range(K):
                                m = pe.transpose(psT[u][:, k * P:(k + 1) * P], xn[:, u, k * P:(k + 1) * P], ident[:, :])
                            m.then_inc(s_T, 1)
                        for u in range(2):
                            t = i * 2 + u
                            hold(pe, s_xT, t + 3)
                            hold(pe, s_out, t * 2 + 2)
                            hold(pe, s_rb, t + 1)
                            for k in range(K):
                                pe.matmul(psH[u][:, :], xT[:, u, k * P:(k + 1) * P], Wx[:, k, :], start=k == 0, stop=k == K - 1)
                            for k in range(K):
                                m = pe.matmul(psR[u][:, :], Wx[:, k, D + nh:W2], xT[:, u, k * P:(k + 1) * P],
                                              start=k == 0, stop=k == K - 1)
                            m.then_inc(s_M, 1)

            cw = dh + 1
            S2 = nh * 2 * cw
            UV = Rh[:, 0:NT * 2 * S2].rearrange("p (t l c) -> p t l c", l=2, c=S2)
            TH = NT * nh
            heads = Phase()
            with heads as hp:
                cB, nC = hp.sb("cB", [P, TH], f32), hp.sb("nC", [P, TH], f32)
                F1, F2 = hp.sb("F1", [P, TH], f32), hp.sb("F2", [P, TH], f32)
                with Phase() as ph:
                    U, V = ph.sb("U", [P, TH], f32), ph.sb("V", [P, TH], f32)
                    XC, tt = ph.sb("XC", [P, TH], f32), ph.sb("tt", [P, TH], f32)
                    tt2 = ph.sb("tt2", [P, TH], f32)
                    top1, most = ph.sb("top1", [P, nh + 1], f32), ph.sb("most", [P, nh + 1], f32)
                    kap = ph.sb("kap", [P, 1], f32)
                    F = ph.sb("F", [P, 2, S2], f32)
                    L = ph.sb("L", [P, 2, S2], f32)
                    s_v, s_top, s_all, s_e, s_ex, s_F, s_hi, s_lo = (ph.sem(n) for n in ("v", "top", "all", "e", "ex", "F", "hi", "lo"))
                    block = ph.enter_context(nc.Block())
                    th = lambda q: q[:, :].rearrange("p (t h) -> p t h", h=nh)
                    cv, rv = ABv[:, :, 0:nh], ABv[:, :, nh:2 * nh]

                    @block.gpsimd
                    def _(g):
                        g.wait_ge(s_top, 1)
                        g.partition_all_reduce(most[:, :], top1[:, :], P, bass.bass_isa.ReduceOp.max).then_inc(s_all, 1)

                    @block.vector
                    def _(v):
                        ch = Chain(v, s_v)
                        ch(v.tensor_scalar(th(XC), cv, float(sgn), None, ALU.mult))
                        ch(v.tensor_scalar(th(cB), cv, BIG, None, ALU.mult))
                        ch(v.tensor_scalar(th(nC), cv, -1.0, None, ALU.mult))
                        ch(v.tensor_reduce(top1[:, nh:nh + 1], HB[:, 0:NT * D], AX.X, ALU.max, apply_absolute_value=True))
                        ch.wait()
                        ch(v.tensor_scalar(XC[:, TH - nh:TH], XC[:, TH - nh:TH], padneg[:, 0:1], None, ALU.add))
                        ch.wait()
                        ch(v.tensor_reduce(top1[:, 0:nh], XC[:, :].rearrange("p (t h) -> p h t", h=nh), AX.X, ALU.max))
                        ch.wait()
                        v.sem_inc(s_top, 1)
                        v.wait_ge(s_all, 1)
                        A = most[:, 0:nh].unsqueeze(1).to_broadcast([P, NT, nh])
                        ch(v.tensor_tensor(th(XC), th(XC), A, ALU.subtract))
                        ch(v.tensor_tensor(th(tt), rv, A, ALU.add if sgn > 0 else ALU.subtract))
                        ch(v.tensor_scalar(kap[:, :], most[:, nh:nh + 1], 1.0, None, ALU.max))
                        ch.wait()
                        if sgn > 0:
                            ch(v.tensor_scalar(tt2[:, :], tt[:, :], -(1 - SLOPE), 0.0, ALU.mult, ALU.min))
                            ch.wait()
                            ch(v.tensor_scalar(tt[:, :], tt[:, :], 1 - SLOPE, 0.0, ALU.mult, ALU.min))
                        else:
                            ch(v.tensor_scalar(tt2[:, :], tt[:, :], 1 - SLOPE, 0.0, ALU.mult, ALU.max))
                            ch.wait()
                            ch(v.tensor_scalar(tt[:, :], tt[:, :], -(1 - SLOPE), 0.0, ALU.mult, ALU.max))
                            ch.wait()
                            ch(v.tensor_scalar(tt2[:, :], tt2[:, :], 80.0, None, ALU.min))
                            ch(v.tensor_scalar(tt[:, :], tt[:, :], 80.0, None, ALU.min))
                        ch(v.reciprocal(kap[:, :], kap[:, :]))
                        ch.wait()
                        v.tensor_scalar(kap[:, :], kap[:, :], TOP, None, ALU.mult).then_inc(s_e, 1)
                        v.wait_ge(s_ex, 4)
                        ch(v.tensor_scalar(U[:, :], U[:, :], kap[:, 0:1], None, ALU.mult))
                        ch(v.tensor_scalar(V[:, :], V[:, :], kap[:, 0:1], None, ALU.mult))
                        ch.wait()
                        v.sem_inc(s_lo, 2)
                        with v.Fori(0, NT // 2) as i:
                            for u in range(2):
                                t = i * 2 + u
                                Fv = F[:, u, :].rearrange("p (h w c) -> p h w c", w=2, c=cw)
                                Ht = HB[:, ds(t * D, D)].rearrange("p (h d) -> p h d", d=dh)
                                hold(v, s_hi, t * 2 + 2)
                                for w, q in enumerate((U, V)):
                                    qt = q[:, ds(t * nh, nh)].unsqueeze(2)
                                    v.tensor_tensor(Fv[:, :, w, 0:dh], Ht, qt.to_broadcast([P, nh, dh]),
                                                    ALU.mult).then_inc(s_F, 1)
                                    v.tensor_copy(Fv[:, :, w, dh:cw], qt).then_inc(s_F, 1)
                            for u in range(2):
                                t = i * 2 + u
                                hold(v, s_hi, t * 2 + 6)
                                v.scalar_tensor_tensor(UV[:, ds(t, 1), 1, :], UV[:, ds(t, 1), 0, :], -LO,
                                                       L[:, u, :].unsqueeze(1), ALU.mult, ALU.add).then_inc(s_lo, 1)

                    @block.scalar
                    def _(a):
                        a.sem_inc(s_hi, 4)
                        a.wait_ge(s_e, 1)
                        a.activation(U[:, :], XC[:, :], ACT.Exp).then_inc(s_ex, 1)
                        a.activation(V[:, :], XC[:, :], ACT.Exp, scale=SLOPE).then_inc(s_ex, 1)
                        a.activation(F1[:, :], tt[:, :], ACT.Exp).then_inc(s_ex, 1)
                        a.activation(F2[:, :], tt2[:, :], ACT.Exp).then_inc(s_ex, 1)
                        with a.Fori(0, NT // 2) as i:
                            for u in range(2):
                                t = i * 2 + u
                                hold(a, s_F, t * 4 + 4)
                                hold(a, s_lo, t + 1)
                                a.activation(UV[:, ds(t, 1), 0, :], F[:, u, :].unsqueeze(1), ACT.Copy).then_inc(s_hi, 1)
                                a.activation(L[:, u, :], F[:, u, :], ACT.Copy, scale=LO).then_inc(s_hi, 1)

                if not split:
                    GW = nh * cw
                    with Phase() as ph:
                        tl = ph.sb("tl", [P, 2, GW], f32)
                        psG = [[ph.ps(f"psG{u}{l}", [P, GW]) for l in range(2)] for u in range(2)]
                        s_g, s_l, s_out = (ph.sem(n) for n in ("g", "l", "out"))
                        block = ph.enter_context(nc.Block())

                        @block.tensor
                        def _(pe):
                            pe.sem_inc(s_out, 2)
                            with pe.Fori(0, NT // 2) as i:
                                for u in range(2):
                                    t = i * 2 + u
                                    hold(pe, s_out, t + 1)
                                    for s in range(NT):
                                        lhsT = C[:, ds(t * P + s * NP, P)]
                                        for l in range(2):
                                            rhs = UV[:, s, l, :].rearrange("p (h w c) -> p h w c", w=2, c=cw)[:, :, 1, :]
                                            m = pe.matmul(psG[u][l][:, :], lhsT, rhs, start=s == 0, stop=s == NT - 1)
                                    m.then_inc(s_g, 1)

                        @block.scalar
                        def _(a):
                            a.sem_inc(s_l, 2)
                            with a.Fori(0, NT // 2) as i:
                                for u in range(2):
                                    t = i * 2 + u
                                    hold(a, s_g, t + 1)
                                    hold(a, s_out, t + 1)
                                    a.activation(tl[:, u, :], psG[u][1][:, :], ACT.Copy, scale=1 / LO).then_inc(s_l, 1)

                        @block.vector
                        def _(v):
                            with v.Fori(0, NT // 2) as i:
                                for u in range(2):
                                    t = i * 2 + u
                                    hold(v, s_l, t + 3)
                                    v.tensor_tensor(HB[:, ds(t * GW, GW)], psG[u][0][:, :], tl[:, u, :],
                                                    ALU.add).then_inc(s_out, 1)

                PARTS = 4 if split else 2
                TP = NT // PARTS
                W = TP * P
                RG = 10
                NB = (RG + 2) // 3
                SG = 4
                KR = NT // SG
                assert RG == TP * (2 if split else 1)
                with Phase() as ph:
                    rows = ph.sb("rows", [P, 2, W], f32)
                    Rm = ph.sb("Rm", [P, SG, W], bf16)
                    M = ph.sb("M", [P, SG, W], f16)
                    Mn = ph.sb("Mn", [P, SG, W], f16) if split else None
                    tl = ph.sb("tl", [P, RG, cw if split else 2 * cw], f32)
                    X = ph.sb("X", [P, RG, cw if split else 2 * cw], f32)
                    q1 = ph.sb("q1", [P, TP, cw], f32)
                    rec = ph.sb("rec", [P, TP], f32)
                    if scatter:
                        wi, wv = ph.sb("wi", [P, 1], i32), ph.sb("wv", [P, 1], f32)
                    XW = cw if split else 2 * cw
                    ps = [[ph.ps(f"ps{b}{j}", [P, 3 * 2 * XW]) for j in range(NB)] for b in range(2)]
                    s_row = [ph.sem(f"row{b}") for b in range(2)]
                    s_R, s_M, s_cut, s_D, s_P, s_E, s_tl, s_v, s_wc, s_wd = (
                        ph.sem(n) for n in ("R", "M", "cut", "D", "P", "E", "tl", "v", "wc", "wd"))
                    block = ph.enter_context(nc.Block())

                    def region(b, r, l0=0, l1=2):
                        return ps[b][r // 3][:, (r % 3) * 2 * XW + l0 * XW:(r % 3) * 2 * XW + l1 * XW]

                    def banks(b, l):
                        for j in range(NB):
                            n = min(3, RG - 3 * j)
                            yield 3 * j, n, ps[b][j][:, 0:n * 2 * XW].rearrange("p (r l c) -> p r l c", l=2, c=XW)[:, :, l, :]

                    @block.sync
                    def _(sp):
                        with sp.Fori(0, nh) as h:
                            for p in range(PARTS):
                                sp.wait_ge(s_M, (h * PARTS + p) * NT + NT)
                                sp.dma_start(rows[:, p % 2, :], rowd[ds(h, 1), p * W:(p + 1) * W].to_broadcast([P, W])
                                             ).then_inc(s_row[p % 2], 16)

                    def landed(eng, h, p):
                        hold(eng, s_row[p % 2], (h * (PARTS // 2) + p // 2 + 1) * 16)

                    @block.scalar
                    def _(a):
                        with a.Fori(0, nh) as h:
                            for p in range(PARTS):
                                q = h * PARTS + p
                                landed(a, h, p)
                                with a.Fori(0, KR) as k:
                                    for u in range(SG - 1):
                                        g = q * NT + k * SG + u
                                        hold(a, s_M, g + 1 + 2 * NT - SG)
                                        a.activation(Rm[:, u, :], rows[:, p % 2, :], ACT.Relu,
                                                     bias=cB[:, ds((k * SG + u) * nh + h, 1)], scale=BIG).then_inc(s_R, 1)
                                hold(a, s_P, (q + 1) * NT + SG)
                                hold(a, s_E, q + 2)
                                for r, n, part in banks(p % 2, 1):
                                    ins = a.activation(tl[:, r:r + n, :], part, ACT.Copy, scale=1 / LO)
                                ins.then_inc(s_tl, 1)

                    @block.vector
                    def _(v):
                        v.sem_inc(s_M, 2 * NT)
                        v.sem_inc(s_E, 2)
                        ch = Chain(v, s_v)
                        with v.Fori(0, nh) as h:
                            per = PARTS * (NB + (6 if split else 7))
                            ch.begin(h, per)
                            for p in range(PARTS):
                                q = h * PARTS + p
                                landed(v, h, p)
                                with v.Fori(0, KR) as k:
                                    for u in range(SG):
                                        g = q * NT + k * SG + u
                                        if u < SG - 1:
                                            v.wait_ge(s_R, (q * KR + k) * (SG - 1) + u + 1)
                                        else:
                                            v.wait_ge(s_M, g + 1 + 2 * NT - SG)
                                            v.tensor_scalar(Rm[:, u, :], rows[:, p % 2, :],
                                                            nC[:, ds((k * SG + u) * nh + h, 1)], BIG, ALU.is_gt,
                                                            ALU.mult).then_inc(s_D, 1)
                                            v.wait_ge(s_D, q * KR + k + 1)
                                        v.wait_ge(s_P, g + 1)
                                        Cs = C[:, ds((k * SG + u) * NP + p * W, W)]
                                        v.tensor_tensor(M[:, u, :], Rm[:, u, :], Cs, ALU.min).then_inc(s_cut if split else s_M, 1)
                                        if split:
                                            v.wait_ge(s_cut, g + 1)
                                            v.tensor_tensor(Mn[:, u, :], Cs, M[:, u, :], ALU.subtract).then_inc(s_M, 1)
                                hold(v, s_tl, q + 1)
                                for r, n, part in banks(p % 2, 0):
                                    ch(v.tensor_tensor(X[:, r:r + n, :], part, tl[:, r:r + n, :], ALU.add))
                                ch.wait()
                                v.sem_inc(s_E, 1)
                                one = lambda Fq: Fq[:, :].rearrange("p (t h) -> p t h", h=nh)[
                                    :, p * TP:(p + 1) * TP, ds(h, 1)].to_broadcast([P, TP, cw])
                                if split:
                                    xu, xv = X[:, 0:TP, :], X[:, TP:2 * TP, :]
                                    ch(v.tensor_tensor(xv, xv, one(F2), ALU.mult))
                                    ch(v.tensor_tensor(q1[:, :, :], xu, one(F1), ALU.mult))
                                    ch.wait()
                                    ch(v.tensor_tensor(q1[:, :, :], q1[:, :, :], xv, ALU.add))
                                else:
                                    xu, xv = X[:, :, 0:cw], X[:, :, cw:2 * cw]
                                    Gq = HB[:, :].rearrange("p (t c) -> p t c", c=nh * cw)[:, p * TP:(p + 1) * TP, ds(h * cw, cw)]
                                    ch(v.tensor_tensor(xv, Gq, xv, ALU.subtract))
                                    ch(v.tensor_tensor(q1[:, :, :], xu, one(F1), ALU.mult))
                                    ch.wait()
                                    ch(v.tensor_tensor(xv, xv, one(F2), ALU.mult))
                                    ch.wait()
                                    ch(v.tensor_tensor(q1[:, :, :], q1[:, :, :], xv, ALU.add))
                                ch.wait()
                                ch(v.tensor_scalar(rec[:, :], q1[:, :, dh], 1e-30, None, ALU.max))
                                ch.wait()
                                ch(v.reciprocal(rec[:, :], rec[:, :]))
                                ch.wait()
                                o = HB[:, 0:NT * nh * cw].rearrange("p (t c) -> p t c", c=nh * cw)[
                                    :, p * TP:(p + 1) * TP, ds(h * cw, dh)]
                                ch(v.tensor_tensor(o, q1[:, :, 0:dh], rec[:, :].unsqueeze(2).to_broadcast([P, TP, dh]),
                                                   ALU.mult))
                            ch.end(nh)

                    @block.tensor
                    def _(pe):
                        pe.sem_inc(s_P, SG)

                        def step(h, p, s, u, opening):
                            for r in range(RG):
                                first = opening and r % 3 == 0
                                if split:
                                    lhsT = (M, Mn)[r // TP][:, u, (r % TP) * P:(r % TP + 1) * P]
                                    rhs = UV[:, ds(s, 1), :, ds(h * 2 * cw + (r // TP) * cw, cw)]
                                else:
                                    lhsT = M[:, u, r * P:(r + 1) * P]
                                    rhs = UV[:, ds(s, 1), :, ds(h * 2 * cw, 2 * cw)]
                                m = pe.matmul(region(p % 2, r), lhsT, rhs.rearrange("p a l c -> p (a l) c"),
                                              start=first, stop=True, skip_group_check=True)
                            m.then_inc(s_P, 1)

                        with pe.Fori(0, nh) as h:
                            for p in range(PARTS):
                                q = h * PARTS + p
                                hold(pe, s_E, q + 1)
                                for u in range(SG):
                                    hold(pe, s_M, q * NT + u + 1 + 2 * NT)
                                    step(h, p, u, u, u == 0)
                                with pe.Fori(1, KR) as k:
                                    for u in range(SG):
                                        hold(pe, s_M, q * NT + k * SG + u + 1 + 2 * NT)
                                        step(h, p, k * SG + u, u, False)

                    if scatter:
                        @block.gpsimd
                        def _(g):
                            lo = g.value_load(table[0:1, 3 * NT:3 * NT + 1], min_val=0, max_val=NCH - 1)
                            n = g.value_load(table[0:1, 3 * NT + 1:3 * NT + 2], min_val=1, max_val=(NCH + 3) // 4)

                            def write(i, c, opening):
                                if not opening:
                                    hold(g, s_wd, i * 16)
                                g.tensor_copy(wi[:, :], widx[:, ds(c, 1)]).then_inc(s_wc, 1)
                                g.tensor_copy(wv[:, :], ewT[:, ds(c, 1)]).then_inc(s_wc, 1)
                                hold(g, s_wc, i * 2 + 2)
                                g.indirect_dma_start(out=wd[:, :], out_offset=bass.IndirectOffsetOnAxis(ap=wi[:, :], axis=0),
                                                     in_=wv[:, :], in_offset=None, bounds_check=D * D - 1,
                                                     oob_is_err=False).then_inc(s_wd, 16)

                            write(0, lo, True)
                            with g.Fori(1, n * 4) as i:
                                write(i, chunk(lo + i, NG * P - 1), False)
                            hold(g, s_wd, n * 64)

        def elu_into_xb(bias_dram, nh, twice):
            cw = D // nh + 1
            TB = 4
            BW = TB * D
            with Phase() as ph:
                bias = ph.sb("bias", [P, D], f32)
                e = ph.sb("e", [P, BW], f32)
                s_b, s_v, s_y, s_e, s_ee, s_o = (ph.sem(n) for n in ("b", "v", "y", "e", "ee", "o"))
                block = ph.enter_context(nc.Block())
                rounds = 2 if twice else 1

                if bias_dram is not None:
                    @block.sync
                    def _(sp):
                        sp.dma_start(bias[:, :], bias_dram.rearrange("(a f) -> a f", a=1).to_broadcast([P, D])).then_inc(s_b, 16)

                @block.vector
                def _(v):
                    v.sem_inc(s_o, 1)
                    if bias_dram is not None:
                        v.wait_ge(s_b, 16)
                    with v.Fori(0, NT // TB) as i:
                        y = XB[:, ds(i * BW, BW)]
                        yh = y.rearrange("p (t h c) -> p t h c", c=cw - 1, h=nh)
                        src_ = HB[:, ds(i * (TB * nh * cw), TB * nh * cw)].rearrange("p (t h c) -> p t h c", c=cw, h=nh)[:, :, :, 0:cw - 1]
                        for j in range(TB):
                            if bias_dram is not None:
                                v.tensor_tensor(yh[:, j], src_[:, j], bias[:, :].rearrange("p (h c) -> p h c", c=cw - 1),
                                                ALU.add).then_inc(s_b, 1)
                            else:
                                v.tensor_copy(yh[:, j], src_[:, j]).then_inc(s_b, 1)
                        hold(v, s_b, i * TB + TB + (16 if bias_dram is not None else 0))
                        hold(v, s_o, i + 1)
                        for w in range(rounds):
                            n = i * rounds + w
                            if w:
                                hold(v, s_y, i + 1)
                            v.tensor_scalar(e[:, :], y, 0.0, None, ALU.min).then_inc(s_e, 1)
                            hold(v, s_ee, n + 1)
                            v.tensor_scalar(y, y, 0.0, -1.0, ALU.max, ALU.add).then_inc(s_v, 1)
                            hold(v, s_v, n + 1)
                            v.tensor_tensor(y, y, e[:, :], ALU.add).then_inc(s_y if w + 1 < rounds else s_o, 1)

                @block.scalar
                def _(a):
                    with a.Fori(0, NT // TB * rounds) as n:
                        hold(a, s_e, n + 1)
                        a.activation(e[:, :], e[:, :], ACT.Exp).then_inc(s_ee, 1)

        def load_rows(dest):
            with Phase() as ph:
                s_z, s_in = ph.sem("z"), ph.sem("in")
                block = ph.enter_context(nc.Block())

                @block.gpsimd
                def _(g):
                    g.memset(dest[:, (NT - 1) * D:NT * D], 0.0).then_inc(s_z, 1)

                @block.sync
                def _(sp):
                    sp.wait_ge(s_z, 1)
                    rows_in(sp, dest, x, s_in)
                    sp.wait_ge(s_in, 32)

        load_rows(XB)
        attention(gat0[0:3], 8, 32, False, True, 1, AB, True)
        elu_into_xb(gat0[3], 8, False)
        attention(gat1[0:3], 8, 32, False, False, 1, AB, False)
        elu_into_xb(gat1[3], 8, False)
        late_.close()
        K = D // P
        load_rows(HB)

        with Phase() as ph:
            Wl = ph.sb("Wl", [P, K, D], f32)
            xn, xT = ph.sb("xn", [P, 2, D], f32), ph.sb("xT", [P, 2, D], f32)
            m_ = norm_memory(ph)
            psT = [ph.ps(f"psT{u}", [P, D]) for u in range(2)]
            psH = [ph.ps(f"psH{u}", [P, D]) for u in range(2)]
            s_w, s_xn, s_T, s_xT, s_M, s_out = (ph.sem(n) for n in ("w", "xn", "T", "xT", "M", "out"))
            block = ph.enter_context(nc.Block())

            @block.sync
            def _(sp):
                sp.dma_start(Wl[:, :, :], wd.rearrange("(k p c) a -> p k (c a)", p=P, c=D)).then_inc(s_w, 16)

            @block.vector
            def _(v):
                norm_vector(v, m_, residual=HB)
                v.sem_inc(s_out, 2)
                with v.Fori(0, NT // 2) as i:
                    for u in range(2):
                        t = i * 2 + u
                        hold(v, s_M, t + 3)
                        v.tensor_tensor(XB[:, ds(t * D, D)], XB[:, ds(t * D, D)], psH[u][:, :], ALU.add).then_inc(s_out, 1)

            @block.scalar
            def _(a):
                norm_scalar(a, m_)
                with a.Fori(0, NT // 2) as i:
                    for u in range(2):
                        t = i * 2 + u
                        hold(a, s_T, t + 1)
                        a.activation(xn[:, u, :], XB[:, ds(t * D, D)], ACT.Relu, bias=m_["nmr"][:, ds(t, 1)],
                                     scale=m_["sd"][:, ds(t, 1)]).then_inc(s_xn, 1)
                    for u in range(2):
                        t = i * 2 + u
                        hold(a, s_T, t + 3)
                        hold(a, s_M, t + 1)
                        a.activation(xT[:, u, :], psT[u][:, :], ACT.Copy).then_inc(s_xT, 1)

            @block.tensor
            def _(pe):
                pe.sem_inc(s_T, 2)
                pe.sem_inc(s_M, 2)
                pe.sem_inc(s_xT, 2)
                pe.wait_ge(s_w, 16)
                with pe.Fori(0, NT // 2) as i:
                    for u in range(2):
                        t = i * 2 + u
                        hold(pe, s_xn, t + 1)
                        hold(pe, s_xT, t + 1)
                        for k in range(K):
                            m = pe.transpose(psT[u][:, k * P:(k + 1) * P], xn[:, u, k * P:(k + 1) * P], ident[:, :])
                        m.then_inc(s_T, 1)
                    for u in range(2):
                        t = i * 2 + u
                        hold(pe, s_xT, t + 3)
                        hold(pe, s_out, t + 1)
                        for k in range(K):
                            m = pe.matmul(psH[u][:, :], xT[:, u, k * P:(k + 1) * P], Wl[:, k, :], start=k == 0, stop=k == K - 1)
                        m.then_inc(s_M, 1)

        wn0, wr0, b0, wn1, wr1, b1, wn2, wr2, b2 = sage
        dw0, db0, dw1, db1, dw2, db2 = dec
        DL = (2 * D, D, P)
        SP = R[:, NT * D:2 * NT * D].bitcast(f16)
        sg = Phase()
        sg.__enter__()
        scale_ = sg.sb("scale", [P, 1], f32)
        rdk = sg.sb("rdk", [P, NT], f32)

        def parts(w, source, scaled):
            SPv = SP[:, 0:NT * 2 * w].rearrange("p (t l c) -> p t l c", l=2, c=w)
            with Phase() as ph:
                L = ph.sb("L", [P, 2, w], f32)
                lsc = ph.sb("lsc", [P, 1], f32)
                mx, mxa = ph.sb("mx", [P, 1], f32), ph.sb("mxa", [P, 1], f32)
                s_v, s_m, s_a, s_s, s_h, s_lo = (ph.sem(n) for n in ("v", "m", "a", "s", "h", "lo"))
                block = ph.enter_context(nc.Block())

                if scaled:
                    @block.gpsimd
                    def _(g):
                        g.wait_ge(s_m, 1)
                        g.partition_all_reduce(mxa[:, :], mx[:, :], P, bass.bass_isa.ReduceOp.max).then_inc(s_a, 1)

                @block.vector
                def _(v):
                    ch = Chain(v, s_v)
                    if scaled:
                        v.tensor_reduce(mx[:, :], source[:, 0:NT * w], AX.X, ALU.max, apply_absolute_value=True).then_inc(s_m, 1)
                        v.wait_ge(s_a, 1)
                        ch(v.tensor_scalar(mxa[:, :], mxa[:, :], 1e-20, None, ALU.max))
                        ch.wait()
                        ch(v.reciprocal(mx[:, :], mxa[:, :]))
                        ch(v.tensor_scalar(rdk[:, :], rdeg[:, :], mxa[:, 0:1], 1 / TOP, ALU.mult, ALU.mult))
                        ch.wait()
                        ch(v.tensor_scalar(scale_[:, :], mx[:, :], TOP, None, ALU.mult))
                    else:
                        ch(v.memset(scale_[:, :], TOP / 16))
                    ch.wait()
                    ch(v.tensor_scalar(lsc[:, :], scale_[:, :], LO, None, ALU.mult))
                    ch.wait()
                    v.sem_inc(s_s, 1)
                    v.sem_inc(s_lo, 2)
                    with v.Fori(0, NT // 2) as i:
                        for u in range(2):
                            t = i * 2 + u
                            hold(v, s_h, t * 2 + 2)
                            v.scalar_tensor_tensor(SPv[:, ds(t, 1), 1, :], SPv[:, ds(t, 1), 0, :], -LO,
                                                   L[:, u, :].unsqueeze(1), ALU.mult, ALU.add).then_inc(s_lo, 1)

                @block.scalar
                def _(a):
                    a.wait_ge(s_s, 1)
                    with a.Fori(0, NT // 2) as i:
                        for u in range(2):
                            t = i * 2 + u
                            hold(a, s_lo, t + 1)
                            a.activation(SPv[:, ds(t, 1), 0, :], source[:, ds(t * w, w)].unsqueeze(1), ACT.Copy,
                                         scale=scale_[:, 0:1]).then_inc(s_h, 1)
                            a.activation(L[:, u, :], source[:, ds(t * w, w)], ACT.Copy, scale=lsc[:, 0:1]).then_inc(s_h, 1)
            return SPv

        def neighbours(pe, psA, SPv, t, w, psD=None, ones=None):
            for s in range(NT):
                lhsT = C[:, ds(t * P + s * NP, P)]
                m = pe.matmul(psA[:, :], lhsT, SPv[:, s, :, :].rearrange("p l c -> p (l c)"), start=s == 0, stop=s == NT - 1)
                if psD is not None:
                    m = pe.matmul(psD, lhsT, ones, start=s == 0, stop=s == NT - 1)
            return m

        with Phase() as ph:
            m_ = norm_memory(ph)
            s_x, s_n = ph.sem("x"), ph.sem("n")
            block = ph.enter_context(nc.Block())

            @block.sync
            def _(sp):
                sp.dma_start(xd[:, :], XB).then_inc(s_x, 16)
                sp.wait_ge(s_x, 16)

            @block.vector
            def _(v):
                norm_vector(v, m_)

            @block.scalar
            def _(a):
                norm_scalar(a, m_)
                with a.Fori(0, NT) as t:
                    a.activation(HB[:, ds(t * D, D)], XB[:, ds(t * D, D)], ACT.Relu, bias=m_["nmr"][:, ds(t, 1)],
                                 scale=m_["sd"][:, ds(t, 1)]).then_inc(s_n, 1)

        SPv = parts(D, HB, False)
        H0, H1 = DL[0], DL[1]
        F0 = H0 // P
        with Phase() as ph:
            W0 = ph.sb("W0", [P, 2 * K, H0], f32)
            W1 = ph.sb("W1", [P, F0, 2 * H1], f32)
            b0c = ph.sb("b0c", [P, F0], f32)
            b1r = ph.sb("b1r", [P, H1], f32)
            ones = ph.sb("ones", [P, 1], f16)
            tl = ph.sb("tl", [P, 2, D], f32)
            xs = ph.sb("xs", [P, 2, 2 * D], f32)
            xT = ph.sb("xT", [P, 2, 4 * P], f32)
            hT = ph.sb("hT", [P, 2, F0 * P], f32)
            psA = [ph.ps(f"psA{u}", [P, 2 * D]) for u in range(2)]
            psD = [ph.ps(f"psD{u}", [P, 1]) for u in range(2)]
            psT = [ph.ps(f"psT{u}", [P, 4 * P]) for u in range(2)]
            ps1 = ph.ps("ps1", [P, F0 * P])
            psO = ph.ps("psO", [P, 2 * H1])
            s_c, s_w, s_A, s_tl, s_own, s_mean, s_T, s_xT, s_1, s_hT, s_O, s_out, s_v = (
                ph.sem(n) for n in ("c", "w", "A", "tl", "own", "mean", "T", "xT", "1", "hT", "O", "out", "v"))
            block = ph.enter_context(nc.Block())

            @block.gpsimd
            def _(g):
                g.memset(ones[:, :], 1.0).then_inc(s_c, 1)

            @block.sync
            def _(sp):
                for j, w in enumerate((wn0, wr0)):
                    sp.dma_start(W0[:, j * K:(j + 1) * K, :], w.rearrange("(k p) f -> p k f", p=P)).then_inc(s_w, 16)
                for j, w in enumerate((wn1, wr1)):
                    sp.dma_start(W1[:, :, j * H1:(j + 1) * H1], w.rearrange("(k p) f -> p k f", p=P)).then_inc(s_w, 16)
                with nc.allow_non_contiguous_dma("a bias of 512 elements, one to a partition"):
                    sp.dma_start(b0c[:, :], b0.rearrange("(f p) -> p f", p=P)).then_inc(s_w, 16)
                sp.dma_start(b1r[:, :], b1.rearrange("(a f) -> a f", a=1).to_broadcast([P, H1])).then_inc(s_w, 16)

            @block.tensor
            def _(pe):
                pe.sem_inc(s_xT, 2)
                pe.sem_inc(s_hT, 1)
                pe.wait_ge(s_c, 1)
                pe.wait_ge(s_w, 16 * 6)
                with pe.Fori(0, NT // 2) as i:
                    for u in range(2):
                        t = i * 2 + u
                        hold(pe, s_mean, t + 1)
                        neighbours(pe, psA[u], SPv, t, D, psD[u][:, :], ones[:, :]).then_inc(s_A, 1)
                    for u in range(2):
                        t = i * 2 + u
                        hold(pe, s_mean, t + 3)
                        hold(pe, s_own, t + 1)
                        hold(pe, s_xT, t + 1)
                        for k in range(4):
                            m = pe.transpose(psT[u][:, k * P:(k + 1) * P], xs[:, u, k * P:(k + 1) * P], ident[:, :])
                        m.then_inc(s_T, 1)
                    for u in range(2):
                        t = i * 2 + u
                        hold(pe, s_xT, t + 3)
                        hold(pe, s_hT, t + 1)
                        for f in range(F0):
                            for k in range(4):
                                m = pe.matmul(ps1[:, f * P:(f + 1) * P], W0[:, k, f * P:(f + 1) * P],
                                              xT[:, u, k * P:(k + 1) * P], start=k == 0, stop=k == 3)
                        m.then_inc(s_1, 1)
                    for u in range(2):
                        t = i * 2 + u
                        hold(pe, s_hT, t + 2)
                        hold(pe, s_out, t * 2 + 2)
                        for k in range(F0):
                            m = pe.matmul(psO[:, :], hT[:, u, k * P:(k + 1) * P], W1[:, k, :], start=k == 0, stop=k == F0 - 1)
                        m.then_inc(s_O, 1)

            @block.scalar
            def _(a):
                a.sem_inc(s_T, 2)
                a.sem_inc(s_O, 2)
                a.wait_ge(s_w, 16 * 6)
                with a.Fori(0, NT // 2) as i:
                    for u in range(2):
                        t = i * 2 + u
                        hold(a, s_T, t + 1)
                        a.activation(xs[:, u, D:2 * D], HB[:, ds(t * D, D)], ACT.Copy).then_inc(s_own, 1)
                        hold(a, s_mean, t + 1)
                        hold(a, s_A, t + 1)
                        a.activation(tl[:, u, :], psA[u][:, D:2 * D], ACT.Copy, scale=1 / LO).then_inc(s_tl, 1)
                    for u in range(2):
                        t = i * 2 + u
                        hold(a, s_T, t + 3)
                        a.activation(xT[:, u, :], psT[u][:, :], ACT.Copy).then_inc(s_xT, 1)
                    for u in range(2):
                        t = i * 2 + u
                        hold(a, s_1, t + 1)
                        hold(a, s_O, t + 1)
                        for f in range(F0):
                            ins = a.activation(hT[:, u, f * P:(f + 1) * P], ps1[:, f * P:(f + 1) * P], ACT.Relu, bias=b0c[:, f:f + 1])
                        ins.then_inc(s_hT, 1)

            @block.vector
            def _(v):
                v.sem_inc(s_mean, 2)
                v.sem_inc(s_out, 2)
                v.wait_ge(s_w, 16 * 6)
                with v.Fori(0, NT // 2) as i:
                    for u in range(2):
                        t = i * 2 + u
                        hold(v, s_tl, t + 1)
                        hold(v, s_xT, t + 1)
                        v.tensor_scalar(rdeg[:, ds(t, 1)], psD[u][:, :], 1.0, None, ALU.max).then_inc(s_v, 1)
                        v.tensor_tensor(xs[:, u, 0:D], psA[u][:, 0:D], tl[:, u, :], ALU.add).then_inc(s_v, 1)
                        hold(v, s_v, t * 4 + 2)
                        v.reciprocal(rdeg[:, ds(t, 1)], rdeg[:, ds(t, 1)]).then_inc(s_v, 1)
                        hold(v, s_v, t * 4 + 3)
                        v.tensor_scalar(xs[:, u, 0:D], xs[:, u, 0:D], rdeg[:, ds(t, 1)], 16 / TOP, ALU.mult, ALU.mult).then_inc(s_mean, 1)
                        v.sem_inc(s_v, 1)
                    for u in range(2):
                        t = i * 2 + u
                        hold(v, s_O, t + 3)
                        v.tensor_copy(XB[:, ds(t * H1, H1)], psO[:, 0:H1]).then_inc(s_out, 1)
                        v.tensor_tensor(HB[:, ds(t * H1, H1)], psO[:, H1:2 * H1], b1r[:, :], ALU.add).then_inc(s_out, 1)

        SPv = parts(D, XB, True)
        H2 = DL[2]
        with Phase() as ph:
            W2 = ph.sb("W2", [P, K, 2 * H2], f32)
            b2r = ph.sb("b2r", [P, H2], f32)
            tl = ph.sb("tl", [P, 2, D], f32)
            xs = ph.sb("xs", [P, 2, D], f32)
            xT = ph.sb("xT", [P, 2, D], f32)
            psA = [ph.ps(f"psA{u}", [P, 2 * D]) for u in range(2)]
            psT = [ph.ps(f"psT{u}", [P, D]) for u in range(2)]
            psO = [ph.ps(f"psO{u}", [P, 2 * H2]) for u in range(2)]
            s_w, s_A, s_tl, s_x, s_T, s_xT, s_O, s_out, s_v = (
                ph.sem(n) for n in ("w", "A", "tl", "x", "T", "xT", "O", "out", "v"))
            block = ph.enter_context(nc.Block())

            @block.sync
            def _(sp):
                for j, w in enumerate((wn2, wr2)):
                    sp.dma_start(W2[:, :, j * H2:(j + 1) * H2], w.rearrange("(k p) f -> p k f", p=P)).then_inc(s_w, 16)
                sp.dma_start(b2r[:, :], b2.rearrange("(a f) -> a f", a=1).to_broadcast([P, H2])).then_inc(s_w, 16)

            @block.tensor
            def _(pe):
                pe.sem_inc(s_xT, 2)
                pe.wait_ge(s_w, 16 * 3)
                with pe.Fori(0, NT // 2) as i:
                    for u in range(2):
                        t = i * 2 + u
                        hold(pe, s_x, t + 1)
                        neighbours(pe, psA[u], SPv, t, D).then_inc(s_A, 1)
                    for u in range(2):
                        t = i * 2 + u
                        hold(pe, s_x, t + 3)
                        hold(pe, s_xT, t + 1)
                        for k in range(K):
                            m = pe.transpose(psT[u][:, k * P:(k + 1) * P], xs[:, u, k * P:(k + 1) * P], ident[:, :])
                        m.then_inc(s_T, 1)
                    for u in range(2):
                        t = i * 2 + u
                        hold(pe, s_xT, t + 3)
                        hold(pe, s_out, t * 2 + 2)
                        for k in range(K):
                            m = pe.matmul(psO[u][:, :], xT[:, u, k * P:(k + 1) * P], W2[:, k, :], start=k == 0, stop=k == K - 1)
                        m.then_inc(s_O, 1)

            @block.scalar
            def _(a):
                a.sem_inc(s_O, 2)
                with a.Fori(0, NT // 2) as i:
                    for u in range(2):
                        t = i * 2 + u
                        hold(a, s_x, t + 1)
                        hold(a, s_A, t + 1)
                        a.activation(tl[:, u, :], psA[u][:, D:2 * D], ACT.Copy, scale=1 / LO).then_inc(s_tl, 1)
                    for u in range(2):
                        t = i * 2 + u
                        hold(a, s_T, t + 1)
                        hold(a, s_O, t + 1)
                        a.activation(xT[:, u, :], psT[u][:, :], ACT.Copy).then_inc(s_xT, 1)

            @block.vector
            def _(v):
                v.sem_inc(s_x, 2)
                v.sem_inc(s_out, 4)
                v.wait_ge(s_w, 16 * 3)
                with v.Fori(0, NT // 2) as i:
                    for u in range(2):
                        t = i * 2 + u
                        hold(v, s_tl, t + 1)
                        hold(v, s_xT, t + 1)
                        v.tensor_tensor(xs[:, u, :], psA[u][:, 0:D], tl[:, u, :], ALU.add).then_inc(s_v, 1)
                        hold(v, s_v, t * 2 + 1)
                        v.scalar_tensor_tensor(xs[:, u, :], xs[:, u, :], rdk[:, ds(t, 1)], HB[:, ds(t * D, D)],
                                               ALU.mult, ALU.add).then_inc(s_v, 1)
                        hold(v, s_v, t * 2 + 2)
                        v.tensor_scalar(xs[:, u, :], xs[:, u, :], 0.0, None, ALU.max).then_inc(s_x, 1)
                    for u in range(2):
                        t = i * 2 + u
                        hold(v, s_O, t + 3)
                        v.tensor_copy(XB[:, ds(t * H2, H2)], psO[u][:, 0:H2]).then_inc(s_out, 1)
                        v.tensor_tensor(HB[:, ds(t * D, H2)], psO[u][:, H2:2 * H2], b2r[:, :], ALU.add).then_inc(s_out, 1)

        SPv = parts(H2, XB, True)
        G0, G1 = D, 2 * D
        with Phase() as ph:
            E0 = ph.sb("E0", [P, G0], f32)
            E1 = ph.sb("E1", [P, G0 // P, G1], f32)
            E2 = ph.sb("E2", [P, G1 // P, D], f32)
            c0, c1 = ph.sb("c0", [P, G0 // P], f32), ph.sb("c1", [P, G1 // P], f32)
            c2 = ph.sb("c2", [P, D], f32)
            tl = ph.sb("tl", [P, 2, H2], f32)
            xs = ph.sb("xs", [P, 2, H2], f32)
            xT = ph.sb("xT", [P, 2, H2], f32)
            h0 = ph.sb("h0", [P, 2, G0], f32)
            h1 = ph.sb("h1", [P, 2, G1], f32)
            y = ph.sb("y", [P, 2, D], f32)
            xr = ph.sb("xr", [P, 2, D], f32)
            psA = [ph.ps(f"psA{u}", [P, 2 * H2]) for u in range(2)]
            psT = ph.ps("psT", [P, H2])
            ps0 = ph.ps("ps0", [P, G0])
            ps1 = [ph.ps(f"ps1{u}", [P, G1]) for u in range(2)]
            psO = [ph.ps(f"psO{u}", [P, D]) for u in range(2)]
            s_w, s_A, s_tl, s_x, s_T, s_xT, s_0, s_h0, s_1, s_h1, s_O, s_out, s_v, s_y = (
                ph.sem(n) for n in ("w", "A", "tl", "x", "T", "xT", "0", "h0", "1", "h1", "O", "out", "v", "y"))
            s_xr = [ph.sem(f"xr{u}") for u in range(2)]
            block = ph.enter_context(nc.Block())

            @block.sync
            def _(sp):
                sp.dma_start(E0[:, :], dw0).then_inc(s_w, 16)
                for w, m in ((E1, dw1), (E2, dw2)):
                    sp.dma_start(w[:, :, :], m.rearrange("(k p) f -> p k f", p=P)).then_inc(s_w, 16)
                with nc.allow_non_contiguous_dma("biases of 768 elements, one to a partition"):
                    for w, m in ((c0, db0), (c1, db1)):
                        sp.dma_start(w[:, :], m.rearrange("(f p) -> p f", p=P)).then_inc(s_w, 16)
                sp.dma_start(c2[:, :], db2.rearrange("(a f) -> a f", a=1).to_broadcast([P, D])).then_inc(s_w, 16)
                with sp.Fori(0, NT // 2) as i:
                    for u in range(2):
                        t = i * 2 + u
                        sp.wait_ge(s_out, t + 1)
                        sp.dma_start(xr[:, u, :], xd[:, ds(t * D, D)]).then_inc(s_xr[u], 16)

            @block.tensor
            def _(pe):
                pe.sem_inc(s_xT, 1)
                pe.sem_inc(s_h0, 1)
                pe.sem_inc(s_h1, 2)
                pe.wait_ge(s_w, 16 * 6)
                with pe.Fori(0, NT // 2) as i:
                    for u in range(2):
                        t = i * 2 + u
                        hold(pe, s_x, t + 1)
                        neighbours(pe, psA[u], SPv, t, H2).then_inc(s_A, 1)
                    for u in range(2):
                        t = i * 2 + u
                        hold(pe, s_x, t + 3)
                        hold(pe, s_xT, t + 1)
                        pe.transpose(psT[:, :], xs[:, u, :], ident[:, :]).then_inc(s_T, 1)
                    for u in range(2):
                        t = i * 2 + u
                        hold(pe, s_xT, t + 2)
                        hold(pe, s_h0, t + 1)
                        for f in range(G0 // P):
                            m = pe.matmul(ps0[:, f * P:(f + 1) * P], E0[:, f * P:(f + 1) * P], xT[:, u, :], start=True, stop=True)
                        m.then_inc(s_0, 1)
                    for u in range(2):
                        t = i * 2 + u
                        hold(pe, s_h0, t + 2)
                        hold(pe, s_h1, t + 1)
                        for f in range(G1 // P):
                            for k in range(G0 // P):
                                m = pe.matmul(ps1[u][:, f * P:(f + 1) * P], E1[:, k, f * P:(f + 1) * P],
                                              h0[:, u, k * P:(k + 1) * P], start=k == 0, stop=k == G0 // P - 1)
                        m.then_inc(s_1, 1)
                    for u in range(2):
                        t = i * 2 + u
                        hold(pe, s_h1, t + 3)
                        hold(pe, s_out, t + 1)
                        for k in range(G1 // P):
                            m = pe.matmul(psO[u][:, :], h1[:, u, k * P:(k + 1) * P], E2[:, k, :], start=k == 0, stop=k == G1 // P - 1)
                        m.then_inc(s_O, 1)

            @block.scalar
            def _(a):
                a.sem_inc(s_O, 2)
                a.sem_inc(s_0, 2)
                a.sem_inc(s_1, 2)
                a.wait_ge(s_w, 16 * 6)
                with a.Fori(0, NT // 2) as i:
                    for u in range(2):
                        t = i * 2 + u
                        hold(a, s_x, t + 1)
                        hold(a, s_A, t + 1)
                        a.activation(tl[:, u, :], psA[u][:, H2:2 * H2], ACT.Copy, scale=1 / LO).then_inc(s_tl, 1)
                    for u in range(2):
                        t = i * 2 + u
                        hold(a, s_T, t + 1)
                        hold(a, s_0, t + 1)
                        a.activation(xT[:, u, :], psT[:, :], ACT.Copy).then_inc(s_xT, 1)
                    for u in range(2):
                        t = i * 2 + u
                        hold(a, s_0, t + 3)
                        hold(a, s_1, t + 1)
                        for f in range(G0 // P):
                            ins = a.activation(h0[:, u, f * P:(f + 1) * P], ps0[:, f * P:(f + 1) * P], ACT.Relu, bias=c0[:, f:f + 1])
                        ins.then_inc(s_h0, 1)
                    for u in range(2):
                        t = i * 2 + u
                        hold(a, s_1, t + 3)
                        hold(a, s_O, t + 1)
                        for f in range(G1 // P):
                            ins = a.activation(h1[:, u, f * P:(f + 1) * P], ps1[u][:, f * P:(f + 1) * P], ACT.Relu, bias=c1[:, f:f + 1])
                        ins.then_inc(s_h1, 1)

            @block.vector
            def _(v):
                v.sem_inc(s_x, 2)
                v.sem_inc(s_out, 2)
                v.wait_ge(s_w, 16 * 6)
                with v.Fori(0, NT // 2) as i:
                    for u in range(2):
                        t = i * 2 + u
                        hold(v, s_tl, t + 1)
                        hold(v, s_xT, t + 0 + 1)
                        v.tensor_tensor(xs[:, u, :], psA[u][:, 0:H2], tl[:, u, :], ALU.add).then_inc(s_v, 1)
                        hold(v, s_v, t * 2 + 1)
                        v.scalar_tensor_tensor(xs[:, u, :], xs[:, u, :], rdk[:, ds(t, 1)], HB[:, ds(t * D, H2)],
                                               ALU.mult, ALU.add).then_inc(s_v, 1)
                        hold(v, s_v, t * 2 + 2)
                        v.tensor_scalar(xs[:, u, :], xs[:, u, :], 0.0, None, ALU.max).then_inc(s_x, 1)
                    for u in range(2):
                        t = i * 2 + u
                        hold(v, s_O, t + 3)
                        hold(v, s_out, t + 1)
                        v.tensor_tensor(y[:, u, :], psO[u][:, :], c2[:, :], ALU.add).then_inc(s_y, 1)
                        hold(v, s_y, t + 1)
                        hold(v, s_xr[u], i * 16 + 16)
                        v.scalar_tensor_tensor(HB[:, ds(t * D, D)], y[:, u, :], 0.0, xr[:, u, :], ALU.max, ALU.add).then_inc(s_out, 1)
        sg.close()

        with Phase() as ph:
            G4 = 4
            psU = [ph.ps(f"psU{u}", [P, G4 * P], f16) for u in range(2)]
            psL = [ph.ps(f"psL{u}", [P, G4 * P], f16) for u in range(2)]
            s_t, s_u, s_l, s_m, s_st = (ph.sem(n) for n in ("t", "u", "l", "m", "st"))
            block = ph.enter_context(nc.Block())
            Cv = C[:, :].rearrange("p (s d) -> p s d", d=NP)
            groups = [(i, j, min(j + G4, NT)) for i in range(NT) for j in range(i, NT, G4)]

            @block.tensor
            def _(pe):
                for n, (i, j0, j1) in enumerate(groups):
                    if n >= 2:
                        pe.wait_ge(s_u, n - 1)
                        pe.wait_ge(s_l, n - 1)
                    for j in range(j0, j1):
                        q = (j - j0) * P
                        pe.transpose(psU[n % 2][:, q:q + P], Cv[:, i, j * P:(j + 1) * P], ident16[:, :])
                        m = pe.transpose(psL[n % 2][:, q:q + P], Cv[:, j, i * P:(i + 1) * P], ident16[:, :])
                    m.then_inc(s_t, 1)

            @block.vector
            def _(v):
                for n, (i, j0, j1) in enumerate(groups):
                    v.wait_ge(s_t, n + 1)
                    v.tensor_copy(Cv[:, i, j0 * P:j1 * P], psL[n % 2][:, 0:(j1 - j0) * P]).then_inc(s_l, 1)

            @block.scalar
            def _(a):
                for n, (i, j0, j1) in enumerate(groups):
                    a.wait_ge(s_t, n + 1)
                    k = 1 if j0 == i else 0
                    if j1 - j0 > k:
                        a.activation(Cv[:, j0 + k:j1, i * P:(i + 1) * P],
                                     psU[n % 2][:, k * P:(j1 - j0) * P].rearrange("p (s d) -> p s d", d=P),
                                     ACT.Copy).then_inc(s_u, 1)
                    else:
                        a.sem_inc(s_u, 1)

            @block.gpsimd
            def _(g):
                g.tensor_copy(XB, HB[:, 0:NT * D]).then_inc(s_m, 1)

            @block.sync
            def _(sp):
                sp.dma_start(xd[:, :], HB[:, 0:NT * D]).then_inc(s_st, 16)
                sp.wait_ge(s_st, 16)

        attention(gat3, 4, 64, True, True, -1, AB, False)
        elu_into_xb(None, 4, True)
        with Phase() as ph:
            s_x, s_y, s_out = ph.sem("x"), ph.sem("y"), ph.sem("out")
            block = ph.enter_context(nc.Block())

            @block.sync
            def _(sp):
                sp.dma_start(HB[:, 0:NT * D], xd[:, :]).then_inc(s_x, 16)
                sp.wait_ge(s_y, 1)
                sp.dma_start(out[0:(NT - 1) * P, :].rearrange("(t p) f -> p t f", p=P),
                             XB[:, 0:(NT - 1) * D].rearrange("p (t f) -> p t f", f=D)).then_inc(s_out, 16)
                sp.dma_start(out[(NT - 1) * P:N, :], XB[0:LAST, (NT - 1) * D:NT * D]).then_inc(s_out, 16)
                sp.wait_ge(s_out, 32)

            @block.vector
            def _(v):
                v.wait_ge(s_x, 16)
                v.tensor_tensor(XB, XB, HB[:, 0:NT * D], ALU.add).then_inc(s_y, 1)


_INS = ["x", "src", "dst", "edge_weight"] + [f"L0_gnn_{n}" for n in ("W0", "al0", "ar0", "b0", "W1", "al1", "ar1", "b1")] \
    + [f"L2_gnn_{n}" for n in ("wn0", "wr0", "b0", "wn1", "wr1", "b1", "wn2", "wr2", "b2",
                               "dw0", "db0", "dw1", "db1", "dw2", "db2")] + ["L3_gnn_W", "L3_gnn_a"]


def kernel(**inputs):
    import numpy as _np
    import concourse.bacc as _bacc
    from concourse import mybir as _mybir
    from concourse.bass_utils import run_bass_kernel_spmd as _run

    nc = _bacc.Bacc("TRN2", target_bir_lowering=False, num_devices=1)
    arrays, args = {}, []
    for name in _INS:
        a = _np.ascontiguousarray(inputs[name])
        arrays[f"in_{name}"] = a
        args.append(nc.dram_tensor(f"in_{name}", a.shape, _mybir.dt.from_np(a.dtype), kind="ExternalInput").ap())
    out = nc.dram_tensor("out_0", (N, D), _mybir.dt.float32, kind="ExternalOutput").ap()
    build(nc, args[0], args[1], args[2], args[3], args[4:8], args[8:12], args[12:21], args[21:27], args[27:29], out)
    r = _run(nc, [arrays], core_ids=[0])
    return r.results[0]["out_0"]
```

```python
import concourse.bass as bass
from concourse import mybir
from contextlib import ExitStack

P = 128
N = 2500
E = 40000
D = 256
NT = (N + P - 1) // P
NP = NT * P
LAST = N - (NT - 1) * P
NCH = (E + P - 1) // P
NG = (NCH + P - 1) // P
CENTRE = NP // 2
FAR = 1.0e6
BIG = float(2 ** 60)
LO = 2048.0
TOP = 32768.0
SLOPE = 0.2
EPS = 1e-5
OOB = 1 << 20


class Chain:

    def __init__(self, eng, sem):
        self.eng, self.sem, self.base, self.n = eng, sem, 0, 0

    def __call__(self, ins):
        ins.then_inc(self.sem, 1)
        self.n += 1
        return ins

    def wait(self):
        self.eng.wait_ge(self.sem, self.base + self.n)

    def begin(self, i, per):
        self.start, self.per = self.base + self.n, per
        self.base, self.n = self.start + i * per, 0

    def end(self, trips):
        assert self.n == self.per, (self.n, self.per)
        self.base, self.n = self.start + trips * self.per, 0


def build(nc, x, src, dst, ew, gat0, gat1, sage, dec, gat3, out):
    f32, f16, bf16, i32 = mybir.dt.float32, mybir.dt.float16, mybir.dt.bfloat16, mybir.dt.int32
    ALU, ACT, AX = mybir.AluOpType, mybir.ActivationFunctionType, mybir.AxisListType
    ds = bass.ds
    top = ExitStack()
    with top:
        def sb(name, shape, dt, ctx=top):
            return ctx.enter_context(nc.sbuf_tensor(name, shape, dt))

        names = [0]
        used = []

        class Phase(ExitStack):

            def sb(self, name, shape, dt):
                names[0] += 1
                return self.enter_context(nc.sbuf_tensor(f"{name}_{names[0]}", shape, dt))

            def ps(self, name, shape, dt=f32):
                names[0] += 1
                return self.enter_context(nc.psum_tensor(f"{name}_{names[0]}", shape, dt))

            def sem(self, name):
                names[0] += 1
                handle = nc.alloc_semaphore(f"{name}_{names[0]}")
                self.callback(lambda: used.append(handle))
                return handle

            def __exit__(self, *failure):
                done = super().__exit__(*failure)
                if used and failure[0] is None:
                    nc.clear_and_free_semaphores(list(used))
                    nc.all_engine_barrier()
                    used.clear()
                return done

        C = sb("C", [P, NT * NP], f16)
        HB = sb("HB", [P, NT * 264], f32)
        R = sb("R", [P, NT * 528], f32)
        Rh = R[:, :].bitcast(f16)
        ident = sb("ident", [P, P], f32)
        ident16 = sb("ident16", [P, P], f16)
        padneg = sb("padneg", [P, 1], f32)
        eps = sb("eps", [P, 1], f32)
        rdeg = sb("rdeg", [P, NT], f32)
        AB = sb("AB", [P, NT * 16], f32)
        table = sb("table", [1, 4 * NT], i32)
        wd = nc.dram_tensor("wd", [D * D, 1], f32, kind="Internal").ap()
        xd = nc.dram_tensor("xd", [P, NT * D], f32, kind="Internal").ap()
        rowd = nc.dram_tensor("rowd", [8, NP], f32, kind="Internal").ap()
        keyd = nc.dram_tensor("keyd", [NG * P, P], f32, kind="Internal").ap()
        late_ = ExitStack()
        edge = ExitStack()
        widx = sb("widx", [P, NG * P], i32, late_)
        ewT = sb("ewT", [P, NG * P], f32, late_)
        srcT = sb("srcT", [P, NG * P], f32, edge)
        dstT = sb("dstT", [P, NG * P], f32, edge)
        keyT = sb("keyT", [P, NG * P], f32, edge)
        wcell = sb("wcell", [P, NG * P], f32, edge)
        late = sb("late", [P, NG * P], f32, edge)

        dum = top.enter_context(nc.semaphore("dum"))

        def hold(eng, sem, value):
            eng.wait_ge(sem, value)
            eng.sem_inc(dum, 1)

        def chunk(value, most):
            return nc.s_assert_within(value, 0, most, skip_runtime_bounds_check_because=
                                      "a range of chunks starts below NCH and is at most NCH or four chunks long")

        def rows_in(eng, dest, dram, sem):
            eng.dma_start(dest[:, 0:(NT - 1) * D].rearrange("p (t f) -> p t f", f=D),
                          dram[0:(NT - 1) * P, :].rearrange("(t p) f -> p t f", p=P)).then_inc(sem, 16)
            eng.dma_start(dest[0:LAST, (NT - 1) * D:NT * D], dram[(NT - 1) * P:N, :]).then_inc(sem, 16)

        with Phase() as ph:
            raw = [ph.sb(f"raw{i}", [P, NG * P], dt) for i, dt in enumerate((i32, i32, f32))]
            rf = [ph.sb(f"rf{i}", [P, NG * P], f32) for i in range(2)]
            key = ph.sb("key", [P, NG * P], f32)
            tmp = ph.sb("tmp", [P, NG * P], f32)
            zero = ph.sb("zero", [P, 512], f32)
            cmin, cmax = ph.sb("cmin", [P, NG], f32), ph.sb("cmax", [P, NG], f32)
            tlo = ph.sb("tlo", [P, NT], f32)
            cidx = ph.sb("cidx", [P, NG], f32)
            away = ph.sb("away", [P, NG], f32)
            ov = ph.sb("ov", [P, NG * NT], f32)
            ov2 = ph.sb("ov2", [P, NG * NT], f32)
            lohi = ph.sb("lohi", [P, 2, NG, NT], f32)
            lohir = ph.sb("lohir", [P, 2, NG, NT], f32)
            lh = ph.sb("lh", [1, 2, NT], f32)
            row = ph.sb("row", [1, 8, NT], f32)
            pst = [ph.ps(f"pst{i}", [P, P]) for i in range(4)]
            s_set, s_in, s_rf, s_t, s_ev, s_lohi, s_all, s_iota, s_z, s_st, s_v = (
                ph.sem(n) for n in ("set", "in", "rf", "t", "ev", "lohi", "all", "iota", "z", "st", "v"))
            block = ph.enter_context(nc.Block())

            @block.gpsimd
            def _(g):
                for q in range(2):
                    g.memset(raw[q][:, :], -1).then_inc(s_set, 1)
                g.memset(raw[2][:, :], 0.0).then_inc(s_set, 1)
                g.memset(zero[:, :], 0.0).then_inc(s_set, 1)
                g.memset(ident[:, :], 0.0).then_inc(s_z, 1)
                g.memset(padneg[:, :], 0.0).then_inc(s_z, 1)
                g.memset(eps[:, :], EPS).then_inc(s_z, 1)
                g.iota(tlo[:, :], pattern=[[P, NT]], base=0, channel_multiplier=0,
                       allow_small_or_imprecise_dtypes=True).then_inc(s_iota, 1)
                g.iota(cidx[:, :], pattern=[[P, NG]], base=0, channel_multiplier=1,
                       allow_small_or_imprecise_dtypes=True).then_inc(s_iota, 1)
                g.wait_ge(s_z, 3)
                g.affine_select(out=ident[:, :], in_=ident[:, :], compare_op=ALU.not_equal, fill=1.0, base=0,
                                pattern=[[-1, P]], channel_multiplier=1).then_inc(s_z, 1)
                g.affine_select(out=padneg[:, :], in_=padneg[:, :], compare_op=ALU.is_gt, fill=-1e9, base=LAST,
                                pattern=[[0, 1]], channel_multiplier=-1).then_inc(s_z, 1)
                g.wait_ge(s_z, 5)
                g.tensor_copy(ident16[:, :], ident[:, :]).then_inc(s_z, 1)
                g.wait_ge(s_lohi, 1)
                g.partition_all_reduce(lohir[:, :, :, :].rearrange("p a g t -> p (a g t)"),
                                       lohi[:, :, :, :].rearrange("p a g t -> p (a g t)"), P,
                                       bass.bass_isa.ReduceOp.max).then_inc(s_all, 1)

            @block.sync
            def _(sp):
                sp.wait_ge(s_set, 4)
                full = NCH - 1 - (NG - 1) * P
                for q, a in enumerate((src, dst, ew)):
                    for g in range(NG - 1):
                        sp.dma_start(raw[q][:, g * P:(g + 1) * P],
                                     a[g * P * P:(g + 1) * P * P].rearrange("(c j) -> c j", j=P)).then_inc(s_in, 16)
                    sp.dma_start(raw[q][0:full, (NG - 1) * P:NG * P],
                                 a[(NG - 1) * P * P:(NCH - 1) * P].rearrange("(c j) -> c j", j=P)).then_inc(s_in, 16)
                    sp.dma_start(raw[q][full:full + 1, (NG - 1) * P:(NG - 1) * P + E - (NCH - 1) * P],
                                 a[(NCH - 1) * P:E].rearrange("(c j) -> c j", c=1)).then_inc(s_in, 16)
                sp.dma_start(wd.rearrange("(p c) a -> p (c a)", p=P), zero[:, :]).then_inc(s_st, 16)
                sp.wait_ge(s_rf, 1)
                for g in range(NG):
                    sp.dma_start(keyd[g * P:(g + 1) * P, :], key[:, g * P:(g + 1) * P]).then_inc(s_st, 16)
                sp.wait_ge(s_st, 16 * (NG + 1))

            @block.tensor
            def _(pe):
                pe.wait_ge(s_z, 6)
                pe.wait_ge(s_rf, 1)
                for n in range(4 * NG):
                    q, g = divmod(n, NG)
                    if n >= 4:
                        pe.wait_ge(s_ev, n - 3)
                    a = (rf[0], rf[1], raw[2], key)[q]
                    pe.transpose(pst[n % 4][:, :], a[:, g * P:(g + 1) * P], ident[:, :]).then_inc(s_t, 1)

            @block.vector
            def _(v):
                ch = Chain(v, s_v)
                v.wait_ge(s_in, 16 * 3 * (NG + 1))
                for q in range(2):
                    ch(v.tensor_copy(rf[q][:, :], raw[q][:, :]))
                ch.wait()
                v.scalar_tensor_tensor(key[:, :], rf[0][:, :], float(4096), rf[1][:, :], ALU.mult,
                                       ALU.add).then_inc(s_rf, 1)
                ch(v.tensor_scalar(tmp[:, :], rf[1][:, :], 0.0, FAR, ALU.is_lt, ALU.mult))
                ch(v.tensor_reduce(cmax[:, :], rf[1][:, :].rearrange("p (g j) -> p g j", j=P), AX.X, ALU.max))
                ch.wait()
                ch(v.tensor_tensor(tmp[:, :], tmp[:, :], rf[1][:, :], ALU.add))
                ch.wait()
                ch(v.tensor_reduce(cmin[:, :], tmp[:, :].rearrange("p (g j) -> p g j", j=P), AX.X, ALU.min))
                v.wait_ge(s_iota, 2)
                ch(v.tensor_scalar(away[:, :], cidx[:, :], -1.0, FAR, ALU.mult, ALU.add))
                ch(v.tensor_scalar(cidx[:, :], cidx[:, :], 1.0, None, ALU.add))
                ch.wait()
                for g in range(NG):
                    o = ov[:, g * NT:(g + 1) * NT]
                    o2 = ov2[:, g * NT:(g + 1) * NT]
                    ch(v.tensor_scalar(o, tlo[:, :], float(P), cmin[:, g:g + 1], ALU.add, ALU.is_gt))
                    ch(v.tensor_scalar(o2, tlo[:, :], cmax[:, g:g + 1], None, ALU.is_le))
                ch.wait()
                ch(v.tensor_tensor(ov[:, :], ov[:, :], ov2[:, :], ALU.mult))
                ch.wait()
                for g in range(NG):
                    o = ov[:, g * NT:(g + 1) * NT]
                    ch(v.tensor_scalar(lohi[:, 0, g, :], o, away[:, g:g + 1], None, ALU.mult))
                    ch(v.tensor_scalar(lohi[:, 1, g, :], o, cidx[:, g:g + 1], None, ALU.mult))
                ch.wait()
                v.sem_inc(s_lohi, 1)
                for n in range(4 * NG):
                    q, g = divmod(n, NG)
                    v.wait_ge(s_t, n + 1)
                    if q < 2:
                        v.tensor_scalar((srcT, dstT)[q][:, g * P:(g + 1) * P], pst[n % 4][:, :], -float(CENTRE),
                                        None, ALU.add).then_inc(s_ev, 1)
                    else:
                        v.tensor_copy((ewT, keyT)[q - 2][:, g * P:(g + 1) * P], pst[n % 4][:, :]).then_inc(s_ev, 1)
                v.wait_ge(s_ev, 4 * NG)
                ch(v.tensor_scalar(wcell[:, :], srcT[:, :], float(D - CENTRE), None, ALU.is_lt))
                ch(v.tensor_scalar(late[:, :], dstT[:, :], float(D - CENTRE), None, ALU.is_lt))
                ch.wait()
                ch(v.tensor_tensor(wcell[:, :], wcell[:, :], late[:, :], ALU.mult))
                ch(v.tensor_scalar(tmp[:, :], srcT[:, :], float(-CENTRE), None, ALU.is_ge))
                ch.wait()
                ch(v.tensor_tensor(wcell[:, :], wcell[:, :], tmp[:, :], ALU.mult))
                ch.wait()
                ch(v.tensor_scalar(tmp[:, :], srcT[:, :], float(D), float(CENTRE * D + CENTRE - OOB), ALU.mult, ALU.add))
                ch.wait()
                ch(v.tensor_tensor(tmp[:, :], tmp[:, :], dstT[:, :], ALU.add))
                ch.wait()
                ch(v.tensor_tensor(tmp[:, :], tmp[:, :], wcell[:, :], ALU.mult))
                ch(v.memset(late[:, :], 0.0))
                ch.wait()
                ch(v.tensor_scalar(wcell[:, :], tmp[:, :], float(OOB), None, ALU.add))
                v.wait_ge(s_all, 1)
                ch(v.tensor_reduce(lh[:, :, :], lohir[0:1, :, :, :].rearrange("p a g t -> p a t g"), AX.X, ALU.max))
                ch.wait()
                first, fours, acc, acc2 = (row[:, i, :] for i in range(4))
                ch(v.tensor_scalar(first, lh[:, 0, :], -1.0, FAR, ALU.mult, ALU.add))
                ch.wait()
                ch(v.tensor_scalar(first, first, float(NCH - 1), None, ALU.min))
                ch.wait()
                ch(v.tensor_tensor(fours, lh[:, 1, :], first, ALU.subtract))
                ch.wait()
                ch(v.tensor_scalar(fours, fours, 0.25, 0.375, ALU.mult, ALU.add))
                ch.wait()
                ch(v.tensor_scalar(table[:, NT:2 * NT], fours, 2.0, None, ALU.max))
                ch.wait()
                ch(v.tensor_copy(acc, table[:, NT:2 * NT]))
                ch(v.tensor_copy(table[:, 0:NT], first))
                ch.wait()
                ch(v.tensor_copy(row[:, 4, :], acc))
                step = 1
                while step < NT:
                    ch.wait()
                    ch(v.tensor_tensor(acc2[:, step:NT], acc[:, step:NT], acc[:, 0:NT - step], ALU.add))
                    ch(v.tensor_copy(acc2[:, 0:step], acc[:, 0:step]))
                    acc, acc2 = acc2, acc
                    step *= 2
                ch.wait()
                ch(v.tensor_tensor(table[:, 2 * NT:3 * NT], acc, row[:, 4, :], ALU.subtract))
                wlo, whi = row[:, 5, 0:1], row[:, 5, 1:2]
                WT = D // P
                ch(v.tensor_reduce(wlo, first[:, 0:WT], AX.X, ALU.min))
                ch(v.tensor_reduce(whi, lh[:, 1, 0:WT], AX.X, ALU.max))
                ch.wait()
                ch(v.tensor_tensor(row[:, 5, 2:3], whi, wlo, ALU.subtract))
                ch.wait()
                ch(v.tensor_scalar(row[:, 5, 3:4], row[:, 5, 2:3], 0.25, 0.375, ALU.mult, ALU.add))
                ch.wait()
                ch(v.tensor_scalar(table[:, 3 * NT + 1:3 * NT + 2], row[:, 5, 3:4], 1.0, None, ALU.max))
                ch(v.tensor_copy(table[:, 3 * NT:3 * NT + 1], wlo))
                ch.wait()

        with Phase() as ph:
            node16 = ph.sb("node16", [P, NP], f16)
            ohs = ph.sb("ohs", [P, 4, NP], f16)
            ohd = ph.sb("ohd", [P, 4, P], f16)
            keyr = ph.sb("keyr", [P, 4, P], f32)
            same = ph.sb("same", [P, 4, P], f32)
            notlater = ph.sb("notlater", [P, P], f32)
            junk = ph.sb("junk", [P, 4, P], f32)
            acc = ph.ps("acc", [P, NT * P])
            s_c, s_oh, s_used, s_out, s_key, s_same, s_late, s_abs, s_kdone = (
                ph.sem(n) for n in ("c", "oh", "used", "out", "key", "same", "late", "abs", "kd"))
            block = ph.enter_context(nc.Block())
            PERBANK = 4
            NB = NT // PERBANK
            DR = (NCH + 4 * NT - 1) // (4 * NT)

            @block.gpsimd
            def _(g):
                g.iota(node16[:, :], pattern=[[1, NP]], base=-CENTRE, channel_multiplier=0,
                       allow_small_or_imprecise_dtypes=True).then_inc(s_c, 1)
                g.memset(notlater[:, :], 0.0).then_inc(s_c, 1)
                g.wait_ge(s_c, 2)
                g.affine_select(out=notlater[:, :], in_=notlater[:, :], compare_op=ALU.is_gt, fill=1e9, base=0,
                                pattern=[[1, P]], channel_multiplier=-1).then_inc(s_c, 1)
                g.wait_ge(s_c, 3)
                with g.Fori(0, NT * DR) as i:
                    hold(g, s_key, (i + 1) * 16)
                    hold(g, s_late, i * 4 + 4)
                    g.tensor_tensor(same[:, :, :], keyr[:, :, :],
                                    keyT[:, ds(i * 4, 4)].unsqueeze(2).to_broadcast([P, 4, P]),
                                    ALU.subtract).then_inc(s_same, 1)
                    hold(g, s_same, i * 2 + 1)
                    g.tensor_tensor(same[:, :, :], same[:, :, :],
                                    notlater[:, :].unsqueeze(1).to_broadcast([P, 4, P]), ALU.add).then_inc(s_same, 1)

            @block.sync
            def _(sp):
                with sp.Fori(0, NT * DR) as i:
                    sp.wait_ge(s_kdone, i + 1)
                    sp.dma_start(keyr[:, :, :], keyd[ds(i * 4, 4), :].unsqueeze(0).to_broadcast([P, 4, P])
                                 ).then_inc(s_key, 16)

            @block.scalar
            def _(a):
                a.sem_inc(s_late, 4)
                a.sem_inc(s_kdone, 1)
                with a.Fori(0, NT) as t:
                    fours = a.value_load(table[0:1, ds(t + NT, 1)], min_val=2, max_val=NCH)
                    before = a.value_load(table[0:1, ds(t + 2 * NT, 1)], min_val=0, max_val=NT * NCH)
                    for r in range(DR):
                        n = t * DR + r
                        hold(a, s_same, n * 2 + 2)
                        a.sem_inc(s_kdone, 1)
                        a.activation(junk[:, :, :], same[:, :, :], ACT.Square).then_inc(s_abs, 1)
                        hold(a, s_abs, n + 1)
                        for u in range(4):
                            a.activation(same[:, u, :], junk[:, u, :], ACT.Relu, bias=1.0, scale=-1.0,
                                         accum_out=late[:, ds(n * 4 + u, 1)]).then_inc(s_late, 1)
                    hold(a, s_used, (before + fours) * 4 + 4)
                    for b in range(NB):
                        dest = C[:, :].rearrange("p (s d) -> p s d", d=NP)[:, b * PERBANK:(b + 1) * PERBANK, ds(t * P, P)]
                        a.activation(dest, acc[:, b * PERBANK * P:(b + 1) * PERBANK * P].rearrange(
                            "p (s d) -> p s d", d=P), ACT.Copy).then_inc(s_out, 1)

            @block.vector
            def _(v):
                v.wait_ge(s_c, 1)
                with v.Fori(0, NT) as t:
                    first = v.value_load(table[0:1, ds(t, 1)], min_val=0, max_val=NCH - 1)
                    fours = v.value_load(table[0:1, ds(t + NT, 1)], min_val=2, max_val=NCH)
                    before = v.value_load(table[0:1, ds(t + 2 * NT, 1)], min_val=0, max_val=NT * NCH)
                    with v.Fori(0, fours) as i:
                        for u in range(4):
                            k = chunk(first + i * 4 + u, NG * P - 1)
                            v.wait_ge(s_used, (before + i) * 4 + u + 1)
                            v.tensor_scalar(ohs[:, u, :], node16[:, :], srcT[:, ds(k, 1)], None,
                                            ALU.is_equal).then_inc(s_oh, 1)
                            v.tensor_scalar(ohd[:, u, :], node16[:, ds(t * P, P)], dstT[:, ds(k, 1)], None,
                                            ALU.is_equal).then_inc(s_oh, 1)

            @block.tensor
            def _(pe):
                pe.sem_inc(s_used, 4)
                pe.sem_inc(s_out, NB)
                with pe.Fori(0, NT) as t:
                    fours = pe.value_load(table[0:1, ds(t + NT, 1)], min_val=2, max_val=NCH)
                    before = pe.value_load(table[0:1, ds(t + 2 * NT, 1)], min_val=0, max_val=NT * NCH)

                    def four(i, opening):
                        for u in range(4):
                            pe.wait_ge(s_oh, (before + i) * 8 + u * 2 + 2)
                            for s in range(NT):
                                first_ = opening and u == 0 and s % PERBANK == 0
                                if first_:
                                    pe.wait_ge(s_out, t * NB + s // PERBANK + 1)
                                m = pe.matmul(acc[:, s * P:(s + 1) * P], ohs[:, u, s * P:(s + 1) * P], ohd[:, u, :],
                                              start=first_, stop=True, skip_group_check=True)
                            m.then_inc(s_used, 1)

                    four(0, True)
                    with pe.Fori(1, fours) as i:
                        four(i, False)

        with Phase() as ph:
            s_w = ph.sem("w")
            block = ph.enter_context(nc.Block())

            @block.vector
            def _(v):
                v.scalar_tensor_tensor(widx[:, :], late[:, :], float(OOB), wcell[:, :], ALU.mult, ALU.add).then_inc(s_w, 1)
        edge.close()

        XB = R[:, 0:NT * D]
        X2 = R[:, NT * D:2 * NT * D]
        def skewed(eng, first, step, last):
            first(0, 0)
            with eng.Fori(0, NT // 2 - 1) as i:
                step(i * 2 + 1, i * 2, 1)
                step(i * 2 + 2, i * 2 + 1, 0)
            step(NT - 1, NT - 2, (NT - 1) % 2)
            last(NT - 1, (NT - 1) % 2)

        def bc(ap, shape):
            return ap.to_broadcast(shape)

        def norm_memory(ph):
            return {**{n: ph.sb(n, [P, w * NT], f32) for n, w in (("st", 6), ("mv", 2), ("sd", 1), ("nmr", 1))},
                    **{n: ph.sem(n) for n in ("s_add", "s_bn", "s_mv", "s_sd", "s_rs")}}

        def norm_vector(v, m, residual=None):
            with v.Fori(0, NT) as t:
                tile = XB[:, ds(t * D, D)]
                if residual is not None:
                    v.tensor_tensor(tile, tile, residual[:, ds(t * D, D)], ALU.add).then_inc(m["s_add"], 1)
                    v.wait_ge(m["s_add"], t + 1)
                v.bn_stats(m["st"][:, ds(t * 6, 6)], tile).then_inc(m["s_bn"], 1)
            v.wait_ge(m["s_bn"], NT)
            for t in range(NT):
                last = v.bn_aggr(m["mv"][:, 2 * t:2 * t + 2], m["st"][:, 6 * t:6 * t + 6])
            last.then_inc(m["s_mv"], 1)
            v.wait_ge(m["s_sd"], 1)
            v.reciprocal(m["sd"][:, :], m["sd"][:, :]).then_inc(m["s_rs"], 1)
            v.wait_ge(m["s_rs"], 1)
            mean = m["mv"][:, :].rearrange("p (t c) -> p t c", c=2)[:, :, 0]
            v.scalar_tensor_tensor(m["nmr"][:, :], mean, -1.0, m["sd"][:, :], ALU.mult, ALU.mult).then_inc(m["s_rs"], 1)

        def norm_scalar(a, m):
            a.wait_ge(m["s_mv"], 1)
            var = m["mv"][:, :].rearrange("p (t c) -> p t c", c=2)[:, :, 1]
            a.activation(m["sd"][:, :], var, ACT.Sqrt, bias=eps[:, 0:1]).then_inc(m["s_sd"], 1)
            a.wait_ge(m["s_rs"], 2)

        def attention(gat, nh, dh, split, norm, sgn, AB, scatter):
            K = D // P
            W2 = D + 2 * nh
            ABv = AB[:, 0:NT * 2 * nh].rearrange("p (t c) -> p t c", c=2 * nh)
            with Phase() as ph:
                Wx = ph.sb("Wx", [P, K, W2], f32)
                av = ph.sb("av", [P, 2, D], f32)
                prod = ph.sb("prod", [P, 2 * K, D], f32)
                xn = ph.sb("xn", [P, 2, D], f32)
                xT = ph.sb("xT", [P, 2, D], f32)
                rT = ph.sb("rT", [nh, NP], f32)
                m_ = norm_memory(ph) if norm else None
                psT = [ph.ps(f"psT{u}", [P, D]) for u in range(2)]
                psH = [ph.ps(f"psH{u}", [P, W2]) for u in range(2)]
                psR = [ph.ps(f"psR{u}", [nh, P]) for u in range(2)]
                s_w, s_wx, s_xn, s_T, s_xT, s_M, s_out, s_v, s_rd = (
                    ph.sem(n) for n in ("w", "wx", "xn", "T", "xT", "M", "out", "v", "rd"))
                block = ph.enter_context(nc.Block())
                @block.sync
                def _(sp):
                    if split:
                        for h in range(nh):
                            sp.dma_start(Wx[:, :, h * dh:(h + 1) * dh],
                                         gat[0][h].rearrange("(k p) f -> p k f", p=P)).then_inc(s_w, 16)
                            for j in range(2):
                                sp.dma_start(av[:, 1 - j, h * dh:(h + 1) * dh],
                                             gat[1][h, :, j * dh:(j + 1) * dh].to_broadcast([P, dh])).then_inc(s_w, 16)
                    else:
                        sp.dma_start(Wx[:, :, 0:D], gat[0].rearrange("(k p) f -> p k f", p=P)).then_inc(s_w, 16)
                        for j in range(2):
                            sp.dma_start(av[:, j, :], gat[1 + j].rearrange("(a h) d -> a (h d)", a=1)
                                         .to_broadcast([P, D])).then_inc(s_w, 16)
                    sp.wait_ge(s_out, 3 * NT + 6)
                    sp.dma_start(rowd[0:nh, :], rT[:, :]).then_inc(s_rd, 16)
                    sp.wait_ge(s_rd, 16)

                @block.vector
                def _(v):
                    ch = Chain(v, s_v)
                    v.wait_ge(s_w, 16 * (3 * nh if split else 3))
                    for k in range(K):
                        for j in range(2):
                            ch(v.tensor_tensor(prod[:, 2 * k + j, :], Wx[:, k, 0:D], av[:, j, :], ALU.mult))
                    ch.wait()
                    for k in range(K):
                        for j in range(2):
                            last = v.tensor_reduce(Wx[:, k, D + j * nh:D + (j + 1) * nh],
                                                   prod[:, 2 * k + j, :].rearrange("p (h d) -> p h d", d=dh), AX.X,
                                                   ALU.add)
                    last.then_inc(s_wx, 1)
                    if norm:
                        norm_vector(v, m_)
                    v.sem_inc(s_out, 6)
                    v.sem_inc(s_xT, 2)

                    def turned(t, u):
                        hold(v, s_T, t + 3)
                        hold(v, s_M, t + 1)
                        v.tensor_copy(xT[:, u, :], psT[u][:, :]).then_inc(s_xT, 1)

                    def result(t, u):
                        hold(v, s_M, t + 3)
                        v.tensor_copy(AB[:, ds(t * 2 * nh, 2 * nh)], psH[u][:, D:W2]).then_inc(s_out, 1)
                        v.tensor_copy(HB[:, ds(t * D, D)], psH[u][:, 0:D]).then_inc(s_out, 1)
                        v.tensor_scalar(rT[:, ds(t * P, P)], psR[u][:, :], BIG, None, ALU.mult).then_inc(s_out, 1)

                    def step(t, before, u):
                        turned(t, u)
                        result(before, 1 - u)
                    skewed(v, turned, step, result)

                @block.scalar
                def _(a):
                    if norm:
                        norm_scalar(a, m_)
                    with a.Fori(0, NT // 2) as i:
                        for u in range(2):
                            t = i * 2 + u
                            hold(a, s_T, t + 1)
                            if norm:
                                a.activation(xn[:, u, :], XB[:, ds(t * D, D)], ACT.Relu, bias=m_["nmr"][:, ds(t, 1)],
                                             scale=m_["sd"][:, ds(t, 1)]).then_inc(s_xn, 1)
                            else:
                                a.activation(xn[:, u, :], HB[:, ds(t * D, D)], ACT.Copy).then_inc(s_xn, 1)

                @block.tensor
                def _(pe):
                    pe.sem_inc(s_T, 2)
                    pe.sem_inc(s_M, 2)
                    pe.wait_ge(s_wx, 1)

                    def turn(t, u):
                        hold(pe, s_xn, t + 1)
                        hold(pe, s_xT, t + 1)
                        for k in range(K):
                            m = pe.transpose(psT[u][:, k * P:(k + 1) * P], xn[:, u, k * P:(k + 1) * P], ident[:, :])
                        m.then_inc(s_T, 1)

                    def product(t, u):
                        hold(pe, s_xT, t + 3)
                        hold(pe, s_out, t * 3 + 3)
                        for k in range(K):
                            pe.matmul(psH[u][:, :], xT[:, u, k * P:(k + 1) * P], Wx[:, k, :], start=k == 0, stop=k == K - 1)
                        for k in range(K):
                            m = pe.matmul(psR[u][:, :], Wx[:, k, D + nh:W2], xT[:, u, k * P:(k + 1) * P],
                                          start=k == 0, stop=k == K - 1)
                        m.then_inc(s_M, 1)

                    def step(t, before, u):
                        turn(t, u)
                        product(before, 1 - u)
                    skewed(pe, turn, step, product)

            cw = dh + 1
            S2 = nh * 2 * cw
            UV = Rh[:, 0:NT * 2 * S2].rearrange("p (t l c) -> p t l c", l=2, c=S2)
            VP = HB[:, :].bitcast(f16)[:, 0:NT * S2].rearrange("p (t l c) -> p t l c", l=2, c=S2 // 2)
            TH = NT * nh
            heads = Phase()
            with heads as hp:
                cB = hp.sb("cB", [P, TH], f32)
                F1, F2 = hp.sb("F1", [P, TH], f32), hp.sb("F2", [P, TH], f32)
                with Phase() as ph:
                    U, V = ph.sb("U", [P, TH], f32), ph.sb("V", [P, TH], f32)
                    XC, tt = ph.sb("XC", [P, TH], f32), ph.sb("tt", [P, TH], f32)
                    tt2 = ph.sb("tt2", [P, TH], f32)
                    top1, most = ph.sb("top1", [P, nh + 1], f32), ph.sb("most", [P, nh + 1], f32)
                    kap = ph.sb("kap", [P, 1], f32)
                    F = ph.sb("F", [P, 2, S2], f32)
                    L = ph.sb("L", [P, 2, S2], f32)
                    s_v, s_top, s_all, s_e, s_ex, s_fac, s_F, s_FV, s_hi, s_lo = (
                        ph.sem(n) for n in ("v", "top", "all", "e", "ex", "fac", "F", "FV", "hi", "lo"))
                    block = ph.enter_context(nc.Block())
                    th = lambda q: q[:, :].rearrange("p (t h) -> p t h", h=nh)
                    cv, rv = ABv[:, :, 0:nh], ABv[:, :, nh:2 * nh]

                    def side(eng, t, u, w, q, s_done):
                        Fv = F[:, u, :].rearrange("p (h w c) -> p h w c", w=2, c=cw)
                        Ht = HB[:, ds(t * D, D)].rearrange("p (h d) -> p h d", d=dh)
                        qt = q[:, ds(t * nh, nh)].unsqueeze(2)
                        hold(eng, s_hi, t * 2 + 2)
                        eng.tensor_tensor(Fv[:, :, w, 0:dh], Ht, qt.to_broadcast([P, nh, dh]), ALU.mult).then_inc(s_done, 1)
                        eng.tensor_copy(Fv[:, :, w, dh:cw], qt).then_inc(s_done, 1)

                    @block.gpsimd
                    def _(g):
                        g.wait_ge(s_top, 1)
                        g.partition_all_reduce(most[:, :], top1[:, :], P, bass.bass_isa.ReduceOp.max).then_inc(s_all, 1)
                        g.wait_ge(s_fac, 1)
                        with g.Fori(0, NT // 2) as i:
                            for u in range(2):
                                side(g, i * 2 + u, u, 1, V, s_FV)

                    @block.vector
                    def _(v):
                        ch = Chain(v, s_v)
                        ch(v.tensor_scalar(th(XC), cv, float(sgn), None, ALU.mult))
                        ch(v.tensor_scalar(th(cB), cv, BIG, None, ALU.mult))
                        ch(v.tensor_reduce(top1[:, nh:nh + 1], HB[:, 0:NT * D], AX.X, ALU.max, apply_absolute_value=True))
                        ch.wait()
                        ch(v.tensor_scalar(XC[:, TH - nh:TH], XC[:, TH - nh:TH], padneg[:, 0:1], None, ALU.add))
                        ch.wait()
                        ch(v.tensor_reduce(top1[:, 0:nh], XC[:, :].rearrange("p (t h) -> p h t", h=nh), AX.X, ALU.max))
                        ch.wait()
                        v.sem_inc(s_top, 1)
                        v.wait_ge(s_all, 1)
                        A = most[:, 0:nh].unsqueeze(1).to_broadcast([P, NT, nh])
                        ch(v.tensor_tensor(th(XC), th(XC), A, ALU.subtract))
                        ch(v.tensor_tensor(th(tt), rv, A, ALU.add if sgn > 0 else ALU.subtract))
                        ch(v.tensor_scalar(kap[:, :], most[:, nh:nh + 1], 1.0, None, ALU.max))
                        ch.wait()
                        if sgn > 0:
                            ch(v.tensor_scalar(tt2[:, :], tt[:, :], -(1 - SLOPE), 0.0, ALU.mult, ALU.min))
                            ch.wait()
                            ch(v.tensor_scalar(tt[:, :], tt[:, :], 1 - SLOPE, 0.0, ALU.mult, ALU.min))
                        else:
                            ch(v.tensor_scalar(tt2[:, :], tt[:, :], 1 - SLOPE, 0.0, ALU.mult, ALU.max))
                            ch.wait()
                            ch(v.tensor_scalar(tt[:, :], tt[:, :], -(1 - SLOPE), 0.0, ALU.mult, ALU.max))
                            ch.wait()
                            ch(v.tensor_scalar(tt2[:, :], tt2[:, :], 80.0, None, ALU.min))
                            ch(v.tensor_scalar(tt[:, :], tt[:, :], 80.0, None, ALU.min))
                        ch(v.reciprocal(kap[:, :], kap[:, :]))
                        ch.wait()
                        v.tensor_scalar(kap[:, :], kap[:, :], TOP, None, ALU.mult).then_inc(s_e, 1)
                        v.wait_ge(s_ex, 4)
                        ch(v.tensor_scalar(U[:, :], U[:, :], kap[:, 0:1], None, ALU.mult))
                        ch(v.tensor_scalar(V[:, :], V[:, :], kap[:, 0:1], 1.0 if split else -1.0, ALU.mult, ALU.mult))
                        ch.wait()
                        v.sem_inc(s_lo, 2)
                        v.sem_inc(s_fac, 1)

                        def low(t, u):
                            hold(v, s_hi, t * 2 + 6)
                            v.scalar_tensor_tensor(UV[:, ds(t, 1), 1, :], UV[:, ds(t, 1), 0, :], -LO,
                                                   L[:, u, :].unsqueeze(1), ALU.mult, ALU.add).then_inc(s_lo, 1)

                        def step(t, before, u):
                            side(v, t, u, 0, U, s_F)
                            low(before, 1 - u)
                        skewed(v, lambda t, u: side(v, t, u, 0, U, s_F), step, low)

                    @block.scalar
                    def _(a):
                        a.sem_inc(s_hi, 4)
                        a.wait_ge(s_e, 1)
                        a.activation(U[:, :], XC[:, :], ACT.Exp).then_inc(s_ex, 1)
                        a.activation(V[:, :], XC[:, :], ACT.Exp, scale=SLOPE).then_inc(s_ex, 1)
                        a.activation(F1[:, :], tt[:, :], ACT.Exp).then_inc(s_ex, 1)
                        a.activation(F2[:, :], tt2[:, :], ACT.Exp).then_inc(s_ex, 1)
                        with a.Fori(0, NT // 2) as i:
                            for u in range(2):
                                t = i * 2 + u
                                hold(a, s_F, t * 2 + 2)
                                hold(a, s_FV, t * 2 + 2)
                                hold(a, s_lo, t + 1)
                                a.activation(UV[:, ds(t, 1), 0, :], F[:, u, :].unsqueeze(1), ACT.Copy).then_inc(s_hi, 1)
                                a.activation(L[:, u, :], F[:, u, :], ACT.Copy, scale=LO).then_inc(s_hi, 1)

                if not split:
                    with Phase() as ph:
                        s_n = ph.sem("n")
                        block = ph.enter_context(nc.Block())
                        turned = UV.rearrange("p t l (h w c) -> p t l h w c", w=2, c=cw)
                        plain = VP.rearrange("p t l (h c) -> p t l h c", c=cw)

                        @block.scalar
                        def _(a):
                            for t in range(NT // 2, NT):
                                for l in range(2):
                                    a.activation(plain[:, t, l], turned[:, t, l, :, 1], ACT.Copy, scale=-1.0).then_inc(s_n, 1)

                        @block.vector
                        def _(v):
                            for t in range(0, NT // 2):
                                for l in range(2):
                                    v.tensor_scalar(plain[:, t, l], turned[:, t, l, :, 1], -1.0, None, ALU.mult).then_inc(s_n, 1)

                PARTS = 4 if split else 2
                TP = NT // PARTS
                W = TP * P
                RG = 10
                NB = (RG + 2) // 3
                SG = 4
                SA = SG if split else SG - 1
                KR = NT // SG
                assert RG == TP * (2 if split else 1)
                with Phase() as ph:
                    rows = ph.sb("rows", [P, 2, W], f32)
                    Rm = ph.sb("Rm", [P, SG, W], bf16)
                    M = ph.sb("M", [P, SG, W], f16)
                    Mn = ph.sb("Mn", [P, SG, W], f16) if split else None
                    tl = ph.sb("tl", [P, RG, cw if split else 2 * cw], f32)
                    stash = None if split else ph.sb("stash", [P, TP, dh], f32)
                    q1 = ph.sb("q1", [P, TP, cw], f32)
                    rec = ph.sb("rec", [P, TP], f32)
                    if scatter:
                        wi, wv = ph.sb("wi", [P, 1], i32), ph.sb("wv", [P, 1], f32)
                    XW = cw if split else 2 * cw
                    ps = [[ph.ps(f"ps{b}{j}", [P, 3 * 2 * XW]) for j in range(NB)] for b in range(2)]
                    s_row = [ph.sem(f"row{b}") for b in range(2)]
                    s_R, s_M, s_cut, s_D, s_P, s_E, s_tl, s_v, s_wc, s_wd = (
                        ph.sem(n) for n in ("R", "M", "cut", "D", "P", "E", "tl", "v", "wc", "wd"))
                    block = ph.enter_context(nc.Block())

                    def region(b, r, l0=0, l1=2):
                        return ps[b][r // 3][:, (r % 3) * 2 * XW + l0 * XW:(r % 3) * 2 * XW + l1 * XW]

                    def banks(b, l):
                        for j in range(NB):
                            n = min(3, RG - 3 * j)
                            yield 3 * j, n, ps[b][j][:, 0:n * 2 * XW].rearrange("p (r l c) -> p r l c", l=2, c=XW)[:, :, l, :]

                    @block.sync
                    def _(sp):
                        with sp.Fori(0, nh) as h:
                            for p in range(PARTS):
                                sp.wait_ge(s_M, (h * PARTS + p) * NT + NT)
                                sp.dma_start(rows[:, p % 2, :], rowd[ds(h, 1), p * W:(p + 1) * W].to_broadcast([P, W])
                                             ).then_inc(s_row[p % 2], 16)

                    def landed(eng, h, p):
                        hold(eng, s_row[p % 2], (h * (PARTS // 2) + p // 2 + 1) * 16)

                    def parts_in_order(eng, steps, evacuate):
                        def body(h, opening):
                            for p in range(PARTS):
                                landed(eng, h, p)
                                steps(h, p, 0, SG)
                                if p:
                                    evacuate(h, p - 1)
                                elif not opening:
                                    evacuate(h - 1, PARTS - 1)
                                steps(h, p, SG, NT)

                        body(0, True)
                        return body

                    @block.scalar
                    def _(a):
                        def steps(h, p, s0, s1):
                            for s in range(s0, s1):
                                if s % SG < SA:
                                    g = (h * PARTS + p) * NT + s
                                    hold(a, s_M, g + 1 + 2 * NT - SG)
                                    a.activation(Rm[:, s % SG, :], rows[:, p % 2, :], ACT.Relu,
                                                 bias=cB[:, ds(h + s * nh, 1)]).then_inc(s_R, 1)

                        def evacuate(h, p):
                            q = h * PARTS + p
                            hold(a, s_P, (q + 1) * NT + SG)
                            hold(a, s_E, q + 2)
                            for r, n, part in banks(p % 2, 1):
                                ins = a.activation(tl[:, r:r + n, :], part, ACT.Copy, scale=1 / LO)
                            ins.then_inc(s_tl, 1)

                        body = parts_in_order(a, steps, evacuate)
                        with a.Fori(1, nh) as h:
                            body(h, False)
                        evacuate(nh - 1, PARTS - 1)

                    @block.vector
                    def _(v):
                        v.sem_inc(s_M, 2 * NT)
                        v.sem_inc(s_E, 2)
                        ch = Chain(v, s_v)

                        def steps(h, p, s0, s1):
                            for s in range(s0, s1):
                                part, (k, u) = h * PARTS + p, divmod(s, SG)
                                g = part * NT + s
                                if u < SA:
                                    v.wait_ge(s_R, part * KR * SA + k * SA + u + 1)
                                else:
                                    v.wait_ge(s_M, g + 1 + 2 * NT - SG)
                                    v.tensor_scalar(Rm[:, u, :], rows[:, p % 2, :], cB[:, ds(h + s * nh, 1)], 0.0,
                                                    ALU.add, ALU.max).then_inc(s_D, 1)
                                    v.wait_ge(s_D, part * KR * (SG - SA) + k * (SG - SA) + u - SA + 1)
                                v.wait_ge(s_P, g + 1)
                                Cs = C[:, s * NP + p * W:s * NP + (p + 1) * W]
                                v.tensor_tensor(M[:, u, :], Rm[:, u, :], Cs, ALU.min).then_inc(s_cut if split else s_M, 1)
                                if split:
                                    v.wait_ge(s_cut, g + 1)
                                    v.tensor_tensor(Mn[:, u, :], Cs, M[:, u, :], ALU.subtract).then_inc(s_M, 1)

                        def evacuate(h, p):
                            q = h * PARTS + p
                            hold(v, s_tl, q + 1)
                            for r, n, part in banks(p % 2, 0):
                                ch(v.tensor_tensor(tl[:, r:r + n, :], part, tl[:, r:r + n, :], ALU.add))
                            ch.wait()
                            one = lambda Fq: Fq[:, :].rearrange("p (t h) -> p t h", h=nh)[
                                :, p * TP:(p + 1) * TP, ds(h, 1)].to_broadcast([P, TP, cw])
                            xu, xv = (tl[:, 0:TP, :], tl[:, TP:2 * TP, :]) if split else (tl[:, :, 0:cw], tl[:, :, cw:2 * cw])
                            ch(v.tensor_tensor(xv, xv, one(F2), ALU.mult))
                            ch(v.tensor_tensor(q1[:, :, :], xu, one(F1), ALU.mult))
                            ch.wait()
                            ch(v.tensor_tensor(q1[:, :, :], q1[:, :, :], xv, ALU.add))
                            ch.wait()
                            v.sem_inc(s_E, 1)
                            ch(v.tensor_scalar(rec[:, :], q1[:, :, dh], 1e-30, None, ALU.max))
                            ch.wait()
                            ch(v.reciprocal(rec[:, :], rec[:, :]))
                            ch.wait()
                            room = HB[:, 0:NT * nh * cw] if split else R[:, :]
                            room = room.rearrange("p (t c) -> p t c", t=NT)
                            o = stash[:, :, :] if not split and p == 0 else room[:, p * TP:(p + 1) * TP, ds(h * cw, dh)]
                            ch(v.tensor_tensor(o, q1[:, :, 0:dh], rec[:, :].unsqueeze(2).to_broadcast([P, TP, dh]),
                                               ALU.mult))
                            if not split and p == 1:
                                ch(v.tensor_copy(room[:, 0:TP, ds(h * cw, dh)], stash[:, :, :]))

                        body = parts_in_order(v, steps, evacuate)
                        with v.Fori(1, nh) as h:
                            ch.begin(h - 1, PARTS * (NB + 6) + (0 if split else 1))
                            body(h, False)
                            ch.end(nh - 1)
                        evacuate(nh - 1, PARTS - 1)

                    @block.tensor
                    def _(pe):
                        pe.sem_inc(s_P, SG)

                        with pe.Fori(0, nh) as h:
                            for p in range(PARTS):
                                q = h * PARTS + p
                                hold(pe, s_E, q + 1)
                                for s in range(NT):
                                    pe.wait_ge(s_M, q * NT + s + 1 + 2 * NT)
                                    for r in range(RG):
                                        first = s == 0 and r % 3 == 0
                                        side = r // TP if split else 0
                                        lhsT = (M, Mn)[side][:, s % SG, (r % TP) * P:(r % TP + 1) * P]
                                        rhs = UV[:, s, :, ds(h * (2 * cw) + side * cw, XW)]
                                        m = pe.matmul(region(p % 2, r), lhsT, rhs, start=first, stop=True,
                                                      skip_group_check=True)
                                        if not split:
                                            both = region(p % 2, r).rearrange("p (l c) -> p l c", l=2)
                                            m = pe.matmul(both[:, :, cw:2 * cw], C[:, s * NP + p * W + r * P:][:, 0:P],
                                                          VP[:, s, :, ds(h * cw, cw)], start=False, stop=True,
                                                          skip_group_check=True)
                                    m.then_inc(s_P, 1)

                    if scatter:
                        @block.gpsimd
                        def _(g):
                            lo = g.value_load(table[0:1, 3 * NT:3 * NT + 1], min_val=0, max_val=NCH - 1)
                            n = g.value_load(table[0:1, 3 * NT + 1:3 * NT + 2], min_val=1, max_val=(NCH + 3) // 4)

                            def write(i, c, opening):
                                if not opening:
                                    hold(g, s_wd, i * 16)
                                g.tensor_copy(wi[:, :], widx[:, ds(c, 1)]).then_inc(s_wc, 1)
                                g.tensor_copy(wv[:, :], ewT[:, ds(c, 1)]).then_inc(s_wc, 1)
                                hold(g, s_wc, i * 2 + 2)
                                g.indirect_dma_start(out=wd[:, :], out_offset=bass.IndirectOffsetOnAxis(ap=wi[:, :], axis=0),
                                                     in_=wv[:, :], in_offset=None, bounds_check=D * D - 1,
                                                     oob_is_err=False).then_inc(s_wd, 16)

                            write(0, lo, True)
                            with g.Fori(1, n * 4) as i:
                                write(i, chunk(lo + i, NG * P - 1), False)
                            hold(g, s_wd, n * 64)

        def elu(source, dest, bias_dram, nh, twice):
            cw = D // nh + 1
            TB = 4
            BW = TB * D
            with Phase() as ph:
                bias = ph.sb("bias", [P, D], f32)
                e = ph.sb("e", [P, BW], f32)
                s_b, s_v, s_y, s_e, s_ee, s_o = (ph.sem(n) for n in ("b", "v", "y", "e", "ee", "o"))
                block = ph.enter_context(nc.Block())
                rounds = 2 if twice else 1

                if bias_dram is not None:
                    @block.sync
                    def _(sp):
                        sp.dma_start(bias[:, :], bias_dram.rearrange("(a f) -> a f", a=1).to_broadcast([P, D])).then_inc(s_b, 16)

                @block.vector
                def _(v):
                    v.sem_inc(s_o, 1)
                    if bias_dram is not None:
                        v.wait_ge(s_b, 16)
                    with v.Fori(0, NT // TB) as i:
                        y = dest[:, ds(i * BW, BW)]
                        yh = y.rearrange("p (t h c) -> p t h c", c=cw - 1, h=nh)
                        room = source.rearrange("p (t c) -> p t c", t=NT)[:, ds(i * TB, TB), 0:nh * cw]
                        src_ = room.rearrange("p t (h c) -> p t h c", c=cw)[:, :, :, 0:cw - 1]
                        for j in range(TB):
                            if bias_dram is not None:
                                v.tensor_tensor(yh[:, j], src_[:, j], bias[:, :].rearrange("p (h c) -> p h c", c=cw - 1),
                                                ALU.add).then_inc(s_b, 1)
                            else:
                                v.tensor_copy(yh[:, j], src_[:, j]).then_inc(s_b, 1)
                        hold(v, s_b, i * TB + TB + (16 if bias_dram is not None else 0))
                        hold(v, s_o, i + 1)
                        for w in range(rounds):
                            n = i * rounds + w
                            if w:
                                hold(v, s_y, i + 1)
                            v.tensor_scalar(e[:, :], y, 0.0, None, ALU.min).then_inc(s_e, 1)
                            hold(v, s_ee, n + 1)
                            v.tensor_scalar(y, y, 0.0, -1.0, ALU.max, ALU.add).then_inc(s_v, 1)
                            hold(v, s_v, n + 1)
                            v.tensor_tensor(y, y, e[:, :], ALU.add).then_inc(s_y if w + 1 < rounds else s_o, 1)

                @block.scalar
                def _(a):
                    with a.Fori(0, NT // TB * rounds) as n:
                        hold(a, s_e, n + 1)
                        a.activation(e[:, :], e[:, :], ACT.Exp).then_inc(s_ee, 1)

        def load_rows(dest):
            with Phase() as ph:
                s_z, s_in = ph.sem("z"), ph.sem("in")
                block = ph.enter_context(nc.Block())

                @block.gpsimd
                def _(g):
                    g.memset(dest[:, (NT - 1) * D:NT * D], 0.0).then_inc(s_z, 1)

                @block.sync
                def _(sp):
                    sp.wait_ge(s_z, 1)
                    rows_in(sp, dest, x, s_in)
                    sp.wait_ge(s_in, 32)

        load_rows(XB)
        attention(gat0[0:3], 8, 32, False, True, 1, AB, True)
        elu(R[:, :], HB, gat0[3], 8, False)
        attention(gat1[0:3], 8, 32, False, False, 1, AB, False)
        elu(R[:, :], HB, gat1[3], 8, False)
        late_.close()
        K = D // P
        load_rows(XB)

        with Phase() as ph:
            Wl = ph.sb("Wl", [P, K, D], f32)
            xn, xT = ph.sb("xn", [P, 2, D], f32), ph.sb("xT", [P, 2, D], f32)
            m_ = norm_memory(ph)
            psT = [ph.ps(f"psT{u}", [P, D]) for u in range(2)]
            psH = [ph.ps(f"psH{u}", [P, D]) for u in range(2)]
            s_w, s_xn, s_T, s_xT, s_M, s_out = (ph.sem(n) for n in ("w", "xn", "T", "xT", "M", "out"))
            block = ph.enter_context(nc.Block())

            @block.sync
            def _(sp):
                sp.dma_start(Wl[:, :, :], wd.rearrange("(k p c) a -> p k (c a)", p=P, c=D)).then_inc(s_w, 16)

            @block.vector
            def _(v):
                norm_vector(v, m_, residual=HB)
                v.sem_inc(s_out, 2)
                with v.Fori(0, NT // 2) as i:
                    for u in range(2):
                        t = i * 2 + u
                        hold(v, s_M, t + 3)
                        v.tensor_tensor(XB[:, ds(t * D, D)], XB[:, ds(t * D, D)], psH[u][:, :], ALU.add).then_inc(s_out, 1)

            @block.scalar
            def _(a):
                norm_scalar(a, m_)
                with a.Fori(0, NT // 2) as i:
                    for u in range(2):
                        t = i * 2 + u
                        hold(a, s_T, t + 1)
                        a.activation(xn[:, u, :], XB[:, ds(t * D, D)], ACT.Relu, bias=m_["nmr"][:, ds(t, 1)],
                                     scale=m_["sd"][:, ds(t, 1)]).then_inc(s_xn, 1)
                    for u in range(2):
                        t = i * 2 + u
                        hold(a, s_T, t + 3)
                        hold(a, s_M, t + 1)
                        a.activation(xT[:, u, :], psT[u][:, :], ACT.Copy).then_inc(s_xT, 1)

            @block.tensor
            def _(pe):
                pe.sem_inc(s_T, 2)
                pe.sem_inc(s_M, 2)
                pe.sem_inc(s_xT, 2)
                pe.wait_ge(s_w, 16)
                with pe.Fori(0, NT // 2) as i:
                    for u in range(2):
                        t = i * 2 + u
                        hold(pe, s_xn, t + 1)
                        hold(pe, s_xT, t + 1)
                        for k in range(K):
                            m = pe.transpose(psT[u][:, k * P:(k + 1) * P], xn[:, u, k * P:(k + 1) * P], ident[:, :])
                        m.then_inc(s_T, 1)
                    for u in range(2):
                        t = i * 2 + u
                        hold(pe, s_xT, t + 3)
                        hold(pe, s_out, t + 1)
                        for k in range(K):
                            m = pe.matmul(psH[u][:, :], xT[:, u, k * P:(k + 1) * P], Wl[:, k, :], start=k == 0, stop=k == K - 1)
                        m.then_inc(s_M, 1)

        wn0, wr0, b0, wn1, wr1, b1, wn2, wr2, b2 = sage
        dw0, db0, dw1, db1, dw2, db2 = dec
        DL = (2 * D, D, P)
        SP = R[:, NT * D:2 * NT * D].bitcast(f16)
        sg = Phase()
        sg.__enter__()
        scale_ = sg.sb("scale", [P, 1], f32)
        rdk = sg.sb("rdk", [P, NT], f32)

        def parts(w, source, scaled):
            SPv = SP[:, 0:NT * 2 * w].rearrange("p (t l c) -> p t l c", l=2, c=w)
            with Phase() as ph:
                L = ph.sb("L", [P, 2, w], f32)
                lsc = ph.sb("lsc", [P, 1], f32)
                mx, mxa = ph.sb("mx", [P, 1], f32), ph.sb("mxa", [P, 1], f32)
                s_v, s_m, s_a, s_s, s_h, s_lo = (ph.sem(n) for n in ("v", "m", "a", "s", "h", "lo"))
                block = ph.enter_context(nc.Block())

                if scaled:
                    @block.gpsimd
                    def _(g):
                        g.wait_ge(s_m, 1)
                        g.partition_all_reduce(mxa[:, :], mx[:, :], P, bass.bass_isa.ReduceOp.max).then_inc(s_a, 1)

                @block.vector
                def _(v):
                    ch = Chain(v, s_v)
                    if scaled:
                        v.tensor_reduce(mx[:, :], source[:, 0:NT * w], AX.X, ALU.max, apply_absolute_value=True).then_inc(s_m, 1)
                        v.wait_ge(s_a, 1)
                        ch(v.tensor_scalar(mxa[:, :], mxa[:, :], 1e-20, None, ALU.max))
                        ch.wait()
                        ch(v.reciprocal(mx[:, :], mxa[:, :]))
                        ch(v.tensor_scalar(rdk[:, :], rdeg[:, :], mxa[:, 0:1], 1 / TOP, ALU.mult, ALU.mult))
                        ch.wait()
                        ch(v.tensor_scalar(scale_[:, :], mx[:, :], TOP, None, ALU.mult))
                    else:
                        ch(v.memset(scale_[:, :], TOP / 16))
                    ch.wait()
                    ch(v.tensor_scalar(lsc[:, :], scale_[:, :], LO, None, ALU.mult))
                    ch.wait()
                    v.sem_inc(s_s, 1)
                    v.sem_inc(s_lo, 2)
                    with v.Fori(0, NT // 2) as i:
                        for u in range(2):
                            t = i * 2 + u
                            hold(v, s_h, t * 2 + 2)
                            v.scalar_tensor_tensor(SPv[:, ds(t, 1), 1, :], SPv[:, ds(t, 1), 0, :], -LO,
                                                   L[:, u, :].unsqueeze(1), ALU.mult, ALU.add).then_inc(s_lo, 1)

                @block.scalar
                def _(a):
                    a.wait_ge(s_s, 1)
                    with a.Fori(0, NT // 2) as i:
                        for u in range(2):
                            t = i * 2 + u
                            hold(a, s_lo, t + 1)
                            a.activation(SPv[:, ds(t, 1), 0, :], source[:, ds(t * w, w)].unsqueeze(1), ACT.Copy,
                                         scale=scale_[:, 0:1]).then_inc(s_h, 1)
                            a.activation(L[:, u, :], source[:, ds(t * w, w)], ACT.Copy, scale=lsc[:, 0:1]).then_inc(s_h, 1)
            return SPv

        def neighbours(pe, psA, SPv, t, w, psD=None, ones=None):
            for s in range(NT):
                lhsT = C[:, ds(t * P + s * NP, P)]
                m = pe.matmul(psA[:, :], lhsT, SPv[:, s, :, :].rearrange("p l c -> p (l c)"), start=s == 0, stop=s == NT - 1)
                if psD is not None:
                    m = pe.matmul(psD, lhsT, ones, start=s == 0, stop=s == NT - 1)
            return m

        with Phase() as ph:
            m_ = norm_memory(ph)
            s_x, s_n = ph.sem("x"), ph.sem("n")
            block = ph.enter_context(nc.Block())

            @block.sync
            def _(sp):
                sp.dma_start(xd[:, :], XB).then_inc(s_x, 16)
                sp.wait_ge(s_x, 16)

            @block.vector
            def _(v):
                norm_vector(v, m_)

            @block.scalar
            def _(a):
                norm_scalar(a, m_)
                with a.Fori(0, NT) as t:
                    a.activation(HB[:, ds(t * D, D)], XB[:, ds(t * D, D)], ACT.Relu, bias=m_["nmr"][:, ds(t, 1)],
                                 scale=m_["sd"][:, ds(t, 1)]).then_inc(s_n, 1)

        SPv = parts(D, HB, False)
        H0, H1 = DL[0], DL[1]
        F0 = H0 // P
        with Phase() as ph:
            W0 = ph.sb("W0", [P, 2 * K, H0], f32)
            W1 = ph.sb("W1", [P, F0, 2 * H1], f32)
            b0c = ph.sb("b0c", [P, F0], f32)
            b1r = ph.sb("b1r", [P, H1], f32)
            ones = ph.sb("ones", [P, 1], f16)
            tl = ph.sb("tl", [P, 2, D], f32)
            xs = ph.sb("xs", [P, 2, 2 * D], f32)
            xT = ph.sb("xT", [P, 2, 4 * P], f32)
            hT = ph.sb("hT", [P, 2, F0 * P], f32)
            psA = [ph.ps(f"psA{u}", [P, 2 * D]) for u in range(2)]
            psD = [ph.ps(f"psD{u}", [P, 1]) for u in range(2)]
            psT = [ph.ps(f"psT{u}", [P, 4 * P]) for u in range(2)]
            ps1 = ph.ps("ps1", [P, F0 * P])
            psO = ph.ps("psO", [P, 2 * H1])
            s_c, s_w, s_A, s_tl, s_own, s_mean, s_T, s_xT, s_1, s_hT, s_O, s_out, s_v = (
                ph.sem(n) for n in ("c", "w", "A", "tl", "own", "mean", "T", "xT", "1", "hT", "O", "out", "v"))
            block = ph.enter_context(nc.Block())

            @block.gpsimd
            def _(g):
                g.memset(ones[:, :], 1.0).then_inc(s_c, 1)

            @block.sync
            def _(sp):
                for j, w in enumerate((wn0, wr0)):
                    sp.dma_start(W0[:, j * K:(j + 1) * K, :], w.rearrange("(k p) f -> p k f", p=P)).then_inc(s_w, 16)
                for j, w in enumerate((wn1, wr1)):
                    sp.dma_start(W1[:, :, j * H1:(j + 1) * H1], w.rearrange("(k p) f -> p k f", p=P)).then_inc(s_w, 16)
                with nc.allow_non_contiguous_dma("a bias of 512 elements, one to a partition"):
                    sp.dma_start(b0c[:, :], b0.rearrange("(f p) -> p f", p=P)).then_inc(s_w, 16)
                sp.dma_start(b1r[:, :], b1.rearrange("(a f) -> a f", a=1).to_broadcast([P, H1])).then_inc(s_w, 16)

            @block.tensor
            def _(pe):
                pe.sem_inc(s_xT, 2)
                pe.sem_inc(s_hT, 1)
                pe.wait_ge(s_c, 1)
                pe.wait_ge(s_w, 16 * 6)
                with pe.Fori(0, NT // 2) as i:
                    for u in range(2):
                        t = i * 2 + u
                        hold(pe, s_mean, t + 1)
                        neighbours(pe, psA[u], SPv, t, D, psD[u][:, :], ones[:, :]).then_inc(s_A, 1)
                    for u in range(2):
                        t = i * 2 + u
                        hold(pe, s_mean, t + 3)
                        hold(pe, s_own, t + 1)
                        hold(pe, s_xT, t + 1)
                        for k in range(4):
                            m = pe.transpose(psT[u][:, k * P:(k + 1) * P], xs[:, u, k * P:(k + 1) * P], ident[:, :])
                        m.then_inc(s_T, 1)
                    for u in range(2):
                        t = i * 2 + u
                        hold(pe, s_xT, t + 3)
                        hold(pe, s_hT, t + 1)
                        for f in range(F0):
                            for k in range(4):
                                m = pe.matmul(ps1[:, f * P:(f + 1) * P], W0[:, k, f * P:(f + 1) * P],
                                              xT[:, u, k * P:(k + 1) * P], start=k == 0, stop=k == 3)
                        m.then_inc(s_1, 1)
                    for u in range(2):
                        t = i * 2 + u
                        hold(pe, s_hT, t + 2)
                        hold(pe, s_out, t * 2 + 2)
                        for k in range(F0):
                            m = pe.matmul(psO[:, :], hT[:, u, k * P:(k + 1) * P], W1[:, k, :], start=k == 0, stop=k == F0 - 1)
                        m.then_inc(s_O, 1)

            @block.scalar
            def _(a):
                a.sem_inc(s_T, 2)
                a.sem_inc(s_O, 2)
                a.wait_ge(s_w, 16 * 6)
                with a.Fori(0, NT // 2) as i:
                    for u in range(2):
                        t = i * 2 + u
                        hold(a, s_T, t + 1)
                        a.activation(xs[:, u, D:2 * D], HB[:, ds(t * D, D)], ACT.Copy).then_inc(s_own, 1)
                        hold(a, s_mean, t + 1)
                        hold(a, s_A, t + 1)
                        a.activation(tl[:, u, :], psA[u][:, D:2 * D], ACT.Copy, scale=1 / LO).then_inc(s_tl, 1)
                    for u in range(2):
                        t = i * 2 + u
                        hold(a, s_T, t + 3)
                        a.activation(xT[:, u, :], psT[u][:, :], ACT.Copy).then_inc(s_xT, 1)
                    for u in range(2):
                        t = i * 2 + u
                        hold(a, s_1, t + 1)
                        hold(a, s_O, t + 1)
                        for f in range(F0):
                            ins = a.activation(hT[:, u, f * P:(f + 1) * P], ps1[:, f * P:(f + 1) * P], ACT.Relu, bias=b0c[:, f:f + 1])
                        ins.then_inc(s_hT, 1)

            @block.vector
            def _(v):
                v.sem_inc(s_mean, 2)
                v.sem_inc(s_out, 2)
                v.wait_ge(s_w, 16 * 6)
                with v.Fori(0, NT // 2) as i:
                    for u in range(2):
                        t = i * 2 + u
                        hold(v, s_tl, t + 1)
                        hold(v, s_xT, t + 1)
                        v.tensor_scalar(rdeg[:, ds(t, 1)], psD[u][:, :], 1.0, None, ALU.max).then_inc(s_v, 1)
                        v.tensor_tensor(xs[:, u, 0:D], psA[u][:, 0:D], tl[:, u, :], ALU.add).then_inc(s_v, 1)
                        hold(v, s_v, t * 4 + 2)
                        v.reciprocal(rdeg[:, ds(t, 1)], rdeg[:, ds(t, 1)]).then_inc(s_v, 1)
                        hold(v, s_v, t * 4 + 3)
                        v.tensor_scalar(xs[:, u, 0:D], xs[:, u, 0:D], rdeg[:, ds(t, 1)], 16 / TOP, ALU.mult, ALU.mult).then_inc(s_mean, 1)
                        v.sem_inc(s_v, 1)
                    for u in range(2):
                        t = i * 2 + u
                        hold(v, s_O, t + 3)
                        v.tensor_copy(XB[:, ds(t * H1, H1)], psO[:, 0:H1]).then_inc(s_out, 1)
                        v.tensor_tensor(HB[:, ds(t * H1, H1)], psO[:, H1:2 * H1], b1r[:, :], ALU.add).then_inc(s_out, 1)

        SPv = parts(D, XB, True)
        H2 = DL[2]
        with Phase() as ph:
            W2 = ph.sb("W2", [P, K, 2 * H2], f32)
            b2r = ph.sb("b2r", [P, H2], f32)
            tl = ph.sb("tl", [P, 2, D], f32)
            xs = ph.sb("xs", [P, 2, D], f32)
            xT = ph.sb("xT", [P, 2, D], f32)
            psA = [ph.ps(f"psA{u}", [P, 2 * D]) for u in range(2)]
            psT = [ph.ps(f"psT{u}", [P, D]) for u in range(2)]
            psO = [ph.ps(f"psO{u}", [P, 2 * H2]) for u in range(2)]
            s_w, s_A, s_tl, s_x, s_T, s_xT, s_O, s_out, s_v = (
                ph.sem(n) for n in ("w", "A", "tl", "x", "T", "xT", "O", "out", "v"))
            block = ph.enter_context(nc.Block())

            @block.sync
            def _(sp):
                for j, w in enumerate((wn2, wr2)):
                    sp.dma_start(W2[:, :, j * H2:(j + 1) * H2], w.rearrange("(k p) f -> p k f", p=P)).then_inc(s_w, 16)
                sp.dma_start(b2r[:, :], b2.rearrange("(a f) -> a f", a=1).to_broadcast([P, H2])).then_inc(s_w, 16)

            @block.tensor
            def _(pe):
                pe.sem_inc(s_xT, 2)
                pe.wait_ge(s_w, 16 * 3)
                with pe.Fori(0, NT // 2) as i:
                    for u in range(2):
                        t = i * 2 + u
                        hold(pe, s_x, t + 1)
                        neighbours(pe, psA[u], SPv, t, D).then_inc(s_A, 1)
                    for u in range(2):
                        t = i * 2 + u
                        hold(pe, s_x, t + 3)
                        hold(pe, s_xT, t + 1)
                        for k in range(K):
                            m = pe.transpose(psT[u][:, k * P:(k + 1) * P], xs[:, u, k * P:(k + 1) * P], ident[:, :])
                        m.then_inc(s_T, 1)
                    for u in range(2):
                        t = i * 2 + u
                        hold(pe, s_xT, t + 3)
                        hold(pe, s_out, t * 2 + 2)
                        for k in range(K):
                            m = pe.matmul(psO[u][:, :], xT[:, u, k * P:(k + 1) * P], W2[:, k, :], start=k == 0, stop=k == K - 1)
                        m.then_inc(s_O, 1)

            @block.scalar
            def _(a):
                a.sem_inc(s_O, 2)
                with a.Fori(0, NT // 2) as i:
                    for u in range(2):
                        t = i * 2 + u
                        hold(a, s_x, t + 1)
                        hold(a, s_A, t + 1)
                        a.activation(tl[:, u, :], psA[u][:, D:2 * D], ACT.Copy, scale=1 / LO).then_inc(s_tl, 1)
                    for u in range(2):
                        t = i * 2 + u
                        hold(a, s_T, t + 1)
                        hold(a, s_O, t + 1)
                        a.activation(xT[:, u, :], psT[u][:, :], ACT.Copy).then_inc(s_xT, 1)

            @block.vector
            def _(v):
                v.sem_inc(s_x, 2)
                v.sem_inc(s_out, 4)
                v.wait_ge(s_w, 16 * 3)
                with v.Fori(0, NT // 2) as i:
                    for u in range(2):
                        t = i * 2 + u
                        hold(v, s_tl, t + 1)
                        hold(v, s_xT, t + 1)
                        v.tensor_tensor(xs[:, u, :], psA[u][:, 0:D], tl[:, u, :], ALU.add).then_inc(s_v, 1)
                        hold(v, s_v, t * 2 + 1)
                        v.scalar_tensor_tensor(xs[:, u, :], xs[:, u, :], rdk[:, ds(t, 1)], HB[:, ds(t * D, D)],
                                               ALU.mult, ALU.add).then_inc(s_v, 1)
                        hold(v, s_v, t * 2 + 2)
                        v.tensor_scalar(xs[:, u, :], xs[:, u, :], 0.0, None, ALU.max).then_inc(s_x, 1)
                    for u in range(2):
                        t = i * 2 + u
                        hold(v, s_O, t + 3)
                        v.tensor_copy(XB[:, ds(t * H2, H2)], psO[u][:, 0:H2]).then_inc(s_out, 1)
                        v.tensor_tensor(HB[:, ds(t * D, H2)], psO[u][:, H2:2 * H2], b2r[:, :], ALU.add).then_inc(s_out, 1)

        SPv = parts(H2, XB, True)
        G0, G1 = D, 2 * D
        with Phase() as ph:
            E0 = ph.sb("E0", [P, G0], f32)
            E1 = ph.sb("E1", [P, G0 // P, G1], f32)
            E2 = ph.sb("E2", [P, G1 // P, D], f32)
            c0, c1 = ph.sb("c0", [P, G0 // P], f32), ph.sb("c1", [P, G1 // P], f32)
            c2 = ph.sb("c2", [P, D], f32)
            tl = ph.sb("tl", [P, 2, H2], f32)
            xs = ph.sb("xs", [P, 2, H2], f32)
            xT = ph.sb("xT", [P, 2, H2], f32)
            h0 = ph.sb("h0", [P, 2, G0], f32)
            h1 = ph.sb("h1", [P, 2, G1], f32)
            y = ph.sb("y", [P, 2, D], f32)
            xr = ph.sb("xr", [P, 2, D], f32)
            psA = [ph.ps(f"psA{u}", [P, 2 * H2]) for u in range(2)]
            psT = ph.ps("psT", [P, H2])
            ps0 = ph.ps("ps0", [P, G0])
            ps1 = [ph.ps(f"ps1{u}", [P, G1]) for u in range(2)]
            psO = [ph.ps(f"psO{u}", [P, D]) for u in range(2)]
            s_w, s_A, s_tl, s_x, s_T, s_xT, s_0, s_h0, s_1, s_h1, s_O, s_out, s_v, s_y = (
                ph.sem(n) for n in ("w", "A", "tl", "x", "T", "xT", "0", "h0", "1", "h1", "O", "out", "v", "y"))
            s_xr = [ph.sem(f"xr{u}") for u in range(2)]
            block = ph.enter_context(nc.Block())

            @block.sync
            def _(sp):
                sp.dma_start(E0[:, :], dw0).then_inc(s_w, 16)
                for w, m in ((E1, dw1), (E2, dw2)):
                    sp.dma_start(w[:, :, :], m.rearrange("(k p) f -> p k f", p=P)).then_inc(s_w, 16)
                with nc.allow_non_contiguous_dma("biases of 768 elements, one to a partition"):
                    for w, m in ((c0, db0), (c1, db1)):
                        sp.dma_start(w[:, :], m.rearrange("(f p) -> p f", p=P)).then_inc(s_w, 16)
                sp.dma_start(c2[:, :], db2.rearrange("(a f) -> a f", a=1).to_broadcast([P, D])).then_inc(s_w, 16)
                with sp.Fori(0, NT // 2) as i:
                    for u in range(2):
                        t = i * 2 + u
                        sp.wait_ge(s_out, t + 1)
                        sp.dma_start(xr[:, u, :], xd[:, ds(t * D, D)]).then_inc(s_xr[u], 16)

            @block.tensor
            def _(pe):
                pe.sem_inc(s_xT, 1)
                pe.sem_inc(s_h0, 1)
                pe.sem_inc(s_h1, 2)
                pe.wait_ge(s_w, 16 * 6)
                with pe.Fori(0, NT // 2) as i:
                    for u in range(2):
                        t = i * 2 + u
                        hold(pe, s_x, t + 1)
                        neighbours(pe, psA[u], SPv, t, H2).then_inc(s_A, 1)
                    for u in range(2):
                        t = i * 2 + u
                        hold(pe, s_x, t + 3)
                        hold(pe, s_xT, t + 1)
                        pe.transpose(psT[:, :], xs[:, u, :], ident[:, :]).then_inc(s_T, 1)
                    for u in range(2):
                        t = i * 2 + u
                        hold(pe, s_xT, t + 2)
                        hold(pe, s_h0, t + 1)
                        for f in range(G0 // P):
                            m = pe.matmul(ps0[:, f * P:(f + 1) * P], E0[:, f * P:(f + 1) * P], xT[:, u, :], start=True, stop=True)
                        m.then_inc(s_0, 1)
                    for u in range(2):
                        t = i * 2 + u
                        hold(pe, s_h0, t + 2)
                        hold(pe, s_h1, t + 1)
                        for f in range(G1 // P):
                            for k in range(G0 // P):
                                m = pe.matmul(ps1[u][:, f * P:(f + 1) * P], E1[:, k, f * P:(f + 1) * P],
                                              h0[:, u, k * P:(k + 1) * P], start=k == 0, stop=k == G0 // P - 1)
                        m.then_inc(s_1, 1)
                    for u in range(2):
                        t = i * 2 + u
                        hold(pe, s_h1, t + 3)
                        hold(pe, s_out, t + 1)
                        for k in range(G1 // P):
                            m = pe.matmul(psO[u][:, :], h1[:, u, k * P:(k + 1) * P], E2[:, k, :], start=k == 0, stop=k == G1 // P - 1)
                        m.then_inc(s_O, 1)

            @block.scalar
            def _(a):
                a.sem_inc(s_O, 2)
                a.sem_inc(s_0, 2)
                a.sem_inc(s_1, 2)
                a.wait_ge(s_w, 16 * 6)
                with a.Fori(0, NT // 2) as i:
                    for u in range(2):
                        t = i * 2 + u
                        hold(a, s_x, t + 1)
                        hold(a, s_A, t + 1)
                        a.activation(tl[:, u, :], psA[u][:, H2:2 * H2], ACT.Copy, scale=1 / LO).then_inc(s_tl, 1)
                    for u in range(2):
                        t = i * 2 + u
                        hold(a, s_T, t + 1)
                        hold(a, s_0, t + 1)
                        a.activation(xT[:, u, :], psT[:, :], ACT.Copy).then_inc(s_xT, 1)
                    for u in range(2):
                        t = i * 2 + u
                        hold(a, s_0, t + 3)
                        hold(a, s_1, t + 1)
                        for f in range(G0 // P):
                            ins = a.activation(h0[:, u, f * P:(f + 1) * P], ps0[:, f * P:(f + 1) * P], ACT.Relu, bias=c0[:, f:f + 1])
                        ins.then_inc(s_h0, 1)
                    for u in range(2):
                        t = i * 2 + u
                        hold(a, s_1, t + 3)
                        hold(a, s_O, t + 1)
                        for f in range(G1 // P):
                            ins = a.activation(h1[:, u, f * P:(f + 1) * P], ps1[u][:, f * P:(f + 1) * P], ACT.Relu, bias=c1[:, f:f + 1])
                        ins.then_inc(s_h1, 1)

            @block.vector
            def _(v):
                v.sem_inc(s_x, 2)
                v.sem_inc(s_out, 2)
                v.wait_ge(s_w, 16 * 6)
                with v.Fori(0, NT // 2) as i:
                    for u in range(2):
                        t = i * 2 + u
                        hold(v, s_tl, t + 1)
                        hold(v, s_xT, t + 0 + 1)
                        v.tensor_tensor(xs[:, u, :], psA[u][:, 0:H2], tl[:, u, :], ALU.add).then_inc(s_v, 1)
                        hold(v, s_v, t * 2 + 1)
                        v.scalar_tensor_tensor(xs[:, u, :], xs[:, u, :], rdk[:, ds(t, 1)], HB[:, ds(t * D, H2)],
                                               ALU.mult, ALU.add).then_inc(s_v, 1)
                        hold(v, s_v, t * 2 + 2)
                        v.tensor_scalar(xs[:, u, :], xs[:, u, :], 0.0, None, ALU.max).then_inc(s_x, 1)
                    for u in range(2):
                        t = i * 2 + u
                        hold(v, s_O, t + 3)
                        hold(v, s_out, t + 1)
                        v.tensor_tensor(y[:, u, :], psO[u][:, :], c2[:, :], ALU.add).then_inc(s_y, 1)
                        hold(v, s_y, t + 1)
                        hold(v, s_xr[u], i * 16 + 16)
                        v.scalar_tensor_tensor(HB[:, ds(t * D, D)], y[:, u, :], 0.0, xr[:, u, :], ALU.max, ALU.add).then_inc(s_out, 1)
        sg.close()

        with Phase() as ph:
            G4 = 4
            psU = [ph.ps(f"psU{u}", [P, G4 * P], f16) for u in range(2)]
            psL = [ph.ps(f"psL{u}", [P, G4 * P], f16) for u in range(2)]
            s_t, s_u, s_l, s_m, s_st = (ph.sem(n) for n in ("t", "u", "l", "m", "st"))
            block = ph.enter_context(nc.Block())
            Cv = C[:, :].rearrange("p (s d) -> p s d", d=NP)
            groups = [(i, j, min(j + G4, NT)) for i in range(NT) for j in range(i, NT, G4)]

            @block.tensor
            def _(pe):
                for n, (i, j0, j1) in enumerate(groups):
                    if n >= 2:
                        pe.wait_ge(s_u, n - 1)
                        pe.wait_ge(s_l, n - 1)
                    for j in range(j0, j1):
                        q = (j - j0) * P
                        pe.transpose(psU[n % 2][:, q:q + P], Cv[:, i, j * P:(j + 1) * P], ident16[:, :])
                        m = pe.transpose(psL[n % 2][:, q:q + P], Cv[:, j, i * P:(i + 1) * P], ident16[:, :])
                    m.then_inc(s_t, 1)

            @block.vector
            def _(v):
                for n, (i, j0, j1) in enumerate(groups):
                    v.wait_ge(s_t, n + 1)
                    v.tensor_copy(Cv[:, i, j0 * P:j1 * P], psL[n % 2][:, 0:(j1 - j0) * P]).then_inc(s_l, 1)

            @block.scalar
            def _(a):
                for n, (i, j0, j1) in enumerate(groups):
                    a.wait_ge(s_t, n + 1)
                    k = 1 if j0 == i else 0
                    if j1 - j0 > k:
                        a.activation(Cv[:, j0 + k:j1, i * P:(i + 1) * P],
                                     psU[n % 2][:, k * P:(j1 - j0) * P].rearrange("p (s d) -> p s d", d=P),
                                     ACT.Copy).then_inc(s_u, 1)
                    else:
                        a.sem_inc(s_u, 1)

            @block.gpsimd
            def _(g):
                g.tensor_copy(XB, HB[:, 0:NT * D]).then_inc(s_m, 1)

            @block.sync
            def _(sp):
                sp.dma_start(xd[:, :], HB[:, 0:NT * D]).then_inc(s_st, 16)
                sp.wait_ge(s_st, 16)

        attention(gat3, 4, 64, True, True, -1, AB, False)
        elu(HB[:, 0:NT * (D + 4)], XB, None, 4, True)
        with Phase() as ph:
            s_x, s_y, s_out = ph.sem("x"), ph.sem("y"), ph.sem("out")
            block = ph.enter_context(nc.Block())

            @block.sync
            def _(sp):
                sp.dma_start(HB[:, 0:NT * D], xd[:, :]).then_inc(s_x, 16)
                sp.wait_ge(s_y, 1)
                sp.dma_start(out[0:(NT - 1) * P, :].rearrange("(t p) f -> p t f", p=P),
                             XB[:, 0:(NT - 1) * D].rearrange("p (t f) -> p t f", f=D)).then_inc(s_out, 16)
                sp.dma_start(out[(NT - 1) * P:N, :], XB[0:LAST, (NT - 1) * D:NT * D]).then_inc(s_out, 16)
                sp.wait_ge(s_out, 32)

            @block.vector
            def _(v):
                v.wait_ge(s_x, 16)
                v.tensor_tensor(XB, XB, HB[:, 0:NT * D], ALU.add).then_inc(s_y, 1)


_INS = ["x", "src", "dst", "edge_weight"] + [f"L0_gnn_{n}" for n in ("W0", "al0", "ar0", "b0", "W1", "al1", "ar1", "b1")] \
    + [f"L2_gnn_{n}" for n in ("wn0", "wr0", "b0", "wn1", "wr1", "b1", "wn2", "wr2", "b2",
                               "dw0", "db0", "dw1", "db1", "dw2", "db2")] + ["L3_gnn_W", "L3_gnn_a"]


def kernel(**inputs):
    import numpy as _np
    import concourse.bacc as _bacc
    from concourse import mybir as _mybir
    from concourse.bass_utils import run_bass_kernel_spmd as _run

    nc = _bacc.Bacc("TRN2", target_bir_lowering=False, num_devices=1)
    arrays, args = {}, []
    for name in _INS:
        a = _np.ascontiguousarray(inputs[name])
        arrays[f"in_{name}"] = a
        args.append(nc.dram_tensor(f"in_{name}", a.shape, _mybir.dt.from_np(a.dtype), kind="ExternalInput").ap())
    out = nc.dram_tensor("out_0", (N, D), _mybir.dt.float32, kind="ExternalOutput").ap()
    build(nc, args[0], args[1], args[2], args[3], args[4:8], args[8:12], args[12:21], args[21:27], args[27:29], out)
    r = _run(nc, [arrays], core_ids=[0])
    return r.results[0]["out_0"]
```

```python
import concourse.bass as bass
from concourse import mybir
from contextlib import ExitStack

P = 128
N = 2500
E = 40000
D = 256
NT = (N + P - 1) // P
NP = NT * P
LAST = N - (NT - 1) * P
NCH = (E + P - 1) // P
NG = (NCH + P - 1) // P
CENTRE = NP // 2
FAR = 1.0e6
BIG = float(2 ** 60)
LO = 2048.0
TOP = 32768.0
SLOPE = 0.2
MORE_ON_ACT = {(0, 7), (1, 11)}
EPS = 1e-5
OOB = 1 << 20


class Chain:

    def __init__(self, eng, sem):
        self.eng, self.sem, self.base, self.n = eng, sem, 0, 0

    def __call__(self, ins):
        ins.then_inc(self.sem, 1)
        self.n += 1
        return ins

    def wait(self):
        self.eng.wait_ge(self.sem, self.base + self.n)

    def begin(self, i, per):
        self.start, self.per = self.base + self.n, per
        self.base, self.n = self.start + i * per, 0

    def end(self, trips):
        assert self.n == self.per, (self.n, self.per)
        self.base, self.n = self.start + trips * self.per, 0


def build(nc, x, src, dst, ew, gat0, gat1, sage, dec, gat3, out):
    f32, f16, bf16, i32 = mybir.dt.float32, mybir.dt.float16, mybir.dt.bfloat16, mybir.dt.int32
    ALU, ACT, AX = mybir.AluOpType, mybir.ActivationFunctionType, mybir.AxisListType
    ds = bass.ds
    top = ExitStack()
    with top:
        def sb(name, shape, dt, ctx=top):
            return ctx.enter_context(nc.sbuf_tensor(name, shape, dt))

        names = [0]
        used = []

        class Phase(ExitStack):

            def sb(self, name, shape, dt):
                names[0] += 1
                return self.enter_context(nc.sbuf_tensor(f"{name}_{names[0]}", shape, dt))

            def ps(self, name, shape, dt=f32):
                names[0] += 1
                return self.enter_context(nc.psum_tensor(f"{name}_{names[0]}", shape, dt))

            def sem(self, name):
                names[0] += 1
                handle = nc.alloc_semaphore(f"{name}_{names[0]}")
                self.callback(lambda: used.append(handle))
                return handle

            def __exit__(self, *failure):
                done = super().__exit__(*failure)
                if used and failure[0] is None:
                    nc.clear_and_free_semaphores(list(used))
                    nc.all_engine_barrier()
                    used.clear()
                return done

        C = sb("C", [P, NT * NP], f16)
        HB = sb("HB", [P, NT * 264], f32)
        R = sb("R", [P, NT * 528], f32)
        Rh = R[:, :].bitcast(f16)
        ident = sb("ident", [P, P], f32)
        ident16 = sb("ident16", [P, P], f16)
        padneg = sb("padneg", [P, 1], f32)
        eps = sb("eps", [P, 1], f32)
        rdeg = sb("rdeg", [P, NT], f32)
        XB = R[:, 0:NT * D]
        AB = sb("AB", [P, NT * 16], f32)
        hmax = sb("hmax", [P, NT], f32)
        table = sb("table", [1, 4 * NT], i32)
        wd = nc.dram_tensor("wd", [D * D, 1], f32, kind="Internal").ap()
        xd = nc.dram_tensor("xd", [P, NT * D], f32, kind="Internal").ap()
        rowd = nc.dram_tensor("rowd", [NT * 16, P], f32, kind="Internal").ap()
        keyd = nc.dram_tensor("keyd", [NG * P, P], f32, kind="Internal").ap()
        late_ = ExitStack()
        edge = ExitStack()
        widx = sb("widx", [P, NG * P], i32, late_)
        ewT = sb("ewT", [P, NG * P], f32, late_)
        srcT = sb("srcT", [P, NG * P], f32, edge)
        dstT = sb("dstT", [P, NG * P], f32, edge)
        keyT = sb("keyT", [P, NG * P], f32, edge)
        wcell = sb("wcell", [P, NG * P], f32, edge)
        late = sb("late", [P, NG * P], f32, edge)

        dum = top.enter_context(nc.semaphore("dum"))

        def hold(eng, sem, value):
            eng.wait_ge(sem, value)
            eng.sem_inc(dum, 1)

        def chunk(value, most):
            return nc.s_assert_within(value, 0, most, skip_runtime_bounds_check_because=
                                      "a range of chunks starts below NCH and is at most NCH or four chunks long")

        def rows_in(eng, dest, dram, sem):
            eng.dma_start(dest[:, 0:(NT - 1) * D].rearrange("p (t f) -> p t f", f=D),
                          dram[0:(NT - 1) * P, :].rearrange("(t p) f -> p t f", p=P)).then_inc(sem, 16)
            eng.dma_start(dest[0:LAST, (NT - 1) * D:NT * D], dram[(NT - 1) * P:N, :]).then_inc(sem, 16)

        with Phase() as ph:
            raw = [ph.sb(f"raw{i}", [P, NG * P], dt) for i, dt in enumerate((i32, i32, f32))]
            rf = [ph.sb(f"rf{i}", [P, NG * P], f32) for i in range(2)]
            key = ph.sb("key", [P, NG * P], f32)
            tmp = ph.sb("tmp", [P, NG * P], f32)
            zero = ph.sb("zero", [P, 512], f32)
            cmin, cmax = ph.sb("cmin", [P, NG], f32), ph.sb("cmax", [P, NG], f32)
            tlo = ph.sb("tlo", [P, NT], f32)
            cidx = ph.sb("cidx", [P, NG], f32)
            away = ph.sb("away", [P, NG], f32)
            ov = ph.sb("ov", [P, NG * NT], f32)
            ov2 = ph.sb("ov2", [P, NG * NT], f32)
            lohi = ph.sb("lohi", [P, 2, NG, NT], f32)
            lohir = ph.sb("lohir", [P, 2, NG, NT], f32)
            lh = ph.sb("lh", [1, 2, NT], f32)
            row = ph.sb("row", [1, 8, NT], f32)
            pst = [ph.ps(f"pst{i}", [P, P]) for i in range(4)]
            s_xz, s_set, s_in, s_rf, s_t, s_ev, s_lohi, s_all, s_iota, s_z, s_st, s_v = (
                ph.sem(n) for n in ("xz", "set", "in", "rf", "t", "ev", "lohi", "all", "iota", "z", "st", "v"))
            block = ph.enter_context(nc.Block())

            @block.gpsimd
            def _(g):
                for q in range(2):
                    g.memset(raw[q][:, :], -1).then_inc(s_set, 1)
                g.memset(raw[2][:, :], 0.0).then_inc(s_set, 1)
                g.memset(zero[:, :], 0.0).then_inc(s_set, 1)
                g.memset(ident[:, :], 0.0).then_inc(s_z, 1)
                g.memset(XB[:, (NT - 1) * D:NT * D], 0.0).then_inc(s_xz, 1)
                g.memset(padneg[:, :], 0.0).then_inc(s_z, 1)
                g.memset(eps[:, :], EPS).then_inc(s_z, 1)
                g.iota(tlo[:, :], pattern=[[P, NT]], base=0, channel_multiplier=0,
                       allow_small_or_imprecise_dtypes=True).then_inc(s_iota, 1)
                g.iota(cidx[:, :], pattern=[[P, NG]], base=0, channel_multiplier=1,
                       allow_small_or_imprecise_dtypes=True).then_inc(s_iota, 1)
                g.wait_ge(s_z, 3)
                g.affine_select(out=ident[:, :], in_=ident[:, :], compare_op=ALU.not_equal, fill=1.0, base=0,
                                pattern=[[-1, P]], channel_multiplier=1).then_inc(s_z, 1)
                g.affine_select(out=padneg[:, :], in_=padneg[:, :], compare_op=ALU.is_gt, fill=-1e9, base=LAST,
                                pattern=[[0, 1]], channel_multiplier=-1).then_inc(s_z, 1)
                g.wait_ge(s_z, 5)
                g.tensor_copy(ident16[:, :], ident[:, :]).then_inc(s_z, 1)
                g.wait_ge(s_lohi, 1)
                g.partition_all_reduce(lohir[:, :, :, :].rearrange("p a g t -> p (a g t)"),
                                       lohi[:, :, :, :].rearrange("p a g t -> p (a g t)"), P,
                                       bass.bass_isa.ReduceOp.max).then_inc(s_all, 1)

            @block.sync
            def _(sp):
                sp.wait_ge(s_set, 4)
                full = NCH - 1 - (NG - 1) * P
                for q, a in enumerate((src, dst, ew)):
                    for g in range(NG - 1):
                        sp.dma_start(raw[q][:, g * P:(g + 1) * P],
                                     a[g * P * P:(g + 1) * P * P].rearrange("(c j) -> c j", j=P)).then_inc(s_in, 16)
                    sp.dma_start(raw[q][0:full, (NG - 1) * P:NG * P],
                                 a[(NG - 1) * P * P:(NCH - 1) * P].rearrange("(c j) -> c j", j=P)).then_inc(s_in, 16)
                    sp.dma_start(raw[q][full:full + 1, (NG - 1) * P:(NG - 1) * P + E - (NCH - 1) * P],
                                 a[(NCH - 1) * P:E].rearrange("(c j) -> c j", c=1)).then_inc(s_in, 16)
                sp.dma_start(wd.rearrange("(p c) a -> p (c a)", p=P), zero[:, :]).then_inc(s_st, 16)
                sp.wait_ge(s_rf, 1)
                for g in range(NG):
                    sp.dma_start(keyd[g * P:(g + 1) * P, :], key[:, g * P:(g + 1) * P]).then_inc(s_st, 16)
                sp.wait_ge(s_st, 16 * (NG + 1))

            @block.tensor
            def _(pe):
                pe.wait_ge(s_z, 6)
                pe.wait_ge(s_rf, 1)
                for n in range(4 * NG):
                    q, g = divmod(n, NG)
                    if n >= 4:
                        pe.wait_ge(s_ev, n - 3)
                    a = (rf[0], rf[1], raw[2], key)[q]
                    pe.transpose(pst[n % 4][:, :], a[:, g * P:(g + 1) * P], ident[:, :]).then_inc(s_t, 1)

            @block.vector
            def _(v):
                ch = Chain(v, s_v)
                v.wait_ge(s_in, 16 * 3 * (NG + 1))
                for q in range(2):
                    ch(v.tensor_copy(rf[q][:, :], raw[q][:, :]))
                ch.wait()
                v.scalar_tensor_tensor(key[:, :], rf[0][:, :], float(4096), rf[1][:, :], ALU.mult,
                                       ALU.add).then_inc(s_rf, 1)
                ch(v.tensor_scalar(tmp[:, :], rf[1][:, :], 0.0, FAR, ALU.is_lt, ALU.mult))
                ch(v.tensor_reduce(cmax[:, :], rf[1][:, :].rearrange("p (g j) -> p g j", j=P), AX.X, ALU.max))
                ch.wait()
                ch(v.tensor_tensor(tmp[:, :], tmp[:, :], rf[1][:, :], ALU.add))
                ch.wait()
                ch(v.tensor_reduce(cmin[:, :], tmp[:, :].rearrange("p (g j) -> p g j", j=P), AX.X, ALU.min))
                v.wait_ge(s_iota, 2)
                ch(v.tensor_scalar(away[:, :], cidx[:, :], -1.0, FAR, ALU.mult, ALU.add))
                ch(v.tensor_scalar(cidx[:, :], cidx[:, :], 1.0, None, ALU.add))
                ch.wait()
                for g in range(NG):
                    o = ov[:, g * NT:(g + 1) * NT]
                    o2 = ov2[:, g * NT:(g + 1) * NT]
                    ch(v.tensor_scalar(o, tlo[:, :], float(P), cmin[:, g:g + 1], ALU.add, ALU.is_gt))
                    ch(v.tensor_scalar(o2, tlo[:, :], cmax[:, g:g + 1], None, ALU.is_le))
                ch.wait()
                ch(v.tensor_tensor(ov[:, :], ov[:, :], ov2[:, :], ALU.mult))
                ch.wait()
                for g in range(NG):
                    o = ov[:, g * NT:(g + 1) * NT]
                    ch(v.tensor_scalar(lohi[:, 0, g, :], o, away[:, g:g + 1], None, ALU.mult))
                    ch(v.tensor_scalar(lohi[:, 1, g, :], o, cidx[:, g:g + 1], None, ALU.mult))
                ch.wait()
                v.sem_inc(s_lohi, 1)
                for n in range(4 * NG):
                    q, g = divmod(n, NG)
                    v.wait_ge(s_t, n + 1)
                    if q < 2:
                        v.tensor_scalar((srcT, dstT)[q][:, g * P:(g + 1) * P], pst[n % 4][:, :], -float(CENTRE),
                                        None, ALU.add).then_inc(s_ev, 1)
                    else:
                        v.tensor_copy((ewT, keyT)[q - 2][:, g * P:(g + 1) * P], pst[n % 4][:, :]).then_inc(s_ev, 1)
                v.wait_ge(s_ev, 4 * NG)
                ch(v.tensor_scalar(wcell[:, :], srcT[:, :], float(D - CENTRE), None, ALU.is_lt))
                ch(v.tensor_scalar(late[:, :], dstT[:, :], float(D - CENTRE), None, ALU.is_lt))
                ch.wait()
                ch(v.tensor_tensor(wcell[:, :], wcell[:, :], late[:, :], ALU.mult))
                ch(v.tensor_scalar(tmp[:, :], srcT[:, :], float(-CENTRE), None, ALU.is_ge))
                ch.wait()
                ch(v.tensor_tensor(wcell[:, :], wcell[:, :], tmp[:, :], ALU.mult))
                ch.wait()
                ch(v.tensor_scalar(tmp[:, :], srcT[:, :], float(D), float(CENTRE * D + CENTRE - OOB), ALU.mult, ALU.add))
                ch.wait()
                ch(v.tensor_tensor(tmp[:, :], tmp[:, :], dstT[:, :], ALU.add))
                ch.wait()
                ch(v.tensor_tensor(tmp[:, :], tmp[:, :], wcell[:, :], ALU.mult))
                ch(v.memset(late[:, :], 0.0))
                ch.wait()
                ch(v.tensor_scalar(wcell[:, :], tmp[:, :], float(OOB), None, ALU.add))
                v.wait_ge(s_all, 1)
                ch(v.tensor_reduce(lh[:, :, :], lohir[0:1, :, :, :].rearrange("p a g t -> p a t g"), AX.X, ALU.max))
                ch.wait()
                first, fours, acc, acc2 = (row[:, i, :] for i in range(4))
                ch(v.tensor_scalar(first, lh[:, 0, :], -1.0, FAR, ALU.mult, ALU.add))
                ch.wait()
                ch(v.tensor_scalar(first, first, float(NCH - 1), None, ALU.min))
                ch.wait()
                ch(v.tensor_tensor(fours, lh[:, 1, :], first, ALU.subtract))
                ch.wait()
                ch(v.tensor_scalar(fours, fours, 0.25, 0.375, ALU.mult, ALU.add))
                ch.wait()
                ch(v.tensor_scalar(table[:, NT:2 * NT], fours, 2.0, None, ALU.max))
                ch.wait()
                ch(v.tensor_copy(acc, table[:, NT:2 * NT]))
                ch(v.tensor_copy(table[:, 0:NT], first))
                ch.wait()
                ch(v.tensor_copy(row[:, 4, :], acc))
                step = 1
                while step < NT:
                    ch.wait()
                    ch(v.tensor_tensor(acc2[:, step:NT], acc[:, step:NT], acc[:, 0:NT - step], ALU.add))
                    ch(v.tensor_copy(acc2[:, 0:step], acc[:, 0:step]))
                    acc, acc2 = acc2, acc
                    step *= 2
                ch.wait()
                ch(v.tensor_tensor(table[:, 2 * NT:3 * NT], acc, row[:, 4, :], ALU.subtract))
                wlo, whi = row[:, 5, 0:1], row[:, 5, 1:2]
                WT = D // P
                ch(v.tensor_reduce(wlo, first[:, 0:WT], AX.X, ALU.min))
                ch(v.tensor_reduce(whi, lh[:, 1, 0:WT], AX.X, ALU.max))
                ch.wait()
                ch(v.tensor_tensor(row[:, 5, 2:3], whi, wlo, ALU.subtract))
                ch.wait()
                ch(v.tensor_scalar(row[:, 5, 3:4], row[:, 5, 2:3], 0.25, 0.375, ALU.mult, ALU.add))
                ch.wait()
                ch(v.tensor_scalar(table[:, 3 * NT + 1:3 * NT + 2], row[:, 5, 3:4], 1.0, None, ALU.max))
                ch(v.tensor_copy(table[:, 3 * NT:3 * NT + 1], wlo))
                ch.wait()

        with Phase() as ph:
            node16 = ph.sb("node16", [P, NP], f16)
            ohs = ph.sb("ohs", [P, 4, NP], f16)
            ohd = ph.sb("ohd", [P, 4, P], f16)
            keyr = ph.sb("keyr", [P, 2, 4, P], f32)
            notlater = ph.sb("notlater", [P, P], f32)
            same = HB[:, 0:2 * 4 * P].rearrange("p (w u j) -> p w u j", w=2, j=P)
            junk = HB[:, 2 * 4 * P:3 * 4 * P].rearrange("p (u j) -> p u j", j=P)
            acc = ph.ps("acc", [P, 8, 4 * P])
            s_c, s_oh, s_used, s_out, s_same, s_late, s_abs, s_kdone = (
                ph.sem(n) for n in ("c", "oh", "used", "out", "same", "late", "abs", "kd"))
            s_key = [ph.sem(f"key{w}") for w in range(2)]
            s_x = ph.sem("x")
            block = ph.enter_context(nc.Block())
            PERBANK = 4
            NB = NT // PERBANK
            OWN, SHARED = list(range(8 - NB)), list(range(8 - NB, NB))
            bank = lambda b, side: acc[:, b + NB * (side == 1 and b in OWN), :]
            DR = (NCH + 4 * NT - 1) // (4 * NT)

            @block.gpsimd
            def _(g):
                g.iota(node16[:, :], pattern=[[1, NP]], base=-CENTRE, channel_multiplier=0,
                       allow_small_or_imprecise_dtypes=True).then_inc(s_c, 1)
                g.memset(notlater[:, :], 0.0).then_inc(s_c, 1)
                g.wait_ge(s_c, 2)
                g.affine_select(out=notlater[:, :], in_=notlater[:, :], compare_op=ALU.is_gt, fill=1e9, base=0,
                                pattern=[[1, P]], channel_multiplier=-1).then_inc(s_c, 1)
                g.wait_ge(s_c, 3)
                with g.Fori(0, NT * DR // 2) as j:
                    for w in range(2):
                        i = j * 2 + w
                        hold(g, s_key[w], (j + 1) * 16)
                        hold(g, s_late, i * 4 + 4)
                        g.tensor_tensor(same[:, w, :, :], keyr[:, w, :, :],
                                        keyT[:, ds(i * 4, 4)].unsqueeze(2).to_broadcast([P, 4, P]),
                                        ALU.subtract).then_inc(s_same, 1)
                        hold(g, s_same, i * 2 + 1)
                        g.tensor_tensor(same[:, w, :, :], same[:, w, :, :],
                                        notlater[:, :].unsqueeze(1).to_broadcast([P, 4, P]), ALU.add).then_inc(s_same, 1)

            @block.sync
            def _(sp):
                rows_in(sp, XB, x, s_x)
                with sp.Fori(0, NT * DR // 2) as j:
                    for w in range(2):
                        i = j * 2 + w
                        sp.wait_ge(s_kdone, i + 1)
                        sp.dma_start(keyr[:, w, :, :], keyd[ds(i * 4, 4), :].unsqueeze(0).to_broadcast([P, 4, P])
                                     ).then_inc(s_key[w], 16)
                sp.wait_ge(s_x, 32)

            @block.scalar
            def _(a):
                a.sem_inc(s_late, 8)
                a.sem_inc(s_kdone, 2)
                with a.Fori(0, NT // 2) as half:
                    for side in range(2):
                        t = half * 2 + side
                        fours = a.value_load(table[0:1, ds(t + NT, 1)], min_val=2, max_val=NCH)
                        before = a.value_load(table[0:1, ds(t + 2 * NT, 1)], min_val=0, max_val=NT * NCH)
                        for r in range(DR):
                            n = t * DR + r
                            hold(a, s_same, n * 2 + 2)
                            a.sem_inc(s_kdone, 1)
                            hold(a, s_late, n * 4 + 8)
                            a.activation(junk[:, :, :], same[:, r % 2, :, :], ACT.Square).then_inc(s_abs, 1)
                            hold(a, s_abs, n + 1)
                            for u in range(4):
                                a.activation(same[:, r % 2, u, :], junk[:, u, :], ACT.Relu, bias=1.0, scale=-1.0,
                                             accum_out=late[:, ds(n * 4 + u, 1)]).then_inc(s_late, 1)
                        hold(a, s_used, (before + fours) * 4 + 4)
                        for b in SHARED + OWN:
                            dest = C[:, :].rearrange("p (s d) -> p s d", d=NP)[:, b * PERBANK:(b + 1) * PERBANK, ds(t * P, P)]
                            a.activation(dest, bank(b, side).rearrange("p (s d) -> p s d", d=P), ACT.Copy).then_inc(s_out, 1)

            @block.vector
            def _(v):
                v.wait_ge(s_c, 1)
                with v.Fori(0, NT) as t:
                    first = v.value_load(table[0:1, ds(t, 1)], min_val=0, max_val=NCH - 1)
                    fours = v.value_load(table[0:1, ds(t + NT, 1)], min_val=2, max_val=NCH)
                    before = v.value_load(table[0:1, ds(t + 2 * NT, 1)], min_val=0, max_val=NT * NCH)
                    with v.Fori(0, fours) as i:
                        for u in range(4):
                            k = chunk(first + i * 4 + u, NG * P - 1)
                            v.wait_ge(s_used, (before + i) * 4 + u + 1)
                            v.tensor_scalar(ohs[:, u, :], node16[:, :], srcT[:, ds(k, 1)], None,
                                            ALU.is_equal).then_inc(s_oh, 1)
                            v.tensor_scalar(ohd[:, u, :], node16[:, ds(t * P, P)], dstT[:, ds(k, 1)], None,
                                            ALU.is_equal).then_inc(s_oh, 1)

            @block.tensor
            def _(pe):
                pe.sem_inc(s_used, 4)
                pe.sem_inc(s_out, NB + 1)
                with pe.Fori(0, NT // 2) as half:
                    for side in range(2):
                        t = half * 2 + side
                        fours = pe.value_load(table[0:1, ds(t + NT, 1)], min_val=2, max_val=NCH)
                        before = pe.value_load(table[0:1, ds(t + 2 * NT, 1)], min_val=0, max_val=NT * NCH)

                        def four(i, opening):
                            for u in range(4):
                                pe.wait_ge(s_oh, (before + i) * 8 + u * 2 + 2)
                                for s in range(NT):
                                    b, q = divmod(s, PERBANK)
                                    first_ = opening and u == 0 and q == 0
                                    if first_ and b in [OWN[0]] + SHARED:
                                        pe.wait_ge(s_out, t * NB + 1 + (b in SHARED and 1 + SHARED.index(b)))
                                    m = pe.matmul(bank(b, side)[:, q * P:(q + 1) * P], ohs[:, u, s * P:(s + 1) * P],
                                                  ohd[:, u, :], start=first_, stop=True, skip_group_check=True)
                                m.then_inc(s_used, 1)

                        four(0, True)
                        with pe.Fori(1, fours) as i:
                            four(i, False)

        with Phase() as ph:
            s_w = ph.sem("w")
            block = ph.enter_context(nc.Block())

            @block.vector
            def _(v):
                v.scalar_tensor_tensor(widx[:, :], late[:, :], float(OOB), wcell[:, :], ALU.mult, ALU.add).then_inc(s_w, 1)
        edge.close()

        def skewed(eng, first, step, last, slots=2):
            SIX = 6
            assert (NT - 2) % SIX == 0 and SIX % slots == 0
            first(0, 0)
            with eng.Fori(0, (NT - 2) // SIX) as i:
                for k in range(1, SIX + 1):
                    step(i * SIX + k, i * SIX + k - 1, k % slots)
            step(NT - 1, NT - 2, (NT - 1) % slots)
            last(NT - 1, (NT - 1) % slots)

        def norm_memory(ph):
            return {**{n: ph.sb(n, [P, w * NT], f32) for n, w in (("st", 6), ("mv", 2), ("sd", 1), ("nmr", 1))},
                    **{n: ph.sem(n) for n in ("s_add", "s_bn", "s_mv", "s_sd", "s_rs")}}

        def norm_vector(v, m, residual=None):
            for t in range(NT):
                tile = XB[:, t * D:(t + 1) * D]
                if residual is not None:
                    v.tensor_tensor(tile, tile, residual[:, t * D:(t + 1) * D], ALU.add).then_inc(m["s_add"], 1)
                    if t:
                        v.wait_ge(m["s_add"], t)
                        v.bn_stats(m["st"][:, (t - 1) * 6:t * 6], XB[:, (t - 1) * D:t * D]).then_inc(m["s_bn"], 1)
                else:
                    v.bn_stats(m["st"][:, t * 6:t * 6 + 6], tile).then_inc(m["s_bn"], 1)
            if residual is not None:
                v.wait_ge(m["s_add"], NT)
                v.bn_stats(m["st"][:, (NT - 1) * 6:NT * 6], tile).then_inc(m["s_bn"], 1)
            v.wait_ge(m["s_bn"], NT)
            for t in range(NT):
                last = v.bn_aggr(m["mv"][:, 2 * t:2 * t + 2], m["st"][:, 6 * t:6 * t + 6])
            last.then_inc(m["s_mv"], 1)
            v.wait_ge(m["s_sd"], 1)
            v.reciprocal(m["sd"][:, :], m["sd"][:, :]).then_inc(m["s_rs"], 1)
            v.wait_ge(m["s_rs"], 1)
            mean = m["mv"][:, :].rearrange("p (t c) -> p t c", c=2)[:, :, 0]
            v.scalar_tensor_tensor(m["nmr"][:, :], mean, -1.0, m["sd"][:, :], ALU.mult, ALU.mult).then_inc(m["s_rs"], 1)

        def norm_scalar(a, m):
            a.wait_ge(m["s_mv"], 1)
            var = m["mv"][:, :].rearrange("p (t c) -> p t c", c=2)[:, :, 1]
            a.activation(m["sd"][:, :], var, ACT.Sqrt, bias=eps[:, 0:1]).then_inc(m["s_sd"], 1)
            a.wait_ge(m["s_rs"], 2)

        def attention(gat, nh, dh, split, norm, sgn, AB, scatter):
            K = D // P
            W2 = D + 2 * nh
            ABv = AB[:, 0:NT * 2 * nh].rearrange("p (t c) -> p t c", c=2 * nh)
            with Phase() as ph:
                Wx = ph.sb("Wx", [P, K, W2], f32)
                av = ph.sb("av", [P, 2, D], f32)
                prod = ph.sb("prod", [P, 2 * K, D], f32)
                xn = ph.sb("xn", [P, 2, D], f32)
                xT = ph.sb("xT", [P, 2, D], f32)
                blocks = [(b, min(P, NT * 2 * nh - b)) for b in range(0, NT * 2 * nh, P)]
                rT = ph.sb("rT", [P, len(blocks) * P], f32)
                m_ = norm_memory(ph) if norm else None
                psT = [ph.ps(f"psT{u}", [P, D]) for u in range(2)]
                psH = [ph.ps(f"psH{u}", [P, W2]) for u in range(2)]
                psR = ph.ps("psR", [P, len(blocks) * P])
                s_tR, s_rT, s_w, s_wx, s_xn, s_T, s_xT, s_M, s_out, s_v, s_rd = (
                    ph.sem(n) for n in ("tR", "rT", "w", "wx", "xn", "T", "xT", "M", "out", "v", "rd"))
                block = ph.enter_context(nc.Block())
                @block.sync
                def _(sp):
                    if split:
                        for h in range(nh):
                            sp.dma_start(Wx[:, :, h * dh:(h + 1) * dh],
                                         gat[0][h].rearrange("(k p) f -> p k f", p=P)).then_inc(s_w, 16)
                            for j in range(2):
                                sp.dma_start(av[:, 1 - j, h * dh:(h + 1) * dh],
                                             gat[1][h, :, j * dh:(j + 1) * dh].to_broadcast([P, dh])).then_inc(s_w, 16)
                    else:
                        sp.dma_start(Wx[:, :, 0:D], gat[0].rearrange("(k p) f -> p k f", p=P)).then_inc(s_w, 16)
                        for j in range(2):
                            sp.dma_start(av[:, j, :], gat[1 + j].rearrange("(a h) d -> a (h d)", a=1)
                                         .to_broadcast([P, D])).then_inc(s_w, 16)
                    sp.wait_ge(s_rT, len(blocks))
                    for n, (b, w) in enumerate(blocks):
                        sp.dma_start(rowd[b:b + w, :], rT[0:w, n * P:(n + 1) * P]).then_inc(s_rd, 16)
                    sp.wait_ge(s_rd, 16 * len(blocks))

                @block.vector
                def _(v):
                    ch = Chain(v, s_v)
                    if norm:
                        norm_vector(v, m_)
                    v.wait_ge(s_w, 16 * (3 * nh if split else 3))
                    for k in range(K):
                        for j in range(2):
                            ch(v.tensor_tensor(prod[:, 2 * k + j, :], Wx[:, k, 0:D], av[:, j, :], ALU.mult))
                    ch.wait()
                    for k in range(K):
                        for j in range(2):
                            last = v.tensor_reduce(Wx[:, k, D + j * nh:D + (j + 1) * nh],
                                                   prod[:, 2 * k + j, :].rearrange("p (h d) -> p h d", d=dh), AX.X,
                                                   ALU.add)
                    last.then_inc(s_wx, 1)
                    v.sem_inc(s_out, 6)
                    v.sem_inc(s_xT, 2)

                    def turned(t, u):
                        hold(v, s_T, t + 3)
                        hold(v, s_M, t + 1)
                        v.tensor_copy(xT[:, u, :], psT[u][:, :]).then_inc(s_xT, 1)

                    def result(t, u):
                        hold(v, s_M, t + 3)
                        v.tensor_copy(AB[:, ds(t * 2 * nh, 2 * nh)], psH[u][:, D:W2]).then_inc(s_out, 1)
                        v.tensor_copy(HB[:, ds(t * D, D)], psH[u][:, 0:D]).then_inc(s_out, 1)
                        v.tensor_reduce(hmax[:, ds(t, 1)], psH[u][:, 0:D], AX.X, ALU.max,
                                        apply_absolute_value=True).then_inc(s_out, 1)

                    def step(t, before, u):
                        turned(t, u)
                        result(before, 1 - u)
                    skewed(v, turned, step, result)
                    for n, (b, w) in enumerate(blocks):
                        v.wait_ge(s_tR, len(blocks))
                        v.tensor_scalar(rT[0:w, n * P:(n + 1) * P], psR[0:w, n * P:(n + 1) * P], BIG, None, ALU.mult
                                        ).then_inc(s_rT, 1)

                @block.scalar
                def _(a):
                    if norm:
                        norm_scalar(a, m_)
                    with a.Fori(0, NT // 2) as i:
                        for u in range(2):
                            t = i * 2 + u
                            hold(a, s_T, t + 1)
                            if norm:
                                a.activation(xn[:, u, :], XB[:, ds(t * D, D)], ACT.Relu, bias=m_["nmr"][:, ds(t, 1)],
                                             scale=m_["sd"][:, ds(t, 1)]).then_inc(s_xn, 1)
                            else:
                                a.activation(xn[:, u, :], HB[:, ds(t * D, D)], ACT.Copy).then_inc(s_xn, 1)

                @block.tensor
                def _(pe):
                    pe.sem_inc(s_T, 2)
                    pe.sem_inc(s_M, 2)
                    pe.wait_ge(s_wx, 1)

                    def turn(t, u):
                        hold(pe, s_xn, t + 1)
                        hold(pe, s_xT, t + 1)
                        for k in range(K):
                            m = pe.transpose(psT[u][:, k * P:(k + 1) * P], xn[:, u, k * P:(k + 1) * P], ident[:, :])
                        m.then_inc(s_T, 1)

                    def product(t, u):
                        hold(pe, s_xT, t + 3)
                        hold(pe, s_out, t * 3 + 3)
                        for k in range(K):
                            m = pe.matmul(psH[u][:, :], xT[:, u, k * P:(k + 1) * P], Wx[:, k, :], start=k == 0, stop=k == K - 1)
                        m.then_inc(s_M, 1)

                    def step(t, before, u):
                        turn(t, u)
                        product(before, 1 - u)
                    skewed(pe, turn, step, product)
                    pe.wait_ge(s_out, 3 * NT + 6)
                    for n, (b, w) in enumerate(blocks):
                        pe.transpose(psR[0:w, n * P:(n + 1) * P], AB[:, b:b + w], ident[:, :]).then_inc(s_tR, 1)

            cw = dh + 1
            S2 = nh * 2 * cw
            UV = Rh[:, 0:NT * 2 * S2].rearrange("p (t l c) -> p t l c", l=2, c=S2)
            VP = HB[:, :].bitcast(f16)[:, 0:NT * S2].rearrange("p (t l c) -> p t l c", l=2, c=S2 // 2)
            TH = NT * nh
            heads = Phase()
            with heads as hp:
                cB = hp.sb("cB", [P, TH], f32)
                cN = None if split else hp.sb("cN", [P, TH], f32)
                F1, F2 = hp.sb("F1", [P, TH], f32), hp.sb("F2", [P, TH], f32)
                TURNED = [t for t in range(NT) if not split or t % 5 in (1, 3)]
                VS = hp.sb("VS", [P, len(TURNED), 2, S2 // 2], f16) if split else None
                with Phase() as ph:
                    U, V = ph.sb("U", [P, TH], f32), ph.sb("V", [P, TH], f32)
                    XC, tt = ph.sb("XC", [P, TH], f32), ph.sb("tt", [P, TH], f32)
                    tt2 = ph.sb("tt2", [P, TH], f32)
                    top1, most = ph.sb("top1", [P, nh + 1], f32), ph.sb("most", [P, nh + 1], f32)
                    kap = ph.sb("kap", [P, 1], f32)
                    F = ph.sb("F", [P, 3, S2], f32)
                    s_vp, s_v, s_top, s_all, s_e, s_ex, s_fac, s_F, s_FV, s_hi, s_lo = (
                        ph.sem(n) for n in ("vp", "v", "top", "all", "e", "ex", "fac", "F", "FV", "hi", "lo"))
                    block = ph.enter_context(nc.Block())
                    th = lambda q: q[:, :].rearrange("p (t h) -> p t h", h=nh)
                    cv, rv = ABv[:, :, 0:nh], ABv[:, :, nh:2 * nh]

                    def side(eng, t, u, w, q, s_done):
                        Fv = F[:, u, :].rearrange("p (h w c) -> p h w c", w=2, c=cw)
                        Ht = HB[:, ds(t * D, D)].rearrange("p (h d) -> p h d", d=dh)
                        qt = q[:, ds(t * nh, nh)].unsqueeze(2)
                        hold(eng, s_lo, t + 1)
                        eng.tensor_tensor(Fv[:, :, w, 0:dh], Ht, qt.to_broadcast([P, nh, dh]), ALU.mult).then_inc(s_done, 1)
                        eng.tensor_copy(Fv[:, :, w, dh:cw], qt).then_inc(s_done, 1)

                    @block.gpsimd
                    def _(g):
                        g.wait_ge(s_top, 1)
                        g.partition_all_reduce(most[:, :], top1[:, :], P, bass.bass_isa.ReduceOp.max).then_inc(s_all, 1)
                        g.wait_ge(s_fac, 1)
                        v_side = lambda t, u: side(g, t, u, 1, V, s_FV)
                        skewed(g, v_side, lambda t, before, u: v_side(t, u), lambda t, u: None, slots=3)

                    @block.vector
                    def _(v):
                        ch = Chain(v, s_v)
                        ch(v.tensor_scalar(th(XC), cv, float(sgn), None, ALU.mult))
                        ch(v.tensor_scalar(th(cB), cv, BIG, None, ALU.mult))
                        if not split:
                            ch(v.tensor_scalar(th(cN), cv, -BIG, None, ALU.mult))
                        ch(v.tensor_reduce(top1[:, nh:nh + 1], hmax[:, :], AX.X, ALU.max))
                        ch.wait()
                        ch(v.tensor_scalar(XC[:, TH - nh:TH], XC[:, TH - nh:TH], padneg[:, 0:1], None, ALU.add))
                        ch.wait()
                        ch(v.tensor_reduce(top1[:, 0:nh], XC[:, :].rearrange("p (t h) -> p h t", h=nh), AX.X, ALU.max))
                        ch.wait()
                        v.sem_inc(s_top, 1)
                        v.wait_ge(s_all, 1)
                        A = most[:, 0:nh].unsqueeze(1).to_broadcast([P, NT, nh])
                        ch(v.tensor_tensor(th(XC), th(XC), A, ALU.subtract))
                        ch(v.tensor_tensor(th(tt), rv, A, ALU.add if sgn > 0 else ALU.subtract))
                        ch(v.tensor_scalar(kap[:, :], most[:, nh:nh + 1], 1.0, None, ALU.max))
                        ch.wait()
                        if sgn > 0:
                            ch(v.tensor_scalar(tt2[:, :], tt[:, :], -(1 - SLOPE), 0.0, ALU.mult, ALU.min))
                            ch.wait()
                            ch(v.tensor_scalar(tt[:, :], tt[:, :], 1 - SLOPE, 0.0, ALU.mult, ALU.min))
                        else:
                            ch(v.tensor_scalar(tt2[:, :], tt[:, :], 1 - SLOPE, 0.0, ALU.mult, ALU.max))
                            ch.wait()
                            ch(v.tensor_scalar(tt[:, :], tt[:, :], -(1 - SLOPE), 0.0, ALU.mult, ALU.max))
                            ch.wait()
                            ch(v.tensor_scalar(tt2[:, :], tt2[:, :], 80.0, None, ALU.min))
                            ch(v.tensor_scalar(tt[:, :], tt[:, :], 80.0, None, ALU.min))
                        ch(v.reciprocal(kap[:, :], kap[:, :]))
                        ch.wait()
                        v.tensor_scalar(kap[:, :], kap[:, :], TOP * LO, None, ALU.mult).then_inc(s_e, 1)
                        v.wait_ge(s_ex, 4)
                        ch(v.tensor_scalar(U[:, :], U[:, :], kap[:, 0:1], None, ALU.mult))
                        ch(v.tensor_scalar(V[:, :], V[:, :], kap[:, 0:1], 1.0 if split else -1.0, ALU.mult, ALU.mult))
                        ch.wait()
                        if split:
                            turned = V[:, :].rearrange("p (a b h) -> p a b h", b=5, h=nh)[:, :, 1:4:2, :]
                            ch(v.tensor_scalar(turned, turned, -1.0, None, ALU.mult))
                            ch.wait()
                        v.sem_inc(s_lo, 3)
                        v.sem_inc(s_fac, 1)

                        def low(t, u):
                            hold(v, s_hi, t + 1)
                            v.scalar_tensor_tensor(UV[:, ds(t, 1), 1, :], UV[:, ds(t, 1), 0, :], -LO,
                                                   F[:, u, :].unsqueeze(1), ALU.mult, ALU.add).then_inc(s_lo, 1)

                        def step(t, before, u):
                            side(v, t, u, 0, U, s_F)
                            low(before, (u - 1) % 3)
                        skewed(v, lambda t, u: side(v, t, u, 0, U, s_F), step, low, slots=3)

                    @block.scalar
                    def _(a):
                        a.wait_ge(s_e, 1)
                        a.activation(U[:, :], XC[:, :], ACT.Exp).then_inc(s_ex, 1)
                        a.activation(V[:, :], XC[:, :], ACT.Exp, scale=SLOPE).then_inc(s_ex, 1)
                        a.activation(F1[:, :], tt[:, :], ACT.Exp).then_inc(s_ex, 1)
                        a.activation(F2[:, :], tt2[:, :], ACT.Exp).then_inc(s_ex, 1)

                        def high(t, u):
                            hold(a, s_F, t * 2 + 2)
                            hold(a, s_FV, t * 2 + 2)
                            a.activation(UV[:, ds(t, 1), 0, :], F[:, u, :].unsqueeze(1), ACT.Copy,
                                         scale=1 / LO).then_inc(s_hi, 1)

                        def plain(t, u):
                            if not split:
                                hold(a, s_lo, t + 4)
                                uv = Rh[:, ds(t * 2 * S2, 2 * S2)].rearrange("p (l h w c) -> p l h w c", l=2, w=2, c=cw)
                                vp = HB[:, :].bitcast(f16)[:, ds(t * S2, S2)].rearrange("p (l h c) -> p l h c", l=2, c=cw)
                                a.activation(vp, uv[:, :, :, 1], ACT.Copy, scale=-1.0).then_inc(s_vp, 1)

                        def step(t, before, u):
                            high(t, u)
                            plain(before, (u - 1) % 3)
                        skewed(a, high, step, plain, slots=3)
                        if split:
                            a.wait_ge(s_lo, NT + 3)
                            uv = UV.rearrange("p t l (h w c) -> p t l h w c", w=2, c=cw)
                            for n, t in enumerate(TURNED):
                                a.activation(VS[:, n].rearrange("p l (h c) -> p l h c", c=cw), uv[:, t, :, :, 1], ACT.Copy,
                                             scale=-1.0).then_inc(s_vp, 1)

                PARTS = 4 if split else 2
                TP = NT // PARTS
                W = TP * P
                RG = 10
                NB = (RG + 2) // 3
                SG = 5 if split else 4
                LEAD = 7 if split else 4
                on_act = [[s for s in range(NT) if split or s % SG < SG - 1 or (p, s) in MORE_ON_ACT] for p in range(PARTS)]
                compared = lambda h, p, s: (h * sum(map(len, on_act)) + sum(map(len, on_act[:p])) +
                                            sum(q < s for q in on_act[p]))
                assert RG == TP * (2 if split else 1)
                with Phase() as ph:
                    rows = ph.sb("rows", [P, 2, W], f32)
                    Rm = ph.sb("Rm", [P, SG, W], bf16)
                    M = ph.sb("M", [P, SG, W], f16)
                    Mn = ph.sb("Mn", [P, SG, W], f16) if split else None
                    tl = ph.sb("tl", [P, RG, cw if split else 2 * cw], f32)
                    stash = None if split else ph.sb("stash", [P, TP, dh], f32)
                    q1 = ph.sb("q1", [P, TP, cw], f32)
                    rec = ph.sb("rec", [P, TP], f32)
                    if scatter:
                        wi, wv = ([ph.sb(f"{n}{w}", [P, 1], dt) for w in range(2)] for n, dt in (("wi", i32), ("wv", f32)))
                    XW = cw if split else 2 * cw
                    ps = [[ph.ps(f"ps{b}{j}", [P, 3 * 2 * XW]) for j in range(NB)] for b in range(2)]
                    s_row = [ph.sem(f"row{b}") for b in range(2)]
                    s_R, s_M, s_Mn, s_cut, s_P, s_E, s_tl, s_v, s_wc, s_wd = (
                        ph.sem(n) for n in ("R", "M", "Mn", "cut", "P", "E", "tl", "v", "wc", "wd"))
                    block = ph.enter_context(nc.Block())

                    def region(b, r, l0=0, l1=2):
                        return ps[b][r // 3][:, (r % 3) * 2 * XW + l0 * XW:(r % 3) * 2 * XW + l1 * XW]

                    def banks(b, l):
                        for j in range(NB):
                            n = min(3, RG - 3 * j)
                            yield 3 * j, n, ps[b][j][:, 0:n * 2 * XW].rearrange("p (r l c) -> p r l c", l=2, c=XW)[:, :, l, :]

                    ONE = TURNED
                    TWO = [s for s in range(NT) if s not in ONE]

                    def cut(eng, q, s, wait):
                        if s < 0:
                            q, s = q - 1, s + NT
                        steps, sem = (ONE, s_M) if s in ONE else (TWO, s_Mn)
                        wait(eng, sem, (q + 2) * len(steps) + steps.index(s) + 1)

                    row_terms = rowd[0:NT * 2 * nh, :].rearrange("(t c) j -> c t j", c=2 * nh)

                    @block.sync
                    def _(sp):
                        with sp.Fori(0, nh) as h:
                            for p in range(PARTS):
                                if TWO:
                                    hold(sp, s_Mn, (h * PARTS + p + 1) * len(TWO))
                                sp.wait_ge(s_M, (h * PARTS + p + 1) * len(ONE))
                                sp.dma_start(rows[:, p % 2, :].rearrange("p (t j) -> p t j", j=P),
                                             row_terms[ds(h + nh, 1), p * TP:(p + 1) * TP, :].to_broadcast([P, TP, P])
                                             ).then_inc(s_row[p % 2], 16)

                    def landed(eng, h, p):
                        hold(eng, s_row[p % 2], (h * (PARTS // 2) + p // 2 + 1) * 16)

                    def parts_in_order(eng, steps, rest):
                        def body(h, opening):
                            for p in range(PARTS):
                                landed(eng, h, p)
                                steps(h, p, 0, LEAD)
                                before = (h, p - 1) if p else None if opening else (h - 1, PARTS - 1)
                                rest(h, p, before)

                        body(0, True)
                        return body

                    @block.scalar
                    def _(a):
                        def steps(h, p, s0, s1):
                            for s in range(s0, s1):
                                if s in on_act[p]:
                                    cut(a, h * PARTS + p, s - SG, hold)
                                    a.activation(Rm[:, s % SG, :], rows[:, p % 2, :], ACT.Relu,
                                                 bias=cB[:, ds(h + s * nh, 1)]).then_inc(s_R, 1)

                        def evacuate(h, p):
                            q = h * PARTS + p
                            hold(a, s_P, (q + 1) * NT + SG)
                            hold(a, s_E, q + 2)
                            for r, n, part in banks(p % 2, 1):
                                ins = a.activation(tl[:, r:r + n, :], part, ACT.Copy, scale=1 / LO)
                            ins.then_inc(s_tl, 1)

                        def rest(h, p, before):
                            if before:
                                evacuate(*before)
                            steps(h, p, LEAD, NT)

                        body = parts_in_order(a, steps, rest)
                        with a.Fori(1, nh) as h:
                            body(h, False)
                        evacuate(nh - 1, PARTS - 1)

                    @block.vector
                    def _(v):
                        v.sem_inc(s_M, 2 * len(ONE))
                        if TWO:
                            v.sem_inc(s_Mn, 2 * len(TWO))
                        v.sem_inc(s_E, 2)
                        ch = Chain(v, s_v)

                        def low_part(h, p, s):
                            u = s % SG
                            v.wait_ge(s_cut, (h * PARTS + p) * len(TWO) + TWO.index(s) + 1)
                            Cs = C[:, s * NP + p * W:s * NP + (p + 1) * W]
                            v.tensor_tensor(Mn[:, u, :], Cs, M[:, u, :], ALU.subtract).then_inc(s_Mn, 1)

                        def steps(h, p, s0, s1, between=()):
                            between = list(between)
                            for s in range(s0, s1):
                                g, u = (h * PARTS + p) * NT + s, s % SG
                                Cs = C[:, s * NP + p * W:s * NP + (p + 1) * W]
                                if s in on_act[p]:
                                    v.wait_ge(s_R, compared(h, p, s) + 1)
                                    v.wait_ge(s_P, g + 1)
                                    v.tensor_tensor(M[:, u, :], Rm[:, u, :], Cs, ALU.min).then_inc(s_M if s in ONE else s_cut, 1)
                                else:
                                    v.wait_ge(s_P, g + 1)
                                    v.scalar_tensor_tensor(M[:, u, :], rows[:, p % 2, :], cN[:, ds(h + s * nh, 1)], Cs,
                                                           ALU.is_gt, ALU.mult).then_inc(s_M, 1)
                                if s - 1 in TWO:
                                    low_part(h, p, s - 1)
                                if between:
                                    between.pop(0)()
                            if s1 == NT and s in TWO:
                                low_part(h, p, s)
                            assert not between

                        def evacuation(h, p):
                            q = h * PARTS + p
                            factor = lambda Fq: Fq[:, :].rearrange("p (t h) -> p t h", h=nh)[
                                :, p * TP:(p + 1) * TP, ds(h, 1)].to_broadcast([P, TP, cw])
                            xu, xv = (tl[:, 0:TP, :], tl[:, TP:2 * TP, :]) if split else (tl[:, :, 0:cw], tl[:, :, cw:2 * cw])
                            room = HB[:, 0:NT * nh * cw] if split else R[:, :]
                            room = room.rearrange("p (t c) -> p t c", t=NT)
                            held = not split and p == 0
                            o = stash[:, :, :] if held else room[:, p * TP:(p + 1) * TP, ds(h * cw, dh)]

                            def add():
                                hold(v, s_tl, q + 1)
                                for r, n, part in banks(p % 2, 0):
                                    ch(v.tensor_tensor(tl[:, r:r + n, :], part, tl[:, r:r + n, :], ALU.add))

                            def scale():
                                ch.wait()
                                ch(v.tensor_tensor(xv, xv, factor(F2), ALU.mult))
                                ch(v.tensor_tensor(q1[:, :, :], xu, factor(F1), ALU.mult))

                            def both():
                                ch.wait()
                                v.tensor_tensor(q1[:, :, :], q1[:, :, :], xv, ALU.add).then_inc(s_E, 1)

                            def weight():
                                hold(v, s_E, q + 3)
                                ch(v.tensor_scalar(rec[:, :], q1[:, :, dh], 1e-30, None, ALU.max))

                            def inverse():
                                ch.wait()
                                ch(v.reciprocal(rec[:, :], rec[:, :]))

                            def mean():
                                ch.wait()
                                ch(v.tensor_tensor(o, q1[:, :, 0:dh], rec[:, :].unsqueeze(2).to_broadcast([P, TP, dh]),
                                                   ALU.mult))

                            def unstash():
                                ch.wait()
                                ch(v.tensor_copy(room[:, 0:TP, ds(h * cw, dh)], stash[:, :, :]))

                            stages = [add, scale, both, weight, inverse, mean]
                            return stages, [unstash] if not split and p == 1 else []

                        def rest(h, p, before):
                            stages, last = evacuation(*before) if before else ([], [])
                            steps(h, p, LEAD, NT, stages + last)

                        body = parts_in_order(v, steps, rest)
                        with v.Fori(1, nh) as h:
                            ch.begin(h - 1, PARTS * (NB + 5) + (0 if split else 1))
                            body(h, False)
                            ch.end(nh - 1)
                        stages, last = evacuation(nh - 1, PARTS - 1)
                        for stage in stages + last:
                            stage()

                    @block.tensor
                    def _(pe):
                        pe.sem_inc(s_P, SG)

                        with pe.Fori(0, nh) as h:
                            for p in range(PARTS):
                                q = h * PARTS + p
                                hold(pe, s_E, q + 1)
                                for s in range(NT):
                                    cut(pe, q, s, lambda eng, sem, value: eng.wait_ge(sem, value))
                                    for r in range(RG):
                                        first = s == 0 and r % 3 == 0
                                        side = r // TP if split else 0
                                        lhsT = (Mn if side and s in TWO else M)[:, s % SG, (r % TP) * P:(r % TP + 1) * P]
                                        rhs = UV[:, s, :, ds(h * (2 * cw) + side * cw, XW)]
                                        m = pe.matmul(region(p % 2, r), lhsT, rhs, start=first, stop=True,
                                                      skip_group_check=True)
                                        if split and side and s in TURNED:
                                            m = pe.matmul(region(p % 2, r), C[:, s * NP + p * W + (r % TP) * P:][:, 0:P],
                                                          VS[:, TURNED.index(s), :, ds(h * cw, cw)], start=False, stop=True,
                                                          skip_group_check=True)
                                        if not split:
                                            both = region(p % 2, r).rearrange("p (l c) -> p l c", l=2)
                                            m = pe.matmul(both[:, :, cw:2 * cw], C[:, s * NP + p * W + r * P:][:, 0:P],
                                                          VP[:, s, :, ds(h * cw, cw)], start=False, stop=True,
                                                          skip_group_check=True)
                                    m.then_inc(s_P, 1)

                    if scatter:
                        @block.gpsimd
                        def _(g):
                            lo = g.value_load(table[0:1, 3 * NT:3 * NT + 1], min_val=0, max_val=NCH - 1)
                            n = g.value_load(table[0:1, 3 * NT + 1:3 * NT + 2], min_val=1, max_val=(NCH + 3) // 4)

                            def write(i, w, c, opening):
                                g.tensor_copy(wi[w][:, :], widx[:, ds(c, 1)]).then_inc(s_wc, 1)
                                g.tensor_copy(wv[w][:, :], ewT[:, ds(c, 1)]).then_inc(s_wc, 1)
                                if not opening:
                                    hold(g, s_wd, i * 16)
                                hold(g, s_wc, i * 2 + 2)
                                g.indirect_dma_start(out=wd[:, :], out_offset=bass.IndirectOffsetOnAxis(ap=wi[w][:, :], axis=0),
                                                     in_=wv[w][:, :], in_offset=None, bounds_check=D * D - 1,
                                                     oob_is_err=False).then_inc(s_wd, 16)

                            write(0, 0, lo, True)
                            write(1, 1, chunk(lo + 1, NG * P - 1), False)
                            with g.Fori(1, n * 2) as i:
                                for w in range(2):
                                    write(i * 2 + w, w, chunk(lo + i * 2 + w, NG * P - 1), False)
                            hold(g, s_wd, n * 64)

        def elu(source, dest, bias_dram, nh, twice, around=None, residual=None):
            cw = D // nh + 1
            TB = 4
            BW = TB * D
            NBAT = NT // TB
            with Phase() as ph:
                bias = ph.sb("bias", [P, D], f32)
                e = ph.sb("e", [P, 2, BW], f32)
                s_b, s_v, s_in, s_e, s_ee, s_o = (ph.sem(n) for n in ("b", "v", "in", "e", "ee", "o"))
                block = ph.enter_context(nc.Block())
                rounds = 2 if twice else 1
                y = lambda i: dest[:, i * BW:(i + 1) * BW]
                order = [(i, w) for j in range(0, NBAT + 1, 2) for w in range(rounds) for i in range(j, min(j + 2, NBAT))]

                @block.sync
                def _(sp):
                    if bias_dram is not None:
                        sp.dma_start(bias[:, :], bias_dram.rearrange("(a f) -> a f", a=1).to_broadcast([P, D])).then_inc(s_b, 16)

                if around:
                    around(ph, block, s_in, lambda i: (s_o, order.index((i, rounds - 1)) + 1))

                @block.vector
                def _(v):
                    if bias_dram is not None:
                        v.wait_ge(s_b, 16)

                    def heads_of(i):
                        room = source.rearrange("p (t c) -> p t c", t=NT)[:, i * TB:(i + 1) * TB, 0:nh * cw]
                        return room.rearrange("p t (h c) -> p t h c", c=cw)[:, :, :, 0:cw - 1]

                    apart = lambda q: q.rearrange("p (t h c) -> p t h c", c=cw - 1, h=nh)

                    def take(n):
                        i, w = order[n]
                        if n >= 2:
                            v.wait_ge(s_o, n - 1)
                        if w == 0 and bias_dram is None:
                            for j in range(TB):
                                ins = v.tensor_scalar(apart(e[:, n % 2, :])[:, j], heads_of(i)[:, j], 0.0, None, ALU.min)
                            ins.then_inc(s_e, 1)
                            return
                        if w == 0:
                            for j in range(TB):
                                v.tensor_tensor(apart(y(i))[:, j], heads_of(i)[:, j],
                                                bias[:, :].rearrange("p (h c) -> p h c", c=cw - 1), ALU.add).then_inc(s_in, 1)
                            v.wait_ge(s_in, (i + 1) * TB)
                        else:
                            v.wait_ge(s_o, order.index((i, 0)) + 1)
                        v.tensor_scalar(e[:, n % 2, :], y(i), 0.0, None, ALU.min).then_inc(s_e, 1)

                    def finish(n):
                        i, w = order[n]
                        v.wait_ge(s_e, n + 1)
                        more = residual is not None and w == rounds - 1
                        if more:
                            v.wait_ge(residual[1], 16)
                            v.scalar_tensor_tensor(y(i), y(i), 0.0, residual[0][:, i * BW:(i + 1) * BW], ALU.max,
                                                   ALU.add).then_inc(s_v, 1)
                        elif w == 0 and bias_dram is None:
                            for j in range(TB):
                                ins = v.tensor_scalar(apart(y(i))[:, j], heads_of(i)[:, j], 0.0, -1.0, ALU.max, ALU.add)
                            ins.then_inc(s_v, 1)
                        else:
                            v.tensor_scalar(y(i), y(i), 0.0, -1.0, ALU.max, ALU.add).then_inc(s_v, 1)
                        v.wait_ge(s_ee, n + 1)
                        v.wait_ge(s_v, n + 1)
                        if more:
                            v.scalar_tensor_tensor(y(i), e[:, n % 2, :], -1.0, y(i), ALU.add, ALU.add).then_inc(s_o, 1)
                        else:
                            v.tensor_tensor(y(i), y(i), e[:, n % 2, :], ALU.add).then_inc(s_o, 1)

                    for n in range(len(order) + 1):
                        late_take = n < len(order) and n and order[n][0] == order[n - 1][0]
                        if n < len(order) and not late_take:
                            take(n)
                        if n:
                            finish(n - 1)
                        if late_take:
                            take(n)

                @block.scalar
                def _(a):
                    for n in range(len(order)):
                        a.wait_ge(s_e, n + 1)
                        a.activation(e[:, n % 2, :], e[:, n % 2, :], ACT.Exp).then_inc(s_ee, 1)

        def load_residual(ph, block, read, done):
            s_z, s_in = ph.sem("z"), ph.sem("rows")

            @block.gpsimd
            def _(g):
                g.wait_ge(read, 12)
                g.memset(XB[:, (NT - 1) * D:NT * D], 0.0).then_inc(s_z, 1)
                g.wait_ge(s_z, 1)
                rows_in(g, XB, x, s_in)
                g.wait_ge(s_in, 32)

        attention(gat0[0:3], 8, 32, False, True, 1, AB, True)
        elu(R[:, :], HB, gat0[3], 8, False)
        attention(gat1[0:3], 8, 32, False, False, 1, AB, False)
        elu(R[:, :], HB, gat1[3], 8, False, load_residual)
        late_.close()
        K = D // P

        with Phase() as ph:
            Wl = ph.sb("Wl", [P, K, D], f32)
            xn, xT = ph.sb("xn", [P, 2, D], f32), ph.sb("xT", [P, 2, D], f32)
            m_ = norm_memory(ph)
            psT = [ph.ps(f"psT{u}", [P, D]) for u in range(2)]
            psH = [ph.ps(f"psH{u}", [P, D]) for u in range(2)]
            s_w, s_xn, s_T, s_xT, s_M, s_out = (ph.sem(n) for n in ("w", "xn", "T", "xT", "M", "out"))
            block = ph.enter_context(nc.Block())

            @block.sync
            def _(sp):
                sp.dma_start(Wl[:, :, :], wd.rearrange("(k p c) a -> p k (c a)", p=P, c=D)).then_inc(s_w, 16)

            @block.vector
            def _(v):
                norm_vector(v, m_, residual=HB)
                v.sem_inc(s_out, 2)
                v.sem_inc(s_xT, 2)

                def turned(t, u):
                    hold(v, s_T, t + 3)
                    hold(v, s_M, t + 1)
                    v.tensor_copy(xT[:, u, :], psT[u][:, :]).then_inc(s_xT, 1)

                def result(t, u):
                    hold(v, s_M, t + 3)
                    v.tensor_tensor(XB[:, ds(t * D, D)], XB[:, ds(t * D, D)], psH[u][:, :], ALU.add).then_inc(s_out, 1)

                def step(t, before, u):
                    turned(t, u)
                    result(before, 1 - u)
                skewed(v, turned, step, result)

            @block.scalar
            def _(a):
                norm_scalar(a, m_)
                with a.Fori(0, NT // 2) as i:
                    for u in range(2):
                        t = i * 2 + u
                        hold(a, s_T, t + 1)
                        a.activation(xn[:, u, :], XB[:, ds(t * D, D)], ACT.Relu, bias=m_["nmr"][:, ds(t, 1)],
                                     scale=m_["sd"][:, ds(t, 1)]).then_inc(s_xn, 1)

            @block.tensor
            def _(pe):
                pe.sem_inc(s_T, 2)
                pe.sem_inc(s_M, 2)
                pe.wait_ge(s_w, 16)

                def turn(t, u):
                    hold(pe, s_xn, t + 1)
                    hold(pe, s_xT, t + 1)
                    for k in range(K):
                        m = pe.transpose(psT[u][:, k * P:(k + 1) * P], xn[:, u, k * P:(k + 1) * P], ident[:, :])
                    m.then_inc(s_T, 1)

                def product(t, u):
                    hold(pe, s_xT, t + 3)
                    hold(pe, s_out, t + 1)
                    for k in range(K):
                        m = pe.matmul(psH[u][:, :], xT[:, u, k * P:(k + 1) * P], Wl[:, k, :], start=k == 0, stop=k == K - 1)
                    m.then_inc(s_M, 1)

                def step(t, before, u):
                    turn(t, u)
                    product(before, 1 - u)
                skewed(pe, turn, step, product)

        wn0, wr0, b0, wn1, wr1, b1, wn2, wr2, b2 = sage
        dw0, db0, dw1, db1, dw2, db2 = dec
        DL = (2 * D, D, P)
        SP = R[:, NT * D:2 * NT * D].bitcast(f16)
        sg = Phase()
        sg.__enter__()
        scale_ = sg.sb("scale", [P, 1], f32)
        rdk = sg.sb("rdk", [P, NT], f32)

        def parts(w, source, scaled):
            SPv = SP[:, 0:NT * 2 * w].rearrange("p (t l c) -> p t l c", l=2, c=w)
            with Phase() as ph:
                PU = 4
                L = ph.sb("L", [P, PU, w], f32)
                lsc = ph.sb("lsc", [P, 1], f32)
                mx, mxa = ph.sb("mx", [P, 1], f32), ph.sb("mxa", [P, 1], f32)
                s_v, s_m, s_a, s_s, s_h, s_L, s_lo = (ph.sem(n) for n in ("v", "m", "a", "s", "h", "L", "lo"))
                block = ph.enter_context(nc.Block())

                if scaled:
                    @block.gpsimd
                    def _(g):
                        g.wait_ge(s_m, 1)
                        g.partition_all_reduce(mxa[:, :], mx[:, :], P, bass.bass_isa.ReduceOp.max).then_inc(s_a, 1)

                @block.vector
                def _(v):
                    ch = Chain(v, s_v)
                    if scaled:
                        v.tensor_reduce(mx[:, :], hmax[:, :], AX.X, ALU.max).then_inc(s_m, 1)
                        v.wait_ge(s_a, 1)
                        ch(v.tensor_scalar(mxa[:, :], mxa[:, :], 1e-20, None, ALU.max))
                        ch.wait()
                        ch(v.reciprocal(mx[:, :], mxa[:, :]))
                        ch(v.tensor_scalar(rdk[:, :], rdeg[:, :], mxa[:, 0:1], 1 / TOP, ALU.mult, ALU.mult))
                        ch.wait()
                        ch(v.tensor_scalar(scale_[:, :], mx[:, :], TOP, None, ALU.mult))
                    else:
                        ch(v.memset(scale_[:, :], TOP / 16))
                    ch.wait()
                    ch(v.tensor_scalar(lsc[:, :], scale_[:, :], LO, None, ALU.mult))
                    ch.wait()
                    v.sem_inc(s_s, 1)
                    v.sem_inc(s_lo, 1)
                    with v.Fori(0, NT // PU) as i:
                        for u in range(PU):
                            t = i * PU + u
                            hold(v, s_lo, i * PU + 1)
                            v.tensor_scalar(L[:, u, :], source[:, ds(t * w, w)], lsc[:, 0:1], None, ALU.mult).then_inc(s_L, 1)
                        hold(v, s_L, i * PU + PU)
                        for u in range(PU):
                            t = i * PU + u
                            hold(v, s_h, t + 1)
                            v.scalar_tensor_tensor(SPv[:, ds(t, 1), 1, :], SPv[:, ds(t, 1), 0, :], -LO,
                                                   L[:, u, :].unsqueeze(1), ALU.mult, ALU.add).then_inc(s_lo, 1)

                @block.scalar
                def _(a):
                    a.wait_ge(s_s, 1)
                    with a.Fori(0, NT // PU) as i:
                        for u in range(PU):
                            t = i * PU + u
                            a.activation(SPv[:, ds(t, 1), 0, :], source[:, ds(t * w, w)].unsqueeze(1), ACT.Copy,
                                         scale=scale_[:, 0:1]).then_inc(s_h, 1)
            return SPv

        def neighbours(pe, psA, SPv, t, s0, s1, psD=None, ones=None):
            for s in range(s0, s1):
                lhsT = C[:, ds(t * P + s * NP, P)]
                m = pe.matmul(psA[:, :], lhsT, SPv[:, s, :, :].rearrange("p l c -> p (l c)"), start=s == 0, stop=s == NT - 1)
                if psD is not None:
                    m = pe.matmul(psD, lhsT, ones, start=s == 0, stop=s == NT - 1)
            return m

        with Phase() as ph:
            m_ = norm_memory(ph)
            s_x, s_n = ph.sem("x"), ph.sem("n")
            block = ph.enter_context(nc.Block())

            @block.sync
            def _(sp):
                sp.dma_start(xd[:, :], XB).then_inc(s_x, 16)
                sp.wait_ge(s_x, 16)

            @block.vector
            def _(v):
                norm_vector(v, m_)

            @block.scalar
            def _(a):
                norm_scalar(a, m_)
                for t in range(NT):
                    a.activation(HB[:, t * D:(t + 1) * D], XB[:, t * D:(t + 1) * D], ACT.Relu, bias=m_["nmr"][:, t:t + 1],
                                 scale=m_["sd"][:, t:t + 1]).then_inc(s_n, 1)

        SPv = parts(D, HB, False)
        H0, H1 = DL[0], DL[1]
        F0 = H0 // P
        with Phase() as ph:
            W0 = ph.sb("W0", [P, 2 * K, H0], f32)
            W1 = ph.sb("W1", [P, F0, 2 * H1], f32)
            b0c = ph.sb("b0c", [P, F0], f32)
            b1r = ph.sb("b1r", [P, H1], f32)
            ones = ph.sb("ones", [P, 1], f16)
            tl = ph.sb("tl", [P, 2, D], f32)
            xs = ph.sb("xs", [P, 2, 2 * D], f32)
            xT = ph.sb("xT", [P, 2, 4 * P], f32)
            hT = ph.sb("hT", [P, 2, F0 * P], f32)
            psA = [ph.ps(f"psA{u}", [P, 2 * D]) for u in range(2)]
            psD = [ph.ps(f"psD{u}", [P, 1]) for u in range(2)]
            psT = ph.ps("psT", [P, 4 * P])
            ps1 = ph.ps("ps1", [P, F0 * P])
            psO = ph.ps("psO", [P, 2 * H1])
            s_c, s_w, s_A, s_tl, s_own, s_mean, s_T, s_xT, s_1, s_hT, s_O, s_out, s_v = (
                ph.sem(n) for n in ("c", "w", "A", "tl", "own", "mean", "T", "xT", "1", "hT", "O", "out", "v"))
            block = ph.enter_context(nc.Block())

            @block.gpsimd
            def _(g):
                g.memset(ones[:, :], 1.0).then_inc(s_c, 1)

            @block.sync
            def _(sp):
                for j, w in enumerate((wn0, wr0)):
                    sp.dma_start(W0[:, j * K:(j + 1) * K, :], w.rearrange("(k p) f -> p k f", p=P)).then_inc(s_w, 16)
                for j, w in enumerate((wn1, wr1)):
                    sp.dma_start(W1[:, :, j * H1:(j + 1) * H1], w.rearrange("(k p) f -> p k f", p=P)).then_inc(s_w, 16)
                with nc.allow_non_contiguous_dma("a bias of 512 elements, one to a partition"):
                    sp.dma_start(b0c[:, :], b0.rearrange("(f p) -> p f", p=P)).then_inc(s_w, 16)
                sp.dma_start(b1r[:, :], b1.rearrange("(a f) -> a f", a=1).to_broadcast([P, H1])).then_inc(s_w, 16)

            @block.tensor
            def _(pe):
                pe.sem_inc(s_xT, 2)
                pe.sem_inc(s_hT, 1)
                pe.wait_ge(s_c, 1)

                def total(t, u, s0=0, s1=NT):
                    if s0 == 0:
                        hold(pe, s_mean, t + 1)
                    m = neighbours(pe, psA[u], SPv, t, s0, s1, psD[u][:, :], ones[:, :])
                    if s1 == NT:
                        m.then_inc(s_A, 1)

                def turn(t, u):
                    hold(pe, s_mean, t + 3)
                    hold(pe, s_own, t + 1)
                    hold(pe, s_xT, t + 2)
                    for k in range(4):
                        m = pe.transpose(psT[:, k * P:(k + 1) * P], xs[:, u, k * P:(k + 1) * P], ident[:, :])
                    m.then_inc(s_T, 1)

                def wide(t, u):
                    hold(pe, s_xT, t + 3)
                    hold(pe, s_hT, t + 1)
                    for f in range(F0):
                        for k in range(4):
                            m = pe.matmul(ps1[:, f * P:(f + 1) * P], W0[:, k, f * P:(f + 1) * P],
                                          xT[:, u, k * P:(k + 1) * P], start=k == 0, stop=k == 3)
                    m.then_inc(s_1, 1)

                def both(t, u):
                    hold(pe, s_hT, t + 2)
                    hold(pe, s_out, t * 3 + 3)
                    for k in range(F0):
                        m = pe.matmul(psO[:, :], hT[:, u, k * P:(k + 1) * P], W1[:, k, :], start=k == 0, stop=k == F0 - 1)
                    m.then_inc(s_O, 1)

                def first(t, u):
                    total(t, u)
                    pe.wait_ge(s_w, 16 * 6)

                def step(t, before, u):
                    total(t, u, 0, 7)
                    turn(before, 1 - u)
                    total(t, u, 7, 12)
                    wide(before, 1 - u)
                    total(t, u, 12, NT)
                    both(before, 1 - u)

                def last(t, u):
                    turn(t, u)
                    wide(t, u)
                    both(t, u)
                skewed(pe, first, step, last)

            @block.scalar
            def _(a):
                a.sem_inc(s_T, 2)
                a.sem_inc(s_O, 2)

                def own(t, u):
                    hold(a, s_T, t + 1)
                    a.activation(xs[:, u, D:2 * D], HB[:, ds(t * D, D)], ACT.Copy).then_inc(s_own, 1)

                def low(t, u):
                    hold(a, s_mean, t + 1)
                    hold(a, s_A, t + 1)
                    a.activation(tl[:, u, :], psA[u][:, D:2 * D], ACT.Copy, scale=1 / LO).then_inc(s_tl, 1)

                def copies(t, u):
                    hold(a, s_T, t + 3)
                    a.activation(xT[:, u, :], psT[:, :], ACT.Copy).then_inc(s_xT, 1)
                    hold(a, s_1, t + 1)
                    hold(a, s_O, t + 1)
                    for f in range(F0):
                        ins = a.activation(hT[:, u, f * P:(f + 1) * P], ps1[:, f * P:(f + 1) * P], ACT.Relu, bias=b0c[:, f:f + 1])
                    ins.then_inc(s_hT, 1)

                def first(t, u):
                    own(t, u)
                    low(t, u)
                    a.wait_ge(s_w, 16 * 6)

                def step(t, before, u):
                    own(t, u)
                    copies(before, 1 - u)
                    low(t, u)
                skewed(a, first, step, copies)

            @block.vector
            def _(v):
                v.sem_inc(s_mean, 2)
                v.sem_inc(s_out, 3)

                def mean(t, u):
                    hold(v, s_tl, t + 1)
                    hold(v, s_xT, t + 1)
                    v.tensor_scalar(rdeg[:, ds(t, 1)], psD[u][:, :], 1.0, None, ALU.max).then_inc(s_v, 1)
                    v.tensor_tensor(xs[:, u, 0:D], psA[u][:, 0:D], tl[:, u, :], ALU.add).then_inc(s_v, 1)
                    hold(v, s_v, t * 4 + 2)
                    v.reciprocal(rdeg[:, ds(t, 1)], rdeg[:, ds(t, 1)]).then_inc(s_v, 1)
                    hold(v, s_v, t * 4 + 3)
                    v.tensor_scalar(xs[:, u, 0:D], xs[:, u, 0:D], rdeg[:, ds(t, 1)], 16 / TOP, ALU.mult, ALU.mult).then_inc(s_mean, 1)
                    v.sem_inc(s_v, 1)

                def results(t, u):
                    hold(v, s_O, t + 3)
                    v.tensor_copy(XB[:, ds(t * H1, H1)], psO[:, 0:H1]).then_inc(s_out, 1)
                    v.tensor_reduce(hmax[:, ds(t, 1)], psO[:, 0:H1], AX.X, ALU.max, apply_absolute_value=True
                                    ).then_inc(s_out, 1)
                    v.tensor_tensor(HB[:, ds(t * H1, H1)], psO[:, H1:2 * H1], b1r[:, :], ALU.add).then_inc(s_out, 1)

                def first(t, u):
                    mean(t, u)
                    v.wait_ge(s_w, 16 * 6)

                def step(t, before, u):
                    mean(t, u)
                    results(before, 1 - u)
                skewed(v, first, step, results)

        SPv = parts(D, XB, True)
        H2 = DL[2]
        with Phase() as ph:
            W2 = ph.sb("W2", [P, K, 2 * H2], f32)
            b2r = ph.sb("b2r", [P, H2], f32)
            tl = ph.sb("tl", [P, 2, D], f32)
            xs = ph.sb("xs", [P, 2, D], f32)
            xT = ph.sb("xT", [P, 2, D], f32)
            psA = [ph.ps(f"psA{u}", [P, 2 * D]) for u in range(2)]
            psT = [ph.ps(f"psT{u}", [P, D]) for u in range(2)]
            psO = [ph.ps(f"psO{u}", [P, 2 * H2]) for u in range(2)]
            s_w, s_A, s_tl, s_x, s_T, s_xT, s_O, s_out, s_v = (
                ph.sem(n) for n in ("w", "A", "tl", "x", "T", "xT", "O", "out", "v"))
            block = ph.enter_context(nc.Block())

            @block.sync
            def _(sp):
                for j, w in enumerate((wn2, wr2)):
                    sp.dma_start(W2[:, :, j * H2:(j + 1) * H2], w.rearrange("(k p) f -> p k f", p=P)).then_inc(s_w, 16)
                sp.dma_start(b2r[:, :], b2.rearrange("(a f) -> a f", a=1).to_broadcast([P, H2])).then_inc(s_w, 16)

            @block.tensor
            def _(pe):
                pe.sem_inc(s_xT, 2)

                def total(t, u, s0=0, s1=NT):
                    if s0 == 0:
                        hold(pe, s_x, t + 1)
                    m = neighbours(pe, psA[u], SPv, t, s0, s1)
                    if s1 == NT:
                        m.then_inc(s_A, 1)

                def turn(t, u):
                    hold(pe, s_x, t + 3)
                    hold(pe, s_xT, t + 1)
                    for k in range(K):
                        m = pe.transpose(psT[u][:, k * P:(k + 1) * P], xs[:, u, k * P:(k + 1) * P], ident[:, :])
                    m.then_inc(s_T, 1)

                def both(t, u):
                    hold(pe, s_xT, t + 3)
                    hold(pe, s_out, t * 3 + 3)
                    for k in range(K):
                        m = pe.matmul(psO[u][:, :], xT[:, u, k * P:(k + 1) * P], W2[:, k, :], start=k == 0, stop=k == K - 1)
                    m.then_inc(s_O, 1)

                def first(t, u):
                    total(t, u)
                    pe.wait_ge(s_w, 16 * 3)

                def step(t, before, u):
                    total(t, u, 0, 13)
                    turn(before, 1 - u)
                    total(t, u, 13, NT)
                    both(before, 1 - u)

                def last(t, u):
                    turn(t, u)
                    both(t, u)
                skewed(pe, first, step, last)

            @block.scalar
            def _(a):
                a.sem_inc(s_O, 2)

                def low(t, u):
                    hold(a, s_x, t + 1)
                    hold(a, s_A, t + 1)
                    a.activation(tl[:, u, :], psA[u][:, D:2 * D], ACT.Copy, scale=1 / LO).then_inc(s_tl, 1)

                def copy(t, u):
                    hold(a, s_T, t + 1)
                    hold(a, s_O, t + 1)
                    a.activation(xT[:, u, :], psT[u][:, :], ACT.Copy).then_inc(s_xT, 1)

                def step(t, before, u):
                    copy(before, 1 - u)
                    low(t, u)
                skewed(a, low, step, copy)

            @block.vector
            def _(v):
                v.sem_inc(s_x, 2)
                v.sem_inc(s_out, 6)

                def layer(t, u):
                    hold(v, s_tl, t + 1)
                    hold(v, s_xT, t + 1)
                    v.tensor_tensor(xs[:, u, :], psA[u][:, 0:D], tl[:, u, :], ALU.add).then_inc(s_v, 1)
                    hold(v, s_v, t * 2 + 1)
                    v.scalar_tensor_tensor(xs[:, u, :], xs[:, u, :], rdk[:, ds(t, 1)], HB[:, ds(t * D, D)],
                                           ALU.mult, ALU.add).then_inc(s_v, 1)
                    hold(v, s_v, t * 2 + 2)
                    v.tensor_scalar(xs[:, u, :], xs[:, u, :], 0.0, None, ALU.max).then_inc(s_x, 1)

                def results(t, u):
                    hold(v, s_O, t + 3)
                    v.tensor_copy(XB[:, ds(t * H2, H2)], psO[u][:, 0:H2]).then_inc(s_out, 1)
                    v.tensor_reduce(hmax[:, ds(t, 1)], psO[u][:, 0:H2], AX.X, ALU.max, apply_absolute_value=True
                                    ).then_inc(s_out, 1)
                    v.tensor_tensor(HB[:, ds(t * D, H2)], psO[u][:, H2:2 * H2], b2r[:, :], ALU.add).then_inc(s_out, 1)

                def first(t, u):
                    layer(t, u)
                    v.wait_ge(s_w, 16 * 3)

                def step(t, before, u):
                    layer(t, u)
                    results(before, 1 - u)
                skewed(v, first, step, results)

        SPv = parts(H2, XB, True)
        G0, G1 = D, 2 * D
        with Phase() as ph:
            E0 = ph.sb("E0", [P, G0], f32)
            E1 = ph.sb("E1", [P, G0 // P, G1], f32)
            E2 = ph.sb("E2", [P, G1 // P, D], f32)
            c0, c1 = ph.sb("c0", [P, G0 // P], f32), ph.sb("c1", [P, G1 // P], f32)
            c2 = ph.sb("c2", [P, D], f32)
            tl = ph.sb("tl", [P, 2, H2], f32)
            xs = ph.sb("xs", [P, 2, H2], f32)
            xT = ph.sb("xT", [P, 2, H2], f32)
            h0 = ph.sb("h0", [P, 2, G0], f32)
            h1 = ph.sb("h1", [P, 2, G1], f32)
            y = ph.sb("y", [P, 2, D], f32)
            xr = ph.sb("xr", [P, 2, D], f32)
            psA = [ph.ps(f"psA{u}", [P, 2 * H2]) for u in range(2)]
            psT = ph.ps("psT", [P, H2])
            ps0 = ph.ps("ps0", [P, G0])
            ps1 = [ph.ps(f"ps1{u}", [P, G1]) for u in range(2)]
            psO = [ph.ps(f"psO{u}", [P, D]) for u in range(2)]
            s_w, s_A, s_tl, s_x, s_T, s_xT, s_0, s_h0, s_1, s_h1, s_O, s_out, s_v, s_y = (
                ph.sem(n) for n in ("w", "A", "tl", "x", "T", "xT", "0", "h0", "1", "h1", "O", "out", "v", "y"))
            s_xr = [ph.sem(f"xr{u}") for u in range(2)]
            block = ph.enter_context(nc.Block())

            @block.sync
            def _(sp):
                sp.dma_start(E0[:, :], dw0).then_inc(s_w, 16)
                for w, m in ((E1, dw1), (E2, dw2)):
                    sp.dma_start(w[:, :, :], m.rearrange("(k p) f -> p k f", p=P)).then_inc(s_w, 16)
                with nc.allow_non_contiguous_dma("biases of 768 elements, one to a partition"):
                    for w, m in ((c0, db0), (c1, db1)):
                        sp.dma_start(w[:, :], m.rearrange("(f p) -> p f", p=P)).then_inc(s_w, 16)
                sp.dma_start(c2[:, :], db2.rearrange("(a f) -> a f", a=1).to_broadcast([P, D])).then_inc(s_w, 16)
                with sp.Fori(0, NT // 2) as i:
                    for u in range(2):
                        t = i * 2 + u
                        sp.wait_ge(s_out, t + 1)
                        sp.dma_start(xr[:, u, :], xd[:, ds(t * D, D)]).then_inc(s_xr[u], 16)

            def three_deep(eng, step):
                step(0, 0, 0, layers=False, last=False)
                step(1, 0, 1, last=False)
                with eng.Fori(0, (NT // 2 - 1) // 3) as j:
                    for i in (j * 3 + 1, j * 3 + 2, j * 3 + 3):
                        step(i * 2, i, 0)
                        step(i * 2 + 1, i, 1)
                step(NT, NT // 2, 0, sums=False)
                step(NT + 1, NT // 2, 1, sums=False, layers=False)

            @block.tensor
            def _(pe):
                pe.sem_inc(s_xT, 1)
                pe.sem_inc(s_h0, 1)
                pe.sem_inc(s_h1, 2)

                def total(t, u, s0=0, s1=NT):
                    if s0 == 0:
                        hold(pe, s_x, t + 1)
                    m = neighbours(pe, psA[u], SPv, t, s0, s1)
                    if s1 == NT:
                        m.then_inc(s_A, 1)

                def turn(t, u):
                    hold(pe, s_x, t + 3)
                    hold(pe, s_xT, t + 1)
                    pe.transpose(psT[:, :], xs[:, u, :], ident[:, :]).then_inc(s_T, 1)

                def dense0(t, u):
                    hold(pe, s_xT, t + 2)
                    hold(pe, s_h0, t + 1)
                    for f in range(G0 // P):
                        m = pe.matmul(ps0[:, f * P:(f + 1) * P], E0[:, f * P:(f + 1) * P], xT[:, u, :], start=True, stop=True)
                    m.then_inc(s_0, 1)

                def dense1(t, u):
                    hold(pe, s_h0, t + 2)
                    hold(pe, s_h1, t + 1)
                    for f in range(G1 // P):
                        for k in range(G0 // P):
                            m = pe.matmul(ps1[u][:, f * P:(f + 1) * P], E1[:, k, f * P:(f + 1) * P],
                                          h0[:, u, k * P:(k + 1) * P], start=k == 0, stop=k == G0 // P - 1)
                    m.then_inc(s_1, 1)

                def dense2(t, u):
                    hold(pe, s_h1, t + 3)
                    hold(pe, s_out, t + 1)
                    for k in range(G1 // P):
                        m = pe.matmul(psO[u][:, :], h1[:, u, k * P:(k + 1) * P], E2[:, k, :], start=k == 0, stop=k == G1 // P - 1)
                    m.then_inc(s_O, 1)

                def step(t, i, u, sums=True, layers=True, last=True):
                    if sums:
                        total(t, u, 0, NT // 2)
                    if layers:
                        turn(t - 1, 1 - u)
                    if sums:
                        total(t, u, NT // 2, NT)
                    if layers:
                        dense0(t - 1, 1 - u)
                    if last:
                        dense2(t - 2, u)
                    if layers:
                        dense1(t - 1, 1 - u)
                    if not layers and sums:
                        pe.wait_ge(s_w, 16 * 6)
                three_deep(pe, step)

            @block.scalar
            def _(a):
                a.sem_inc(s_O, 2)
                a.sem_inc(s_0, 2)
                a.sem_inc(s_1, 2)

                def low(t, u):
                    hold(a, s_x, t + 1)
                    hold(a, s_A, t + 1)
                    a.activation(tl[:, u, :], psA[u][:, H2:2 * H2], ACT.Copy, scale=1 / LO).then_inc(s_tl, 1)

                def copy(t, u):
                    hold(a, s_T, t + 1)
                    hold(a, s_0, t + 1)
                    a.activation(xT[:, u, :], psT[:, :], ACT.Copy).then_inc(s_xT, 1)

                def relu0(t, u):
                    hold(a, s_0, t + 3)
                    hold(a, s_1, t + 1)
                    for f in range(G0 // P):
                        ins = a.activation(h0[:, u, f * P:(f + 1) * P], ps0[:, f * P:(f + 1) * P], ACT.Relu, bias=c0[:, f:f + 1])
                    ins.then_inc(s_h0, 1)

                def relu1(t, u):
                    hold(a, s_1, t + 3)
                    hold(a, s_O, t + 1)
                    for f in range(G1 // P):
                        ins = a.activation(h1[:, u, f * P:(f + 1) * P], ps1[u][:, f * P:(f + 1) * P], ACT.Relu, bias=c1[:, f:f + 1])
                    ins.then_inc(s_h1, 1)

                def step(t, i, u, sums=True, layers=True, last=True):
                    if layers:
                        copy(t - 1, 1 - u)
                        relu0(t - 1, 1 - u)
                    if sums:
                        low(t, u)
                    if layers:
                        relu1(t - 1, 1 - u)
                    if not layers and sums:
                        a.wait_ge(s_w, 16 * 6)
                three_deep(a, step)

            @block.vector
            def _(v):
                v.sem_inc(s_x, 2)
                v.sem_inc(s_out, 2)

                def layer(t, u):
                    hold(v, s_tl, t + 1)
                    hold(v, s_xT, t + 1)
                    v.tensor_tensor(xs[:, u, :], psA[u][:, 0:H2], tl[:, u, :], ALU.add).then_inc(s_v, 1)
                    hold(v, s_v, t * 2 + 1)
                    v.scalar_tensor_tensor(xs[:, u, :], xs[:, u, :], rdk[:, ds(t, 1)], HB[:, ds(t * D, H2)],
                                           ALU.mult, ALU.add).then_inc(s_v, 1)
                    hold(v, s_v, t * 2 + 2)
                    v.tensor_scalar(xs[:, u, :], xs[:, u, :], 0.0, None, ALU.max).then_inc(s_x, 1)

                def result(t, i, u):
                    hold(v, s_O, t + 3)
                    hold(v, s_out, t + 1)
                    v.tensor_tensor(y[:, u, :], psO[u][:, :], c2[:, :], ALU.add).then_inc(s_y, 1)
                    hold(v, s_y, t + 1)
                    hold(v, s_xr[u], i * 16 + 16)
                    v.scalar_tensor_tensor(HB[:, ds(t * D, D)], y[:, u, :], 0.0, xr[:, u, :], ALU.max, ALU.add).then_inc(s_out, 1)

                def step(t, i, u, sums=True, layers=True, last=True):
                    if sums:
                        layer(t, u)
                    if last:
                        result(t - 2, i - 1, u)
                    if not layers and sums:
                        v.wait_ge(s_w, 16 * 6)
                three_deep(v, step)
        sg.close()

        with Phase() as ph:
            G4 = 4
            psU = [ph.ps(f"psU{u}", [P, G4 * P], f16) for u in range(4)]
            psL = [ph.ps(f"psL{u}", [P, G4 * P], f16) for u in range(4)]
            s_t, s_u, s_l, s_m, s_st = (ph.sem(n) for n in ("t", "u", "l", "m", "st"))
            block = ph.enter_context(nc.Block())
            Cv = C[:, :].rearrange("p (s d) -> p s d", d=NP)
            groups = [(i, j, min(j + G4, NT)) for i in range(NT) for j in range(i, NT, G4)]

            @block.tensor
            def _(pe):
                for n, (i, j0, j1) in enumerate(groups):
                    if n >= 4:
                        pe.wait_ge(s_u, n - 3)
                        pe.wait_ge(s_l, n - 3)
                    for j in range(j0, j1):
                        q = (j - j0) * P
                        pe.transpose(psU[n % 4][:, q:q + P], Cv[:, i, j * P:(j + 1) * P], ident16[:, :])
                        m = pe.transpose(psL[n % 4][:, q:q + P], Cv[:, j, i * P:(i + 1) * P], ident16[:, :])
                    m.then_inc(s_t, 1)

            @block.vector
            def _(v):
                for n, (i, j0, j1) in enumerate(groups):
                    v.wait_ge(s_t, n + 1)
                    v.tensor_copy(Cv[:, i, j0 * P:j1 * P], psL[n % 4][:, 0:(j1 - j0) * P]).then_inc(s_l, 1)

            @block.scalar
            def _(a):
                for n, (i, j0, j1) in enumerate(groups):
                    a.wait_ge(s_t, n + 1)
                    k = 1 if j0 == i else 0
                    if j1 - j0 > k:
                        a.activation(Cv[:, j0 + k:j1, i * P:(i + 1) * P],
                                     psU[n % 4][:, k * P:(j1 - j0) * P].rearrange("p (s d) -> p s d", d=P),
                                     ACT.Copy).then_inc(s_u, 1)
                    else:
                        a.sem_inc(s_u, 1)

            @block.gpsimd
            def _(g):
                g.tensor_copy(XB, HB[:, 0:NT * D]).then_inc(s_m, 1)

            @block.sync
            def _(sp):
                sp.dma_start(xd[:, :], HB[:, 0:NT * D]).then_inc(s_st, 16)
                sp.wait_ge(s_st, 16)

        attention(gat3, 4, 64, True, True, -1, AB, False)
        with Phase() as last:
            xr = last.sb("xr", [P, NT * D], f32)
            s_xr, s_res = last.sem("xr"), last.sem("res")

            def write_result(ph, block, read, done):
                @block.gpsimd
                def _(g):
                    g.dma_start(xr[:, :], xd[:, :]).then_inc(s_xr, 16)
                    TB = 4
                    for i in range(NT // TB):
                        g.wait_ge(*done(i))
                        t0, t1 = i * TB, min(i * TB + TB, NT - 1)
                        g.dma_start(out[t0 * P:t1 * P, :].rearrange("(t p) f -> p t f", p=P),
                                    XB[:, t0 * D:t1 * D].rearrange("p (t f) -> p t f", f=D)).then_inc(s_res, 16)
                    g.dma_start(out[(NT - 1) * P:N, :], XB[0:LAST, (NT - 1) * D:NT * D]).then_inc(s_res, 16)
                    g.wait_ge(s_res, 16 * (NT // TB + 1))

            elu(HB[:, 0:NT * (D + 4)], XB, None, 4, True, write_result, (xr, s_xr))


_INS = ["x", "src", "dst", "edge_weight"] + [f"L0_gnn_{n}" for n in ("W0", "al0", "ar0", "b0", "W1", "al1", "ar1", "b1")] \
    + [f"L2_gnn_{n}" for n in ("wn0", "wr0", "b0", "wn1", "wr1", "b1", "wn2", "wr2", "b2",
                               "dw0", "db0", "dw1", "db1", "dw2", "db2")] + ["L3_gnn_W", "L3_gnn_a"]


def kernel(**inputs):
    import numpy as _np
    import concourse.bacc as _bacc
    from concourse import mybir as _mybir
    from concourse.bass_utils import run_bass_kernel_spmd as _run

    nc = _bacc.Bacc("TRN2", target_bir_lowering=False, num_devices=1)
    arrays, args = {}, []
    for name in _INS:
        a = _np.ascontiguousarray(inputs[name])
        arrays[f"in_{name}"] = a
        args.append(nc.dram_tensor(f"in_{name}", a.shape, _mybir.dt.from_np(a.dtype), kind="ExternalInput").ap())
    out = nc.dram_tensor("out_0", (N, D), _mybir.dt.float32, kind="ExternalOutput").ap()
    build(nc, args[0], args[1], args[2], args[3], args[4:8], args[8:12], args[12:21], args[21:27], args[27:29], out)
    r = _run(nc, [arrays], core_ids=[0])
    return r.results[0]["out_0"]
```
